# Optimizing a Trainium2 kernel written in Bass

```python
import numpy as np
import jax
import jax.numpy as jnp

def _softmax(x, axis=-1):
    return jax.nn.softmax(x, axis=axis)

def _gelu(x):
    return jax.nn.gelu(x, approximate=True)

def _silu(x):
    return jax.nn.silu(x)

def _sigmoid(x):
    return jax.nn.sigmoid(x)

def _layernorm(x, axis=-1, eps=1e-05):
    m = jnp.mean(x, axis=axis, keepdims=True)
    v = jnp.var(x, axis=axis, keepdims=True)
    return (x - m) / jnp.sqrt(v + eps)

def _scatter_add(tgt, idx, src, axis=0):
    return tgt.at[idx].add(src)

def _segment_sum(src, seg, n):
    return jax.ops.segment_sum(src, seg, n)
kernel_name = 'mk_adaln_d1_jaxref_r4_f95c16'

def setup_inputs(seed: int=0):
    np.random.seed(seed)
    _w = jnp.asarray

    def _L0_attn_setup():
        import jax, jax.numpy as jnp
        import numpy as np
        D_MODEL = 512
        D_STATE = 128
        D_CONV = 4
        EXPAND = 2
        HEADDIM = 64
        NGROUPS = 1
        CHUNK = 64
        D_INNER = EXPAND * D_MODEL
        NHEADS = D_INNER // HEADDIM
        HG = NHEADS // NGROUPS
        CONV_DIM = D_INNER + 2 * NGROUPS * D_STATE
        D_IN_PROJ = 2 * D_INNER + 2 * NGROUPS * D_STATE + NHEADS
        BATCH = 2
        SEQLEN = 512
        EPS = 1e-05

        def _mamba2(u, in_proj_w, conv_w, conv_b, dt_bias, A_log, D_skip, norm_w, out_proj_w):
            b, l, _ = u.shape
            nc = l // CHUNK
            zxbcdt = u @ in_proj_w.T
            z = zxbcdt[..., :D_INNER]
            xBC = zxbcdt[..., D_INNER:D_INNER + CONV_DIM]
            dt = jax.nn.softplus(zxbcdt[..., D_INNER + CONV_DIM:] + dt_bias)
            xp = jnp.pad(xBC, ((0, 0), (D_CONV - 1, 0), (0, 0)))
            conv = conv_b + sum((conv_w[:, k] * xp[:, k:k + l, :] for k in range(D_CONV)))
            xBC = jax.nn.silu(conv)
            x = xBC[..., :D_INNER].reshape(b, l, NHEADS, HEADDIM)
            Bm = xBC[..., D_INNER:D_INNER + NGROUPS * D_STATE].reshape(b, l, NGROUPS, D_STATE)
            Cm = xBC[..., D_INNER + NGROUPS * D_STATE:].reshape(b, l, NGROUPS, D_STATE)
            A = -jnp.exp(A_log)
            xc = x.reshape(b, nc, CHUNK, NGROUPS, HG, HEADDIM)
            dtc = dt.reshape(b, nc, CHUNK, NGROUPS, HG)
            Bc = Bm.reshape(b, nc, CHUNK, NGROUPS, D_STATE)
            Cc = Cm.reshape(b, nc, CHUNK, NGROUPS, D_STATE)
            dA = jnp.transpose(dtc * A.reshape(NGROUPS, HG), (0, 3, 4, 1, 2))
            dA_cs = jnp.cumsum(dA, axis=-1)
            seg = dA_cs[..., :, None] - dA_cs[..., None, :]
            tri = jnp.tril(jnp.ones((CHUNK, CHUNK), bool))
            Lmat = jnp.where(tri, jnp.exp(seg), 0.0)
            xdt = xc * dtc[..., None]
            CB = jnp.einsum('bclgn,bcsgn->bcgls', Cc, Bc)
            Y_diag = jnp.einsum('bcgls,bgHcls,bcsgHp->bclgHp', CB, Lmat, xdt)
            decay_states = jnp.exp(dA_cs[..., -1:] - dA_cs)
            states = jnp.einsum('bcsgn,bgHcs,bcsgHp->bcgHpn', Bc, decay_states, xdt)
            chunk_decay = jnp.exp(dA_cs[..., -1])

            def step(carry, inp):
                st, dec = inp
                return (carry * dec[..., None, None] + st, carry)
            _, prev = jax.lax.scan(step, jnp.zeros_like(states[:, 0]), (jnp.moveaxis(states, 1, 0), jnp.moveaxis(chunk_decay, -1, 0)))
            prev = jnp.moveaxis(prev, 0, 1)
            Y_off = jnp.einsum('bclgn,bcgHpn,bgHcl->bclgHp', Cc, prev, jnp.exp(dA_cs))
            y = (Y_diag + Y_off).reshape(b, l, NHEADS, HEADDIM) + x * D_skip[None, None, :, None]
            y = y.reshape(b, l, D_INNER)
            y = y * jax.nn.silu(z)
            yg = y.reshape(b, l, NGROUPS, D_INNER // NGROUPS)
            yg = yg * jax.lax.rsqrt(jnp.mean(yg * yg, axis=-1, keepdims=True) + EPS)
            y = yg.reshape(b, l, D_INNER) * norm_w
            return y @ out_proj_w.T
        ks = jax.random.split(jax.random.key(seed), 8)
        u = jax.random.normal(ks[0], (BATCH, SEQLEN, D_MODEL), jnp.float32)
        in_proj_w = jax.random.normal(ks[1], (D_IN_PROJ, D_MODEL), jnp.float32) * D_MODEL ** (-0.5)
        conv_w = jax.random.normal(ks[2], (CONV_DIM, D_CONV), jnp.float32) * D_CONV ** (-0.5)
        conv_b = jax.random.normal(ks[3], (CONV_DIM,), jnp.float32) * 0.1
        dt = jnp.exp(jax.random.uniform(ks[4], (NHEADS,), jnp.float32) * (np.float32(np.log(0.1)) - np.float32(np.log(0.001))) + np.float32(np.log(0.001)))
        dt = jnp.clip(dt, 0.0001, None)
        dt_bias = dt + jnp.log(-jnp.expm1(-dt))
        A_log = jnp.log(jax.random.uniform(ks[5], (NHEADS,), jnp.float32, minval=1.0, maxval=16.0))
        D_skip = jnp.ones((NHEADS,), jnp.float32)
        norm_w = jnp.ones((D_INNER,), jnp.float32)
        out_proj_w = jax.random.normal(ks[6], (D_MODEL, D_INNER), jnp.float32) * D_INNER ** (-0.5)
        return dict(u=u, in_proj_w=in_proj_w, conv_w=conv_w, conv_b=conv_b, dt_bias=dt_bias, A_log=A_log, D_skip=D_skip, norm_w=norm_w, out_proj_w=out_proj_w)
    _L0_attn_in = _L0_attn_setup()

    def _L0_ffn_setup():
        import jax, jax.numpy as jnp
        import numpy as np

        def _sparsify_2to4(h):
            B, S, I = h.shape
            g = h.reshape(B, S, I // 4, 4)
            a = jnp.abs(g)
            _, idx = jax.lax.top_k(a, 2)
            pos = jnp.arange(4)
            mask = (pos == idx[..., 0:1]) | (pos == idx[..., 1:2])
            return (g * mask.astype(g.dtype)).reshape(B, S, I)
        key = jax.random.key(seed)
        k1, k2, k3, k4 = jax.random.split(key, 4)
        B, S, H, I = (4, 512, 512, 2048)
        x = jax.random.normal(k1, (B, S, H), dtype=jnp.float32)
        w_gate = jax.random.normal(k2, (H, I), dtype=jnp.float32) / np.sqrt(H)
        w_up = jax.random.normal(k3, (H, I), dtype=jnp.float32) / np.sqrt(H)
        w_down = jax.random.normal(k4, (I, H), dtype=jnp.float32) / np.sqrt(I)
        return {'x': x, 'w_gate': w_gate, 'w_up': w_up, 'w_down': w_down}
    _L0_ffn_in = _L0_ffn_setup()
    _L0_c = _w((lambda *s: np.random.randn(*s).astype(np.float32) * 0.05)(1, 512))
    _L0_wmod = _w((lambda *s: np.random.randn(*s).astype(np.float32) * 0.05)(512, 6 * 512) * 512 ** (-0.5))
    _d = {'L0_attn_u': _L0_attn_in['u'], 'L0_attn_in_proj_w': _L0_attn_in['in_proj_w'], 'L0_attn_conv_w': _L0_attn_in['conv_w'], 'L0_attn_conv_b': _L0_attn_in['conv_b'], 'L0_attn_dt_bias': _L0_attn_in['dt_bias'], 'L0_attn_A_log': _L0_attn_in['A_log'], 'L0_attn_D_skip': _L0_attn_in['D_skip'], 'L0_attn_norm_w': _L0_attn_in['norm_w'], 'L0_attn_out_proj_w': _L0_attn_in['out_proj_w'], 'L0_ffn_w_gate': _L0_ffn_in['w_gate'], 'L0_ffn_w_up': _L0_ffn_in['w_up'], 'L0_ffn_w_down': _L0_ffn_in['w_down'], 'L0_c': _L0_c, 'L0_wmod': _L0_wmod}
    _x0 = _d['L0_attn_u']
    _d['L0_attn_u'] = jax.random.normal(jax.random.fold_in(jax.random.key(seed), 1), (1, 2048, 512), dtype=_x0.dtype)
    del _x0
    return _d

def reference(L0_attn_u, L0_attn_in_proj_w, L0_attn_conv_w, L0_attn_conv_b, L0_attn_dt_bias, L0_attn_A_log, L0_attn_D_skip, L0_attn_norm_w, L0_attn_out_proj_w, L0_ffn_w_gate, L0_ffn_w_up, L0_ffn_w_down, L0_c, L0_wmod):

    def _L0_attn_ref(u, in_proj_w, conv_w, conv_b, dt_bias, A_log, D_skip, norm_w, out_proj_w):
        import jax, jax.numpy as jnp
        import numpy as np
        D_MODEL = 512
        D_STATE = 128
        D_CONV = 4
        EXPAND = 2
        HEADDIM = 64
        NGROUPS = 1
        CHUNK = 64
        D_INNER = EXPAND * D_MODEL
        NHEADS = D_INNER // HEADDIM
        HG = NHEADS // NGROUPS
        CONV_DIM = D_INNER + 2 * NGROUPS * D_STATE
        D_IN_PROJ = 2 * D_INNER + 2 * NGROUPS * D_STATE + NHEADS
        BATCH = 2
        SEQLEN = 512
        EPS = 1e-05

        def _mamba2(u, in_proj_w, conv_w, conv_b, dt_bias, A_log, D_skip, norm_w, out_proj_w):
            b, l, _ = u.shape
            nc = l // CHUNK
            zxbcdt = u @ in_proj_w.T
            z = zxbcdt[..., :D_INNER]
            xBC = zxbcdt[..., D_INNER:D_INNER + CONV_DIM]
            dt = jax.nn.softplus(zxbcdt[..., D_INNER + CONV_DIM:] + dt_bias)
            xp = jnp.pad(xBC, ((0, 0), (D_CONV - 1, 0), (0, 0)))
            conv = conv_b + sum((conv_w[:, k] * xp[:, k:k + l, :] for k in range(D_CONV)))
            xBC = jax.nn.silu(conv)
            x = xBC[..., :D_INNER].reshape(b, l, NHEADS, HEADDIM)
            Bm = xBC[..., D_INNER:D_INNER + NGROUPS * D_STATE].reshape(b, l, NGROUPS, D_STATE)
            Cm = xBC[..., D_INNER + NGROUPS * D_STATE:].reshape(b, l, NGROUPS, D_STATE)
            A = -jnp.exp(A_log)
            xc = x.reshape(b, nc, CHUNK, NGROUPS, HG, HEADDIM)
            dtc = dt.reshape(b, nc, CHUNK, NGROUPS, HG)
            Bc = Bm.reshape(b, nc, CHUNK, NGROUPS, D_STATE)
            Cc = Cm.reshape(b, nc, CHUNK, NGROUPS, D_STATE)
            dA = jnp.transpose(dtc * A.reshape(NGROUPS, HG), (0, 3, 4, 1, 2))
            dA_cs = jnp.cumsum(dA, axis=-1)
            seg = dA_cs[..., :, None] - dA_cs[..., None, :]
            tri = jnp.tril(jnp.ones((CHUNK, CHUNK), bool))
            Lmat = jnp.where(tri, jnp.exp(seg), 0.0)
            xdt = xc * dtc[..., None]
            CB = jnp.einsum('bclgn,bcsgn->bcgls', Cc, Bc)
            Y_diag = jnp.einsum('bcgls,bgHcls,bcsgHp->bclgHp', CB, Lmat, xdt)
            decay_states = jnp.exp(dA_cs[..., -1:] - dA_cs)
            states = jnp.einsum('bcsgn,bgHcs,bcsgHp->bcgHpn', Bc, decay_states, xdt)
            chunk_decay = jnp.exp(dA_cs[..., -1])

            def step(carry, inp):
                st, dec = inp
                return (carry * dec[..., None, None] + st, carry)
            _, prev = jax.lax.scan(step, jnp.zeros_like(states[:, 0]), (jnp.moveaxis(states, 1, 0), jnp.moveaxis(chunk_decay, -1, 0)))
            prev = jnp.moveaxis(prev, 0, 1)
            Y_off = jnp.einsum('bclgn,bcgHpn,bgHcl->bclgHp', Cc, prev, jnp.exp(dA_cs))
            y = (Y_diag + Y_off).reshape(b, l, NHEADS, HEADDIM) + x * D_skip[None, None, :, None]
            y = y.reshape(b, l, D_INNER)
            y = y * jax.nn.silu(z)
            yg = y.reshape(b, l, NGROUPS, D_INNER // NGROUPS)
            yg = yg * jax.lax.rsqrt(jnp.mean(yg * yg, axis=-1, keepdims=True) + EPS)
            y = yg.reshape(b, l, D_INNER) * norm_w
            return y @ out_proj_w.T
        return _mamba2(u, in_proj_w, conv_w, conv_b, dt_bias, A_log, D_skip, norm_w, out_proj_w)

    def _L0_ffn_ref(x, w_gate, w_up, w_down):
        import jax, jax.numpy as jnp
        import numpy as np

        def _sparsify_2to4(h):
            B, S, I = h.shape
            g = h.reshape(B, S, I // 4, 4)
            a = jnp.abs(g)
            _, idx = jax.lax.top_k(a, 2)
            pos = jnp.arange(4)
            mask = (pos == idx[..., 0:1]) | (pos == idx[..., 1:2])
            return (g * mask.astype(g.dtype)).reshape(B, S, I)
        h = jax.nn.silu(jnp.einsum('bsh,hi->bsi', x, w_gate)) * jnp.einsum('bsh,hi->bsi', x, w_up)
        h_sparse = _sparsify_2to4(h)
        return jnp.einsum('bsi,ih->bsh', h_sparse, w_down)
    x = L0_attn_u
    mod = (_silu(L0_c) @ L0_wmod).reshape(L0_c.shape[0], 6, 1, -1)
    sa, ca, ga, sb, cb, gb = (mod[:, 0], mod[:, 1], mod[:, 2], mod[:, 3], mod[:, 4], mod[:, 5])
    ga = (2 * (ga >= 0) - 1) * jnp.maximum(jnp.abs(ga), 0.25)
    gb = (2 * (gb >= 0) - 1) * jnp.maximum(jnp.abs(gb), 0.25)
    h = _layernorm(x, axis=-1) * (1 + ca) + sa
    x = x + ga * _L0_attn_ref(h, L0_attn_in_proj_w, L0_attn_conv_w, L0_attn_conv_b, L0_attn_dt_bias, L0_attn_A_log, L0_attn_D_skip, L0_attn_norm_w, L0_attn_out_proj_w)
    h = _layernorm(x, axis=-1) * (1 + cb) + sb
    x = x + gb * _L0_ffn_ref(h, L0_ffn_w_gate, L0_ffn_w_up, L0_ffn_w_down)
    return x

_drawn_inputs = setup_inputs


def setup_inputs(seed=0):
    import zlib

    import numpy as np

    out = dict(_drawn_inputs(seed))
    spreads = {'L0_attn_D_skip': (1.0, 0.6), 'L0_attn_norm_w': (1.0, 0.2)}
    factors = {}
    for name, (base, spread) in spreads.items():
        noise = np.random.default_rng([zlib.crc32(name.encode()), seed]).standard_normal(out[name].shape)
        drawn = base * np.exp(spread * noise) if base else spread * noise
        out[name] = jnp.asarray(drawn.astype(out[name].dtype))
    for name, factor in factors.items():
        out[name] = (out[name] * factor).astype(out[name].dtype)
    return out
```

```python
from contextlib import ExitStack

import concourse.bass as bass
from concourse import mybir

F32 = mybir.dt.float32
F32R = mybir.dt.float32r
BF16 = mybir.dt.bfloat16
ALU = mybir.AluOpType
ACT = mybir.ActivationFunctionType
AX = mybir.AxisListType

P = 128
L = 2048
D = 512
DI = 1024
NS = 128
NH = 16
HD = DI // NH
KT = D // P
CT = DI // P
NXBC = CT + 2
DIN = 2 * DI + 2 * NS + NH
TB = 512
NB = L // TB
TT = TB // P
NCH = L // P
EPS = 1e-5
FI = 2048
NIC = FI // 512
TAPS = 4

WP = DIN // 8
NWP = DIN // WP
NJ = 1 + NXBC + CT
NST = NXBC + CT


def column_of(j):
    if j == 0:
        return DIN - P
    return DI + P * (j - 1) if j <= NXBC else P * (j - 1 - NXBC)


def broadcast(ap, shape):
    return ap.broadcast_to(shape)


def three_pass(pe, out, pairs):
    n = len(pairs)
    for i, (lh, ll, rh, rl) in enumerate(pairs):
        pe.matmul(out, lh, rh, start=(i == 0), stop=False)
        pe.matmul(out, lh, rl, start=False, stop=False)
        last = pe.matmul(out, ll, rh, start=False, stop=(i == n - 1))
    return last


def build(nc, x, w_in, w_out, conv_w, conv_b, dt_bias, a_log, d_skip, norm_w, w_gu, w_down, c, w_mod, out):
    with ExitStack() as ctx:
        sems = {}

        def sem(name):
            if name not in sems:
                sems[name] = ctx.enter_context(nc.semaphore(name))
            return sems[name]

        def sb(name, shape, dt=F32, stack=ctx):
            return stack.enter_context(nc.sbuf_tensor(name, shape, dt))

        xz_dram = nc.dram_tensor("xz_scratch", [NCH, P, NST, P], F32).ap()
        x1_dram = nc.dram_tensor("x1_scratch", [NCH, P, D], F32).ap()

        ident = sb("ident", [P, P])
        upto = sb("upto", [P, P])
        after = sb("after", [P, P])
        after_r = sb("after_r", [P, P], F32R)
        ones = sb("ones", [P, P])
        eps = sb("eps", [P, TT])
        neghalf = sb("neghalf", [P, TT])
        modrow = sb("modrow", [P, 6, D])
        modcol = sb("modcol", [P, 4, KT])
        dt_raw = sb("dt_raw", [P, NCH, NH])
        ps = ctx.enter_context(nc.psum_tensor("ps", [P, 8, 512], F32))

        project_stage(nc, sem, sb, ps, x, w_in, conv_w, conv_b, dt_bias, c, w_mod, xz_dram,
                      ident, upto, after, after_r, ones, neghalf, eps, modrow, modcol, dt_raw)
        scan_stage(nc, sem, sb, ps, x, w_out, a_log, d_skip, norm_w, xz_dram, x1_dram,
                   ident, upto, after, after_r, ones, neghalf, eps, modrow, dt_raw)
        ffn_stage(nc, sem, sb, ps, w_gu, w_down, x1_dram, out, ident, neghalf, eps, modrow, modcol)


def tile_statistics(dve, sem, tag, blk, x_tiles, stats, mv, idle):
    step = sem(f"{tag}_ln_step")
    for i in range(TT):
        ins = dve.bn_stats(stats[:, i, :], x_tiles[:, i, :])
    ins.then_inc(step, 1)
    dve.wait_ge(step, blk * 2 + 1)
    dve.wait_ge(sem(f"{tag}_xn_ready"), blk * TT + 1)
    dve.memset(idle[:, :], 0.0)
    for i in range(TT):
        ins = dve.bn_aggr(mv[:, i, :], stats[:, i, :])
    ins.then_inc(step, 1)


def inverse_deviation(pool, sem, tag, blk, mv, rstd, neghalf, eps):
    pool.wait_ge(sem(f"{tag}_ln_step"), blk * 2 + 2)
    pool.wait_ge(sem(f"{tag}_xn_ready"), blk * TT + 1)
    pool.tensor_tensor(rstd[:, :], mv[:, :, 1], eps[:, :], ALU.add).then_inc(sem(f"{tag}_rstd"), 1)
    pool.wait_ge(sem(f"{tag}_rstd"), blk * 2 + 1)
    pool.tensor_tensor(rstd[:, :], rstd[:, :], neghalf[:, :], ALU.pow).then_inc(sem(f"{tag}_rstd"), 1)


def normalise_tile(dve, sem, tag, n, i, blk, x_tile, xn, mv, rstd):
    dve.wait_ge(sem(f"{tag}_rstd"), blk * 2 + 2)
    dve.wait_ge(sem(f"{tag}_xn_turned"), n + 1)
    dve.tensor_scalar(xn, x_tile, mv[:, i, 0:1], rstd[:, i:i + 1], ALU.subtract, ALU.mult)\
       .then_inc(sem(f"{tag}_xn_ready"), 1)


def turn_tile(pe, sem, tag, n, xn, bank, ident):
    pe.wait_ge(sem(f"{tag}_xn_ready"), n + 2)
    pe.wait_ge(sem(f"{tag}_modulated"), n + 1)
    for kt in range(KT):
        last = pe.transpose(bank[:, kt * P:(kt + 1) * P], xn[:, kt * P:(kt + 1) * P], ident[:, :])
    last.then_inc(sem(f"{tag}_xn_turned"), 1)


def modulate_tile(act, sem, tag, n, bank, full, scale, shift):
    act.wait_ge(sem(f"{tag}_xn_turned"), n + 3)
    act.wait_ge(sem(f"{tag}_h_split"), n + 1)
    for kt in range(KT):
        last = act.activation(full[:, kt * P:(kt + 1) * P], bank[:, kt * P:(kt + 1) * P], ACT.Identity,
                              bias=shift[:, kt:kt + 1], scale=scale[:, kt:kt + 1])
    last.then_inc(sem(f"{tag}_modulated"), 1)


def split_tile(dve, sem, tag, n, full, high, low):
    view = full.rearrange("p (k t) -> p k t", k=KT)
    dve.wait_ge(sem(f"{tag}_modulated"), n + 3)
    dve.tensor_copy(high, view).then_inc(sem(f"{tag}_h_high"), 1)
    dve.wait_ge(sem(f"{tag}_h_high"), n + 1)
    dve.tensor_tensor(low, view, high, ALU.subtract).then_inc(sem(f"{tag}_h_split"), 1)


def project_stage(nc, sem, sb0, ps, x, w_in, conv_w, conv_b, dt_bias, c, w_mod, xz_dram,
                  ident, upto, after, after_r, ones, neghalf, eps, modrow, modcol, dt_raw):
    with ExitStack() as st:
        def sb(name, shape, dt=F32):
            return sb0(name, shape, dt, st)

        win_h = sb("win_h", [P, KT, DIN], F32R)
        win_l = sb("win_l", [P, KT, DIN], F32R)
        raw = sb("win_raw", [P, 2, KT, WP])
        hT_h = sb("hT_h", [P, 2, KT, TB], F32R)
        hT_l = sb("hT_l", [P, 2, KT, TB], F32R)
        xblk = sb("xblk", [P, TT, D])
        xn = sb("xn", [P, 2, D])
        hT = sb("hT", [P, 2, D])
        xraw = sb("xraw", [P, NXBC, TAPS - 1 + TB])
        conv = sb("conv", [P, 2, TB])
        stage = sb("stage", [P, 6, TB])
        wm = sb("wm", [P, 2, KT, D])
        dtT = sb("dtT", [P, TB])
        cw = sb("cw", [P, NXBC, TAPS])
        cb = sb("cb", [P, NXBC])
        dtb = sb("dtb", [P, NH])
        ccol = sb("ccol", [P, KT])
        csilu = sb("csilu", [P, KT])
        cwide = sb("cwide", [P, KT, P])
        idle = sb("idle", [P, 1])
        stats = sb("stats", [P, TT, 6])
        mv = sb("mv", [P, TT, 2])
        rstd = sb("rstd", [P, TT])

        turn_bank = [ps[:, 0, :], ps[:, 1, :]]
        acc_bank = [ps[:, 2 + q, :] for q in range(4)]
        dt_bank = ps[:, 6, :]
        mod_bank = ps[:, 7, :]
        stored = [sem(f"stored{k}") for k in range(6)]

        made = []
        for j in range(NJ):
            if j > NXBC:
                made.append((True, j - 1 - NXBC))
            if 3 <= j < 3 + NXBC:
                made.append((False, j - 3))

        def slot_of(item):
            return made.index(item) % 6

        def turn_of(item):
            return made.index(item) // 6

        with nc.Block() as block:
            @block.sync
            def _(sp):
                for t in stored:
                    sp.sem_inc(t, 16)
                sp.dma_start(ccol[:, :], c).then_inc(sem("c_loaded"), 16)
                for r in range(2):
                    sp.dma_start(wm[:, r, :, :], w_mod[:, :, r * D:(r + 1) * D]).then_inc(sem(f"wm_loaded{r}"), 16)
                for dst, src in ((cw[:, :, :], conv_w), (cb[:, :], conv_b), (dtb[:, :], dt_bias)):
                    sp.dma_start(dst, src).then_inc(sem("params_loaded"), 16)
                for i in range(NWP):
                    if i >= 2:
                        sp.wait_ge(sem("win_low"), i - 1)
                    sp.dma_start(raw[:, i % 2, :, :], w_in[:, :, i * WP:(i + 1) * WP])\
                      .then_inc(sem(f"win_loaded{i % 2}"), 16)
                for r in range(2, 4):
                    sp.wait_ge(sem("mod_product"), r - 1)
                    sp.dma_start(wm[:, r % 2, :, :], w_mod[:, :, r * D:(r + 1) * D])\
                      .then_inc(sem(f"wm_loaded{r % 2}"), 16)
                with sp.Fori(0, NB) as b:
                    for item in made:
                        is_z, t = item
                        k = slot_of(item)
                        if is_z:
                            sp.wait_ge(sem("evacuated"), b * NJ + (1 + NXBC + t) + 1 + 3)
                        else:
                            sp.wait_ge(sem("conv_staged"), b * NXBC + t + 1 + 2)
                        tile_at = NXBC + t if is_z else t
                        sp.dma_start(
                            xz_dram[bass.ds(b * TT, TT), :, tile_at, :].rearrange("c p t -> p c t"),
                            stage[:, k, :].rearrange("p (c t) -> p c t", c=TT)).then_inc(stored[k], 16)
                for r in range(4, 6):
                    sp.wait_ge(sem("mod_product"), r - 1)
                    sp.dma_start(wm[:, r % 2, :, :], w_mod[:, :, r * D:(r + 1) * D])\
                      .then_inc(sem(f"wm_loaded{r % 2}"), 16)
                for t in stored:
                    sp.wait_ge(t, 16 + 16 * (NST // 6) * NB)

            @block.gpsimd
            def _(pool):
                pool.memset(ones[:, :], 1.0).then_inc(sem("const_made"), 1)
                pool.memset(neghalf[:, :], -0.5)
                pool.memset(eps[:, :], EPS)
                pool.memset(ident[:, :], 0.0).then_inc(sem("const_made"), 1)
                pool.wait_ge(sem("const_made"), 2)
                pool.affine_select(out=ident[:, :], in_=ident[:, :], compare_op=ALU.not_equal, fill=1.0, base=0,
                                   pattern=[[-1, P]], channel_multiplier=1).then_inc(sem("const_made"), 1)
                pool.affine_select(out=upto[:, :], in_=ones[:, :], compare_op=ALU.is_ge, fill=0.0, base=0,
                                   pattern=[[1, P]], channel_multiplier=-1).then_inc(sem("const_made"), 1)
                pool.affine_select(out=after[:, :], in_=ones[:, :], compare_op=ALU.is_gt, fill=0.0, base=0,
                                   pattern=[[-1, P]], channel_multiplier=1).then_inc(sem("const_made"), 1)
                with pool.Fori(0, NB) as b:
                    pool.wait_ge(sem("p_xn_ready"), b * TT + 1)
                    pool.dma_start(xblk[:, :, :],
                                   x[bass.ds(b * TT, TT), :, :].rearrange("t p d -> p t d"))\
                        .then_inc(sem("x_loaded"), 16)
                    inverse_deviation(pool, sem, "p", b, mv, rstd, neghalf, eps)

            @block.vector
            def _(dve):
                dve.sem_inc(sem("p_h_split"), 2)
                dve.sem_inc(sem("p_xn_ready"), 1)
                dve.memset(xraw[:, :, 0:TAPS - 1], 0.0).then_inc(sem("tail_kept"), 1)
                dve.wait_ge(sem("c_silu"), 1)
                dve.tensor_copy(cwide[:, :, :], csilu[:, :].unsqueeze(2).broadcast_to([P, KT, P]))\
                   .then_inc(sem("c_wide"), 1)
                dve.wait_ge(sem("const_made"), 5)
                dve.tensor_copy(after_r[:, :], after[:, :]).then_inc(sem("after_rounded"), 1)

                def keep_columns(n, row):
                    dve.wait_ge(sem("mod_turned"), n + 1)
                    src = dt_bank.rearrange("p (k t) -> p k t", k=KT)[:, :, 0]
                    dve.tensor_scalar(modcol[:, n, :], src, 1.0 if row in (1, 4) else 0.0, None, ALU.add)\
                       .then_inc(sem("mod_column"), 1)

                def normalise(b, i):
                    n = b * TT + i
                    normalise_tile(dve, sem, "p", n, i, b, xblk[:, i, :], xn[:, i % 2, :], mv, rstd)

                def statistics(b):
                    dve.wait_ge(sem("x_loaded"), b * 16 + 16)
                    tile_statistics(dve, sem, "p", b, xblk, stats, mv, idle)

                def split(b, i, slot):
                    split_tile(dve, sem, "p", b * TT + i, hT[:, i % 2, :],
                               hT_h[:, slot, :, i * P:(i + 1) * P] if isinstance(slot, int) else
                               hT_h[:, bass.ds(slot, 1), :, i * P:(i + 1) * P].rearrange("p o k t -> p (o k) t"),
                               hT_l[:, slot, :, i * P:(i + 1) * P] if isinstance(slot, int) else
                               hT_l[:, bass.ds(slot, 1), :, i * P:(i + 1) * P].rearrange("p o k t -> p (o k) t"))

                def convolve(b, t):
                    m = b * NXBC + t
                    u = conv[:, t % 2, :]
                    dve.wait_ge(sem("evacuated"), b * NJ + t + 2 + 3)
                    dve.wait_ge(sem("tail_kept"), b + 1)
                    dve.wait_ge(sem("conv_staged"), m + 1)
                    dve.tensor_scalar(u, xraw[:, t, TAPS - 1:TAPS - 1 + TB], cw[:, t, TAPS - 1:TAPS], cb[:, t:t + 1],
                                      ALU.mult, ALU.add).then_inc(sem("conv_step"), 1)
                    for k in range(TAPS - 1):
                        dve.wait_ge(sem("conv_step"), m * TAPS + k + 1)
                        dve.scalar_tensor_tensor(out=u, in0=xraw[:, t, k:k + TB], scalar=cw[:, t, k:k + 1], in1=u,
                                                 op0=ALU.mult, op1=ALU.add).then_inc(sem("conv_step"), 1)

                def keep_tail(b):
                    dve.wait_ge(sem("conv_step"), (b * NXBC + NXBC) * TAPS)
                    dve.tensor_copy(xraw[:, :, 0:TAPS - 1], xraw[:, :, TB:TB + TAPS - 1])\
                       .then_inc(sem("tail_kept"), 1)

                def add_dt_bias(b):
                    dve.wait_ge(sem("dt_turned"), b + 2)
                    dve.tensor_tensor(dt_raw[:, bass.ds(b * TT, TT), :] if not isinstance(b, int) else
                                      dt_raw[:, b * TT:(b + 1) * TT, :],
                                      dt_bank.rearrange("p (t c) -> p t c", t=TT)[:, :, P - NH:P],
                                      dtb[:, :].unsqueeze(1).broadcast_to([P, TT, NH]), ALU.add)\
                       .then_inc(sem("dt_kept"), 1)

                def split_weights(i):
                    dve.wait_ge(sem("win_high"), i + 1)
                    cols = slice(i * WP, (i + 1) * WP)
                    dve.tensor_tensor(win_l[:, :, cols], raw[:, i % 2, :, :], win_h[:, :, cols], ALU.subtract)\
                       .then_inc(sem("win_low"), 1)

                def block_body(b, has_next, slot):
                    for t in range(NXBC):
                        if has_next and t == 0:
                            statistics(b + 1)
                        if has_next and t in (1, 3, 6, 8):
                            normalise(b + 1, (1, 3, 6, 8).index(t))
                        convolve(b, t)
                        if t == 2:
                            add_dt_bias(b)
                        if has_next and t in (5, 8, 9):
                            split(b + 1, (5, 8, 9).index(t), slot)
                    keep_tail(b)
                    if has_next:
                        split(b + 1, 3, slot)

                statistics(0)
                normalise(0, 0)
                normalise(0, 1)
                keep_columns(0, 0)
                keep_columns(1, 1)
                for i in range(TT):
                    split(0, i, 0)
                    if i + 2 < TT:
                        normalise(0, i + 2)
                    split_weights(i)
                for i in range(TT, NWP):
                    split_weights(i)
                dve.wait_ge(sem("params_loaded"), 48)
                with dve.Fori(0, NB - 1) as b:
                    block_body(b, True, (b + 1) % 2)
                block_body(NB - 1, False, None)
                keep_columns(2, 3)
                keep_columns(3, 4)

            @block.scalar
            def _(act):
                act.sem_inc(sem("p_modulated"), 2)
                act.sem_inc(sem("evacuated"), 3)
                act.sem_inc(sem("conv_staged"), 2)
                act.wait_ge(sem("c_loaded"), 16)
                act.activation(csilu[:, :], ccol[:, :], ACT.Silu).then_inc(sem("c_silu"), 1)

                def keep_row(r):
                    act.wait_ge(sem("mod_product"), r + 1)
                    act.activation(modrow[:, r, :], mod_bank, ACT.Copy).then_inc(sem("mod_row"), 1)

                def round_weights(i):
                    act.wait_ge(sem(f"win_loaded{i % 2}"), 16 * (i // 2) + 16)
                    act.activation(win_h[:, :, i * WP:(i + 1) * WP], raw[:, i % 2, :, :], ACT.Copy)\
                       .then_inc(sem("win_high"), 1)

                def modulate(b, i):
                    modulate_tile(act, sem, "p", b * TT + i, turn_bank[i % 2], hT[:, i % 2, :],
                                  modcol[:, 1, :], modcol[:, 0, :])

                def evacuate(b, j):
                    act.wait_ge(sem("product_ready"), b * NJ + j + 1)
                    if j == 0:
                        act.wait_ge(sem("dt_turned"), b + 1)
                        act.activation(dtT[:, :], acc_bank[0], ACT.Copy).then_inc(sem("evacuated"), 1)
                    elif j <= NXBC:
                        act.wait_ge(sem("tail_kept"), b + 1)
                        act.activation(xraw[:, j - 1, TAPS - 1:TAPS - 1 + TB], acc_bank[j % 4], ACT.Copy)\
                           .then_inc(sem("evacuated"), 1)
                    else:
                        item = (True, j - 1 - NXBC)
                        act.wait_ge(stored[slot_of(item)], b * 48 + 16 * turn_of(item) + 16)
                        act.activation(stage[:, slot_of(item), :], acc_bank[j % 4], ACT.Silu)\
                           .then_inc(sem("evacuated"), 1)

                def activate(b, t):
                    item = (False, t)
                    act.wait_ge(sem("conv_step"), (b * NXBC + t + 1) * TAPS)
                    act.wait_ge(stored[slot_of(item)], b * 48 + 16 * turn_of(item) + 16)
                    act.activation(stage[:, slot_of(item), :], conv[:, t % 2, :], ACT.Silu)\
                       .then_inc(sem("conv_staged"), 1)

                def block_body(b, has_next):
                    for j in range(NJ):
                        evacuate(b, j)
                        if 3 <= j < 3 + NXBC:
                            activate(b, j - 3)
                        if has_next and j in (4, 7, 10, 13):
                            modulate(b + 1, (j - 4) // 3)

                keep_row(0)
                keep_row(1)
                act.wait_ge(sem("mod_column"), 2)
                for i in range(TT):
                    modulate(0, i)
                    round_weights(i)
                for i in range(TT, NWP):
                    round_weights(i)
                with act.Fori(0, NB - 1) as b:
                    block_body(b, True)
                block_body(NB - 1, False)
                for r in range(2, 6):
                    keep_row(r)

            @block.tensor
            def _(pe):
                pe.sem_inc(sem("p_xn_turned"), 2)
                pe.sem_inc(sem("dt_turned"), 1)

                def mod_row(r):
                    if r >= 1:
                        pe.wait_ge(sem("mod_row"), r)
                    pe.wait_ge(sem(f"wm_loaded{r % 2}"), 16 * (r // 2) + 16)
                    for kt in range(KT):
                        last = pe.matmul(mod_bank, cwide[:, kt, :], wm[:, r % 2, kt, :], start=(kt == 0),
                                         stop=(kt == KT - 1))
                    last.then_inc(sem("mod_product"), 1)

                def turn_row(n, row):
                    pe.wait_ge(sem("mod_row"), row + 1)
                    if n >= 1:
                        pe.wait_ge(sem("mod_column"), n)
                    for kt in range(KT):
                        last = pe.transpose(dt_bank[:, kt * P:(kt + 1) * P], modrow[:, row, kt * P:(kt + 1) * P],
                                            ident[:, :])
                    last.then_inc(sem("mod_turned"), 1)

                def turn(b, i):
                    turn_tile(pe, sem, "p", b * TT + i, xn[:, i % 2, :], turn_bank[i % 2], ident)

                def project(b, j, slot, first):
                    n = b * NJ + j
                    c0 = column_of(j)
                    pe.wait_ge(sem("evacuated"), n + 1)
                    if first:
                        pe.wait_ge(sem("win_low"), (c0 + P - 1) // WP + 1)
                    if j == 0:
                        pe.wait_ge(sem("p_h_split"), b * TT + TT + 2)
                    rhs = []
                    for kt in range(KT):
                        if isinstance(slot, int):
                            rhs.append((hT_h[:, slot, kt, :], hT_l[:, slot, kt, :]))
                        else:
                            rhs.append(tuple(h[:, bass.ds(slot, 1), kt, :].rearrange("p o t -> p (o t)")
                                             for h in (hT_h, hT_l)))
                    three_pass(pe, acc_bank[j % 4],
                               [(win_h[:, kt, c0:c0 + P], win_l[:, kt, c0:c0 + P], *rhs[kt]) for kt in range(KT)])\
                        .then_inc(sem("product_ready"), 1)

                def turn_dt(b):
                    pe.wait_ge(sem("evacuated"), b * NJ + 1 + 3)
                    if isinstance(b, int) and b == 0:
                        pe.wait_ge(sem("mod_column"), 2)
                    else:
                        pe.wait_ge(sem("dt_kept"), b)
                    for i in range(TT):
                        last = pe.transpose(dt_bank[:, i * P:(i + 1) * P], dtT[:, i * P:(i + 1) * P], ident[:, :])
                    last.then_inc(sem("dt_turned"), 1)

                def block_body(b, has_next, slot, first=False):
                    for j in range(NJ):
                        project(b, j, slot, first)
                        if j == 2:
                            turn_dt(b)
                        if has_next and j in (3, 6, 9, 12):
                            turn(b + 1, (j - 3) // 3)

                pe.wait_ge(sem("c_wide"), 1)
                mod_row(0)
                pe.wait_ge(sem("const_made"), 5)
                turn_row(0, 0)
                mod_row(1)
                turn_row(1, 1)
                for i in range(TT):
                    turn(0, i)
                block_body(0, True, 0, first=True)
                with pe.Fori(1, NB - 1) as b:
                    block_body(b, True, b % 2)
                block_body(NB - 1, False, (NB - 1) % 2)
                for r in range(2, 6):
                    mod_row(r)
                    if r in (3, 4):
                        if r == 3:
                            pe.wait_ge(sem("dt_kept"), NB)
                        turn_row(r - 1, r)


def scan_stage(nc, sem, sb0, ps, x, w_out, a_log, d_skip, norm_w, xz_dram, x1_dram,
               ident, upto, after, after_r, ones, neghalf, eps, modrow, dt_raw):
    with ExitStack() as st:
        def sb(name, shape, dt=F32):
            return sb0(name, shape, dt, st)

        NC = NCH * NH
        wo_h = sb("wo_h", [P, CT, D], F32R)
        wo_l = sb("wo_l", [P, CT, D], F32R)
        wo_raw = sb("wo_raw", [P, 2, D])
        nw = sb("nw", [P, CT])
        dskip = sb("dskip", [P, CT])
        alog = sb("alog", [P, NH])
        arow = sb("arow", [P, NH])
        small = sb("small", [P, 8, NC])
        dt = sb("dt", [P, NCH, NH])
        dA = sb("dA", [P, NCH, NH])
        dA_h = sb("dA_h", [P, NCH, NH], F32R)
        dA_l = sb("dA_l", [P, NCH, NH], F32R)
        grown = sb("grown", [P, NCH, NH])
        left = sb("left", [P, NCH, NH])
        whole = sb("whole", [P, NCH, NH])
        dt_left = sb("dt_left", [P, NCH, NH])
        ga = sb("ga", [P, D])
        ga_t = sb("ga_t", [P, D])
        xz = sb("xz", [P, 2, NST, P])
        xres = sb("xres", [P, 2, D])
        step_h = sb("step_h", [P, NH, P], F32R)
        step_l = sb("step_l", [P, NH, P], F32R)
        M = sb("M", [P, 2, NH, P])
        cbm = sb("cbm", [P, P])
        btok = sb("btok", [P, P])
        xdt = sb("xdt", [P, DI])
        xdl = sb("xdl", [P, DI])
        state = sb("state", [P, DI])
        faded = sb("faded", [P, DI])
        yoff = sb("yoff", [P, DI])
        dx = sb("dx", [P, CT, P])
        y1 = sb("y1", [P, CT, P])
        y = sb("y", [P, CT, P])
        y_h = sb("y_h", [P, CT, P], F32R)
        y_l = sb("y_l", [P, CT, P], F32R)
        ysq = sb("ysq", [P, CT, P])
        ysum = sb("ysum", [P, P])
        rms = sb("rms", [P, 1])
        x1 = sb("x1", [P, 2, D])

        seg_bank = [ps[:, 0, :], ps[:, 1, :]]
        pair = ps[:, 2:4, :]
        pair_flat = pair.rearrange("p a b -> p (a b)")
        y_pair = ps[:, 4:6, :]
        y_flat = y_pair.rearrange("p a b -> p (a b)")
        out_bank = ps[:, 6, :]
        cb_ps = ps[:, 7, 0:P]
        bt_ps = ps[:, 7, P:2 * P]
        ss_ps = ps[:, 7, 2 * P:2 * P + 1]
        x_view = x.rearrange("t p d -> t p d")

        with nc.Block() as block:
            def load_xbc(eng, c, r):
                eng.dma_start(xz[:, r, 0:NXBC, :], one(xz_dram, c, 0, NXBC)).then_inc(sem(f"xbc_loaded{r}"), 16)

            def load_z(eng, c, r):
                eng.dma_start(xz[:, r, NXBC:NST, :], one(xz_dram, c, NXBC, NST)).then_inc(sem(f"z_loaded{r}"), 16)

            def load_x(eng, c, r):
                eng.dma_start(xres[:, r, :], one(x_view, c)).then_inc(sem(f"xres_loaded{r}"), 16)

            def turn(c, r):
                return c // 2 if isinstance(c, int) else (c - r) // 2

            def one(ap, c, lo=0, hi=None):
                if isinstance(c, int):
                    return ap[c] if hi is None else ap[c, :, lo:hi, :]
                if hi is not None:
                    return ap[bass.ds(c, 1), :, lo:hi, :].rearrange("o p a b -> p (o a) b")
                return ap[bass.ds(c, 1), :, :].rearrange("o p a -> p (o a)")

            def chunk_cols(ap, c):
                if isinstance(c, int):
                    return ap[:, c, :]
                return ap[:, bass.ds(c, 1), :].rearrange("p o h -> p (o h)")

            def by_head(ap, width):
                return ap.unsqueeze(2).broadcast_to([P, NH, width])

            def over_chunks(eng, body):
                body(0, 0, False, True)
                with eng.Fori(0, NCH // 2 - 1) as i:
                    body(i * 2 + 1, 1, True, True)
                    body(i * 2 + 2, 0, True, True)
                body(NCH - 1, 1, True, False)

            @block.sync
            def _(sp):
                sp.sem_inc(sem("x1_stored0"), 16)
                sp.sem_inc(sem("x1_stored1"), 16)
                sp.dma_start(alog[:, :], a_log).then_inc(sem("scan_params"), 16)
                sp.dma_start(nw[:, :], norm_w).then_inc(sem("scan_params"), 16)
                for half in range(2):
                    sp.dma_start(dskip[half * HD:(half + 1) * HD, :], d_skip[half]).then_inc(sem("scan_params"), 16)
                for c_ in range(2):
                    load_xbc(sp, c_, c_)
                    load_z(sp, c_, c_)
                    load_x(sp, c_, c_)
                for t in range(CT):
                    if t >= 2:
                        sp.wait_ge(sem("wo_scaled"), t - 1)
                    sp.dma_start(wo_raw[:, t % 2, :], w_out[t]).then_inc(sem(f"wo_loaded{t % 2}"), 16)

                def body(c, r, has_prev, has_second):
                    if has_second:
                        sp.wait_ge(sem("off_ready"), c + 1)
                        sp.wait_ge(sem("dx_made"), c + 1)
                        load_xbc(sp, c + 2, r)
                    if has_prev:
                        sp.wait_ge(sem("x1_made"), c)
                        sp.dma_start(one(x1_dram, c - 1), x1[:, 1 - r, :]).then_inc(sem(f"x1_stored{1 - r}"), 16)
                        if has_second or (isinstance(c, int) and c < NCH - 1):
                            load_x(sp, c + 1, 1 - r)
                    if has_second:
                        sp.wait_ge(sem("gated"), c + 1)
                        load_z(sp, c + 2, r)

                body(0, 0, False, True)
                with sp.Fori(0, NCH // 2 - 2) as i:
                    body(i * 2 + 1, 1, True, True)
                    body(i * 2 + 2, 0, True, True)
                body(NCH - 3, 1, True, True)
                body(NCH - 2, 0, True, False)
                body(NCH - 1, 1, True, False)
                sp.wait_ge(sem("x1_made"), NCH)
                sp.dma_start(x1_dram[NCH - 1], x1[:, 1, :]).then_inc(sem("x1_stored1"), 16)
                for r in range(2):
                    sp.wait_ge(sem(f"x1_stored{r}"), 16 + 16 * NCH // 2)

            @block.gpsimd
            def _(pool):
                pool.memset(state[:, :], 0.0).then_inc(sem("state_made"), 1)

                def skip_part(c, r):
                    pool.wait_ge(sem(f"xbc_loaded{r}"), turn(c, r) * 16 + 16)
                    pool.tensor_tensor(dx[:, :, :], xz[:, r, 0:CT, :], dskip[:, :].unsqueeze(2).broadcast_to([P, CT, P]),
                                       ALU.mult).then_inc(sem("dx_made"), 1)

                def low_steps(c):
                    pool.tensor_tensor(step_l[:, :, :], upto[:, :].unsqueeze(1).broadcast_to([P, NH, P]),
                                       by_head(chunk_cols(dA_l, c), P), ALU.mult).then_inc(sem("step_low"), 1)

                def body(c, r, has_prev, has_next):
                    pool.wait_ge(sem("state_made"), c + 1)
                    pool.wait_ge(sem("whole_made"), 1)
                    pool.tensor_tensor(faded[:, :].rearrange("p (h d) -> p h d", h=NH),
                                       state[:, :].rearrange("p (h d) -> p h d", h=NH),
                                       by_head(chunk_cols(whole, c), HD), ALU.mult).then_inc(sem("state_faded"), 1)
                    if has_next:
                        pool.wait_ge(sem("seg_read"), (c + 1) * 4)
                        low_steps(c + 1)
                        pool.wait_ge(sem("skip_added"), c + 1)
                        skip_part(c + 1, 1 - r)
                    pool.wait_ge(sem("rms_step"), c + 1)
                    pool.tensor_tensor(rms[:, :], rms[:, :], neghalf[:, 0:1], ALU.pow)\
                        .then_inc(sem("rms_inverted"), 1)

                pool.wait_ge(sem("scan_params"), 64)
                skip_part(0, 0)
                pool.wait_ge(sem("dA_split"), 2)
                low_steps(0)
                over_chunks(pool, body)

            @block.vector
            def _(dve):
                link = [0]

                def linked(ins):
                    link[0] += 1
                    ins.then_inc(sem("scan_link"), 1)
                    dve.wait_ge(sem("scan_link"), link[0])

                raw = dt_raw[:, :, :].rearrange("p c h -> p (c h)")
                neg, na, e, t, d, z, q, sp_ = (small[:, k, :] for k in range(8))
                linked(dve.tensor_scalar(neg, raw, -1.0, None, ALU.mult))
                dve.tensor_tensor(na, raw, neg, ALU.min).then_inc(sem("dt_neg"), 1)
                dve.wait_ge(sem("dt_exp"), 1)
                dve.tensor_scalar(t, e, 1.0, None, ALU.add).then_inc(sem("dt_one"), 1)
                dve.wait_ge(sem("dt_one"), 1)
                linked(dve.tensor_scalar(d, t, 1.0, None, ALU.subtract))
                linked(dve.tensor_scalar(z, d, 0.0, None, ALU.is_equal))
                linked(dve.tensor_tensor(d, d, z, ALU.add))
                linked(dve.reciprocal(q, d))
                linked(dve.tensor_tensor(q, q, e, ALU.mult))
                dve.wait_ge(sem("dt_ln"), 1)
                linked(dve.tensor_tensor(q, q, sp_, ALU.mult))
                linked(dve.tensor_tensor(z, z, e, ALU.mult))
                linked(dve.tensor_tensor(q, q, z, ALU.add))
                linked(dve.scalar_tensor_tensor(out=dt[:, :, :].rearrange("p c h -> p (c h)"), in0=raw, scalar=0.0,
                                                in1=q, op0=ALU.max, op1=ALU.add))
                dve.wait_ge(sem("a_exp"), 1)
                dve.scalar_tensor_tensor(out=dA[:, :, :], in0=dt[:, :, :], scalar=-1.0,
                                         in1=arow[:, :].unsqueeze(1).broadcast_to([P, NCH, NH]),
                                         op0=ALU.mult, op1=ALU.mult).then_inc(sem("dA_made"), 1)
                dve.wait_ge(sem("dA_made"), 1)
                dve.tensor_copy(dA_h[:, :, :], dA[:, :, :]).then_inc(sem("dA_split"), 1)
                dve.wait_ge(sem("dA_split"), 1)
                dve.tensor_tensor(dA_l[:, :, :], dA[:, :, :], dA_h[:, :, :], ALU.subtract).then_inc(sem("dA_split"), 1)
                dve.wait_ge(sem("decays_exp"), 1)
                linked(dve.tensor_tensor(dt_left[:, :, :], dt[:, :, :], left[:, :, :], ALU.mult))

                def set_gate(dst, tmp, row):
                    linked(dve.scalar_tensor_tensor(out=dst, in0=row, scalar=-1.0, in1=row, op0=ALU.mult, op1=ALU.max))
                    linked(dve.tensor_scalar(tmp, row, 0.0, 2.0, ALU.is_ge, ALU.mult))
                    linked(dve.tensor_scalar(tmp, tmp, -1.0, None, ALU.add))
                    linked(dve.scalar_tensor_tensor(out=dst, in0=dst, scalar=0.25, in1=tmp, op0=ALU.max, op1=ALU.mult))

                set_gate(ga[:, :], ga_t[:, :], modrow[:, 2, :])
                linked(dve.tensor_copy(x1[:, 0, :], modrow[:, 5, :]))
                set_gate(modrow[:, 5, :], ga_t[:, :], x1[:, 0, :])
                dve.wait_ge(sem("scan_params"), 64)
                for t_ in range(CT):
                    dve.wait_ge(sem(f"wo_loaded{t_ % 2}"), 16 * (t_ // 2) + 16)
                    dve.scalar_tensor_tensor(out=yoff[:, (t_ % 2) * D:(t_ % 2 + 1) * D], in0=wo_raw[:, t_ % 2, :],
                                             scalar=nw[:, t_:t_ + 1], in1=ga[:, :], op0=ALU.mult, op1=ALU.mult)\
                       .then_inc(sem("wo_scaled"), 1)
                    dve.wait_ge(sem("wo_scaled"), t_ + 1)
                    scaled = yoff[:, (t_ % 2) * D:(t_ % 2 + 1) * D]
                    linked(dve.tensor_copy(wo_h[:, t_, :], scaled))
                    linked(dve.tensor_tensor(wo_l[:, t_, :], scaled, wo_h[:, t_, :], ALU.subtract))

                def high_steps(c):
                    dve.tensor_tensor(step_h[:, :, :], upto[:, :].unsqueeze(1).broadcast_to([P, NH, P]),
                                      by_head(chunk_cols(dA_h, c), P), ALU.mult).then_inc(sem("step_high"), 1)

                def mask_cb(c):
                    dve.wait_ge(sem("cb_ready"), c + 1)
                    if not (isinstance(c, int) and c == 0):
                        dve.wait_ge(sem("M_ready"), c * 4)
                    dve.tensor_tensor(cbm[:, :], cb_ps, upto[:, :], ALU.mult).then_inc(sem("cb_masked"), 1)

                def mask_decay(c, r):
                    dve.wait_ge(sem("cb_masked"), c + 1)
                    for g in range(4):
                        dve.wait_ge(sem("seg_exp"), c * 4 + g + 1)
                        m = M[:, r, 4 * g:4 * g + 4, :]
                        dve.tensor_tensor(m, m, cbm[:, :].unsqueeze(1).broadcast_to([P, 4, P]), ALU.mult)\
                           .then_inc(sem("M_ready"), 1)

                def weigh_x(c):
                    dve.wait_ge(sem("x_turned"), c + 1)
                    src = pair_flat.rearrange("p (h d) -> p h d", h=NH)
                    dve.tensor_tensor(xdt[:, :].rearrange("p (h d) -> p h d", h=NH), src,
                                      by_head(chunk_cols(dt, c), HD), ALU.mult)
                    dve.tensor_tensor(xdl[:, :].rearrange("p (h d) -> p h d", h=NH), src,
                                      by_head(chunk_cols(dt_left, c), HD), ALU.mult).then_inc(sem("x_weighed"), 1)

                def body(c, r, has_prev, has_next):
                    if has_next:
                        dve.wait_ge(sem("seg_read"), (c + 1) * 4)
                        high_steps(c + 1)
                        mask_cb(c + 1)
                    dve.wait_ge(sem("off_ready"), c + 1)
                    dve.tensor_tensor(yoff[:, :].rearrange("p (h d) -> p h d", h=NH),
                                      pair_flat.rearrange("p (h d) -> p h d", h=NH),
                                      by_head(chunk_cols(grown, c), HD), ALU.mult).then_inc(sem("off_scaled"), 1)
                    if has_prev:
                        finish(c - 1, 1 - r)
                    if has_next:
                        mask_decay(c + 1, 1 - r)
                    dve.wait_ge(sem("y_summed"), c + 1)
                    dve.wait_ge(sem("dx_made"), c + 1)
                    dve.tensor_tensor(y1[:, :, :].rearrange("p t l -> p (t l)"), y_flat,
                                      dx[:, :, :].rearrange("p t l -> p (t l)"), ALU.add)\
                       .then_inc(sem("skip_added"), 1)
                    dve.wait_ge(sem("skip_added"), c + 1)
                    if has_prev:
                        dve.wait_ge(sem("y_squared"), c)
                        dve.wait_ge(sem("y_low"), c)
                    dve.wait_ge(sem(f"z_loaded{r}"), turn(c, r) * 16 + 16)
                    dve.tensor_tensor(y[:, :, :], y1[:, :, :], xz[:, r, NXBC:NST, :], ALU.mult)\
                       .then_inc(sem("gated"), 1)
                    dve.wait_ge(sem("y_high"), c + 1)
                    dve.tensor_tensor(y_l[:, :, :], y[:, :, :], y_h[:, :, :], ALU.subtract).then_inc(sem("y_low"), 1)
                    dve.wait_ge(sem("y_squared"), c + 1)
                    dve.tensor_reduce(ysum[:, :], ysq[:, :, :].rearrange("p t l -> p l t"), AX.X, ALU.add)\
                       .then_inc(sem("squares_summed"), 1)
                    dve.wait_ge(sem("states_ready"), c + 1)
                    dve.wait_ge(sem("state_faded"), c + 1)
                    dve.tensor_tensor(state[:, :], faded[:, :], pair_flat, ALU.add).then_inc(sem("state_made"), 1)
                    if has_next:
                        weigh_x(c + 1)
                    dve.wait_ge(sem("rms_ready"), c + 1)
                    if has_prev:
                        dve.wait_ge(sem("x1_made"), c)
                    dve.tensor_scalar(rms[:, :], ss_ps, 1.0 / DI, EPS, ALU.mult, ALU.add)\
                       .then_inc(sem("rms_step"), 1)

                def finish(c, r):
                    dve.wait_ge(sem("out_ready"), c + 1)
                    dve.wait_ge(sem("rms_inverted"), c + 1)
                    k = turn(c, r)
                    dve.wait_ge(sem(f"xres_loaded{r}"), k * 16 + 16)
                    dve.wait_ge(sem(f"x1_stored{r}"), k * 16 + 16)
                    dve.scalar_tensor_tensor(out=x1[:, r, :], in0=out_bank, scalar=rms[:, 0:1], in1=xres[:, r, :],
                                             op0=ALU.mult, op1=ALU.add).then_inc(sem("x1_made"), 1)

                high_steps(0)
                mask_cb(0)
                mask_decay(0, 0)
                weigh_x(0)
                over_chunks(dve, body)
                finish(NCH - 1, 1)

            @block.scalar
            def _(act):
                na, e, t, sp_ = (small[:, k, :] for k in (1, 2, 3, 7))
                act.wait_ge(sem("scan_params"), 64)
                act.activation(arow[:, :], alog[:, :], ACT.Exp).then_inc(sem("a_exp"), 1)
                act.wait_ge(sem("dt_neg"), 1)
                act.activation(e, na, ACT.Exp).then_inc(sem("dt_exp"), 1)
                act.wait_ge(sem("dt_one"), 1)
                act.activation(sp_, t, ACT.Ln).then_inc(sem("dt_ln"), 1)
                act.wait_ge(sem("decay_sums"), 1)
                flat = lambda a: a[:, :, :].rearrange("p c h -> p (c h)")
                act.activation(flat(grown), seg_bank[0][:, 0:NC], ACT.Exp)
                act.activation(flat(left), seg_bank[0][:, NC:2 * NC], ACT.Exp).then_inc(sem("decays_exp"), 1)
                act.activation(flat(whole), seg_bank[1][:, 0:NC], ACT.Exp).then_inc(sem("whole_made"), 1)

                def decay(c, r):
                    for g in range(4):
                        act.wait_ge(sem("seg_read"), c * 4 + g + 1)
                        act.activation(M[:, r, 4 * g:4 * g + 4, :].rearrange("p h l -> p (h l)"), seg_bank[g % 2],
                                       ACT.Exp).then_inc(sem("seg_exp"), 1)

                def keep_b(c):
                    act.wait_ge(sem("b_turned"), c + 1)
                    act.activation(btok[:, :], bt_ps, ACT.Copy).then_inc(sem("b_kept"), 1)

                def body(c, r, has_prev, has_next):
                    if has_next:
                        decay(c + 1, 1 - r)
                    act.wait_ge(sem("gated"), c + 1)
                    if has_prev:
                        act.wait_ge(sem("out_ready"), c)
                    act.activation(y_h[:, :, :], y[:, :, :], ACT.Copy).then_inc(sem("y_high"), 1)
                    if has_prev:
                        act.wait_ge(sem("squares_summed"), c)
                    act.activation(ysq[:, :, :], y[:, :, :], ACT.Square).then_inc(sem("y_squared"), 1)
                    if has_next:
                        keep_b(c + 1)

                decay(0, 0)
                keep_b(0)
                over_chunks(act, body)

            @block.tensor
            def _(pe):
                pe.wait_ge(sem("dA_made"), 1)
                flat = dA[:, :, :].rearrange("p c h -> p (c h)")
                pe.matmul(seg_bank[0][:, 0:NC], upto[:, :], flat, start=True, stop=True)
                pe.matmul(seg_bank[0][:, NC:2 * NC], after[:, :], flat, start=True, stop=True)
                pe.matmul(seg_bank[1][:, 0:NC], ones[:, :], flat, start=True, stop=True)\
                  .then_inc(sem("decay_sums"), 1)

                def cb(c, r):
                    pe.wait_ge(sem(f"xbc_loaded{r}"), turn(c, r) * 16 + 16)
                    pe.matmul(cb_ps, xz[:, r, CT, :], xz[:, r, CT + 1, :], start=True, stop=True)\
                      .then_inc(sem("cb_ready"), 1)

                def segments(c, first=False):
                    pe.wait_ge(sem("step_high"), c + 1)
                    pe.wait_ge(sem("step_low"), c + 1)
                    for g in range(4):
                        if first:
                            pe.wait_ge(sem("whole_made"), 1)
                            if g >= 2:
                                pe.wait_ge(sem("seg_exp"), g - 1)
                        else:
                            pe.wait_ge(sem("seg_exp"), c * 4 + g - 1)
                        pe.matmul(seg_bank[g % 2], after_r[:, :],
                                  step_h[:, 4 * g:4 * g + 4, :].rearrange("p h l -> p (h l)"), start=True, stop=False)
                        pe.matmul(seg_bank[g % 2], after_r[:, :],
                                  step_l[:, 4 * g:4 * g + 4, :].rearrange("p h l -> p (h l)"), start=False, stop=True)\
                          .then_inc(sem("seg_read"), 1)

                def turn_x(c, r):
                    pe.wait_ge(sem("state_made"), c + 1)
                    for t in range(CT):
                        last = pe.transpose(pair_flat[:, t * P:(t + 1) * P], xz[:, r, t, :], ident[:, :])
                    last.then_inc(sem("x_turned"), 1)
                    pe.wait_ge(sem("cb_masked"), c + 1)
                    pe.transpose(bt_ps, xz[:, r, CT, :], ident[:, :]).then_inc(sem("b_turned"), 1)

                def body(c, r, has_prev, has_next):
                    if has_next:
                        if has_prev:
                            pe.wait_ge(sem("rms_step"), c)
                        else:
                            pe.wait_ge(sem("b_kept"), 1)
                        cb(c + 1, 1 - r)
                    pe.wait_ge(sem("x_weighed"), c + 1)
                    pe.wait_ge(sem("state_made"), c + 1)
                    for n in range(2):
                        last = pe.matmul(pair[:, n, :], xz[:, r, CT + 1, :], state[:, n * 512:(n + 1) * 512],
                                         start=True, stop=True)
                    last.then_inc(sem("off_ready"), 1)
                    if has_prev:
                        project_out(c - 1)
                    if has_next:
                        segments(c + 1)
                    pe.wait_ge(sem("off_scaled"), c + 1)
                    pe.wait_ge(sem("M_ready"), c * 4 + 4)
                    if has_prev:
                        pe.wait_ge(sem("skip_added"), c)
                    for t in range(CT):
                        y_t = y_flat[:, t * P:(t + 1) * P]
                        pe.matmul(y_t, yoff[:, t * P:(t + 1) * P], ident[:, :], start=True, stop=False,
                                  skip_group_check=True)
                        for half in range(2):
                            h = 2 * t + half
                            last = pe.matmul(y_t[half * HD:(half + 1) * HD, :], xdt[:, h * HD:(h + 1) * HD],
                                             M[:, r, h, :], start=False, stop=True, skip_group_check=True)
                    last.then_inc(sem("y_summed"), 1)
                    pe.wait_ge(sem("b_kept"), c + 1)
                    for n in range(2):
                        last = pe.matmul(pair[:, n, :], btok[:, :], xdl[:, n * 512:(n + 1) * 512], start=True, stop=True)
                    last.then_inc(sem("states_ready"), 1)
                    if has_next:
                        pe.wait_ge(sem("state_made"), c + 2)
                        turn_x(c + 1, 1 - r)
                    if has_next:
                        pe.wait_ge(sem("b_kept"), c + 2)
                    pe.wait_ge(sem("squares_summed"), c + 1)
                    pe.matmul(ss_ps, ysum[:, :], ones[:, 0:1], start=True, stop=True).then_inc(sem("rms_ready"), 1)

                def project_out(c):
                    pe.wait_ge(sem("y_low"), c + 1)
                    three_pass(pe, out_bank, [(y_h[:, t, :], y_l[:, t, :], wo_h[:, t, :], wo_l[:, t, :])
                                              for t in range(CT)]).then_inc(sem("out_ready"), 1)

                cb(0, 0)
                segments(0, first=True)
                turn_x(0, 0)
                over_chunks(pe, body)
                project_out(NCH - 1)


def ffn_stage(nc, sem, sb0, ps, w_gu, w_down, x1_dram, out, ident, neghalf, eps, modrow, modcol):
    with ExitStack() as st:
        def sb(name, shape, dt=F32):
            return sb0(name, shape, dt, st)

        HT = 8
        NG = 2
        gu_h = sb("gu_h", [P, 4, 2, KT, P], F32R)
        gu_l = sb("gu_l", [P, 4, 2, KT, P], F32R)
        dn_h = sb("dn_h", [P, 4, D], F32R)
        dn_l = sb("dn_l", [P, 4, D], F32R)
        raw = sb("ffn_raw", [P, 2, 1024])
        dn_s = sb("dn_s", [P, 2, D])
        acc = sb("acc", [P, HT, D])
        gT_h = sb("gT_h", [P, KT, HT * P], F32R)
        gT_l = sb("gT_l", [P, KT, HT * P], F32R)
        xn = sb("xn2", [P, 2, D])
        hT = sb("hT2", [P, 2, D])
        sg = sb("sg", [P, 2, TB])
        hid = sb("hid", [P, 4, TB])
        mag = sb("mag", [P, 4, TB])
        top = sb("top", [P, 2, TB])
        low = sb("low", [P, 2, TB])
        first = sb("first", [P, 2, TB], BF16)
        both = sb("both", [P, 2, TB], BF16)
        lead = sb("lead", [P, TB], BF16)
        keep = sb("keep", [P, 4, TB], BF16)
        hs_h = sb("hs_h", [P, 4, TB], F32R)
        hs_l = sb("hs_l", [P, 4, TB], F32R)
        idle = sb("idle2", [P, 1])
        stats = sb("stats2", [P, TT, 6])
        mv = sb("mv2", [P, TT, 2])
        rstd = sb("rstd2", [P, TT])

        gate_bank = [ps[:, 0, :], ps[:, 1, :]]
        up_bank = [ps[:, 2, :], ps[:, 3, :]]
        down_bank = [ps[:, 4, :], ps[:, 5, :]]
        turn_bank = [ps[:, 6, :], ps[:, 7, :]]
        NCN = 2 * NIC
        x1_t = x1_dram
        out_t = out

        with nc.Block() as block:
            @block.sync
            def _(sp):
                sp.sem_inc(sem("f_half_start"), 1)
                with sp.Fori(0, 2) as h:
                    sp.wait_ge(sem("f_half_start"), h + 1)
                    sp.dma_start(acc[:, :, :], x1_t[bass.ds(h * HT, HT), :, :].rearrange("t p d -> p t d"))\
                      .then_inc(sem("acc_loaded"), 16)
                    sp.wait_ge(sem("acc_done"), (h + 1) * 64)
                    sp.dma_start(out_t[bass.ds(h * HT, HT), :, :].rearrange("t p d -> p t d"), acc[:, :, :])\
                      .then_inc(sem("out_stored"), 16)
                    sp.wait_ge(sem("out_stored"), h * 16 + 16)
                    sp.sem_inc(sem("f_half_start"), 1)

            @block.gpsimd
            def _(pool):
                pool.sem_inc(sem("f_low"), 2)
                with pool.Fori(0, 2) as h:
                    for i in range(2):
                        inverse_deviation(pool, sem, "f", h * 2 + i, mv, rstd, neghalf, eps)
                    with pool.Fori(0, NIC) as ic:
                        n = h * NIC + ic
                        for p in range(6):
                            pool.wait_ge(sem("f_low"), n * 6 + p + 1)
                            if p < 4:
                                src = w_gu[bass.ds(ic, 1), p, :, :].rearrange("o p n -> p (o n)")
                            else:
                                src = w_down[bass.ds(ic, 1), p - 4, :, :].rearrange("o p n -> p (o n)")
                            pool.dma_start(raw[:, p % 2, :], src).then_inc(sem(f"f_loaded{p % 2}"), 16)

            def raw_ready(eng, n, p):
                eng.wait_ge(sem(f"f_loaded{p % 2}"), n * 48 + 16 * (p // 2) + 16)

            @block.scalar
            def _(act):
                act.sem_inc(sem("f_modulated"), 2)

                def modulate(n, i):
                    modulate_tile(act, sem, "f", n, turn_bank[i % 2], hT[:, i % 2, :], modcol[:, 3, :],
                                  modcol[:, 2, :])

                def round_gu(n, p):
                    raw_ready(act, n, p)
                    act.wait_ge(sem("gu_free"), n * 4 + p + 1)
                    act.activation(gu_h[:, p, :, :, :].rearrange("p a k q -> p (a k q)"), raw[:, p % 2, :], ACT.Copy)\
                       .then_inc(sem("gu_high"), 1)

                def group(n, g):
                    for j in range(4):
                        act.wait_ge(sem("gate_ready"), n * 4 + j + 1)
                        act.wait_ge(sem("hid_made"), n * 4 + j + 1)
                        act.activation(sg[:, j % 2, :], gate_bank[j % 2], ACT.Silu).then_inc(sem("gate_silu"), 1)
                        if j >= 1:
                            magnitude(n, j - 1)
                    magnitude(n, 3)

                def magnitude(n, j):
                    act.wait_ge(sem("hid_made"), n * 4 + j + 3)
                    act.activation(mag[:, j, :], hid[:, j, :], ACT.Abs).then_inc(sem("mag_made"), 1)

                def round_kept(n):
                    for j in range(4):
                        act.wait_ge(sem("kept"), n * 4 + j + 1)
                        act.wait_ge(sem("down_ready"), n * 4 + 4)
                        act.activation(hs_h[:, j, :], hid[:, j, :], ACT.Copy).then_inc(sem("hs_high"), 1)

                with act.Fori(0, 2) as h:
                    for i in range(8):
                        modulate(h * 8 + i, i)
                    for p in range(4):
                        round_gu(h * NIC, p)
                    with act.Fori(0, NIC - 1) as ic:
                        n = (h * NIC + ic) * 2
                        group(n, 0)
                        round_kept(n)
                        group(n + 1, 1)
                        for p in range(4):
                            round_gu(h * NIC + ic + 1, p)
                        round_kept(n + 1)
                    n = (h * NIC + NIC - 1) * 2
                    group(n, 0)
                    round_kept(n)
                    group(n + 1, 1)
                    round_kept(n + 1)

            @block.vector
            def _(dve):
                dve.sem_inc(sem("f_h_split"), 2)
                dve.sem_inc(sem("f_xn_ready"), 1)
                dve.sem_inc(sem("hid_made"), 2)

                def low_gu(n, p):
                    dve.wait_ge(sem("gu_high"), n * 4 + p + 1)
                    dve.tensor_tensor(gu_l[:, p, :, :, :].rearrange("p a k q -> p (a k q)"), raw[:, p % 2, :],
                                      gu_h[:, p, :, :, :].rearrange("p a k q -> p (a k q)"), ALU.subtract)\
                       .then_inc(sem("f_low"), 1)

                def split_down(n, p):
                    k = n * 2 + (p - 4)
                    raw_ready(dve, n, p)
                    dve.wait_ge(sem("f_low"), n * 6 + p + 2)
                    dst = slice((p - 4) * 2, (p - 4) * 2 + 2)
                    dve.tensor_tensor(dn_s[:, :, :], raw[:, p % 2, :].rearrange("p (a d) -> p a d", a=2),
                                      modrow[:, 5, :].unsqueeze(1).broadcast_to([P, 2, D]), ALU.mult)\
                       .then_inc(sem("dn_step"), 1)
                    dve.wait_ge(sem("dn_step"), k * 2 + 1)
                    dve.wait_ge(sem("down_ready"), n * 8 + 4)
                    dve.tensor_copy(dn_h[:, dst, :], dn_s[:, :, :]).then_inc(sem("dn_step"), 1)
                    dve.wait_ge(sem("dn_step"), k * 2 + 2)
                    dve.tensor_tensor(dn_l[:, dst, :], dn_s[:, :, :], dn_h[:, dst, :], ALU.subtract)\
                       .then_inc(sem("f_low"), 1)

                def hidden(n):
                    for j in range(4):
                        dve.wait_ge(sem("gate_silu"), n * 4 + j + 1)
                        dve.wait_ge(sem("up_ready"), n * 4 + j + 1)
                        dve.wait_ge(sem("hs_low"), n * 4 + 4)
                        dve.tensor_tensor(hid[:, j, :], sg[:, j % 2, :], up_bank[j % 2], ALU.mult)\
                           .then_inc(sem("hid_made"), 1)

                def compare(n):
                    m4 = mag[:, :, :].rearrange("p (a e) t -> p a e t", e=2)
                    dve.wait_ge(sem("mag_made"), n * 4 + 4)
                    dve.tensor_tensor(top[:, :, :], m4[:, :, 0, :], m4[:, :, 1, :], ALU.max)
                    dve.tensor_tensor(low[:, :, :], m4[:, :, 0, :], m4[:, :, 1, :], ALU.min)
                    dve.tensor_tensor(first[:, :, :], m4[:, :, 0, :], m4[:, :, 1, :], ALU.is_ge)\
                       .then_inc(sem("compared"), 1)
                    dve.wait_ge(sem("compared"), n * 3 + 1)
                    dve.tensor_tensor(both[:, 0, :], low[:, 0, :], top[:, 1, :], ALU.is_ge)
                    dve.tensor_tensor(both[:, 1, :], low[:, 1, :], top[:, 0, :], ALU.is_gt)\
                       .then_inc(sem("compared"), 1)
                    dve.wait_ge(sem("compared"), n * 3 + 2)
                    dve.tensor_tensor(lead[:, :], both[:, 0, :], both[:, 1, :], ALU.subtract)\
                       .then_inc(sem("compared"), 1)
                    dve.wait_ge(sem("compared"), n * 3 + 3)
                    dve.tensor_tensor(keep[:, 0, :], first[:, 0, :], lead[:, :], ALU.add)
                    dve.tensor_tensor(keep[:, 1, :], lead[:, :], first[:, 0, :], ALU.subtract)
                    dve.tensor_tensor(keep[:, 2, :], first[:, 1, :], lead[:, :], ALU.subtract)
                    dve.tensor_tensor(keep[:, 3, :], first[:, 1, :], lead[:, :], ALU.add)\
                       .then_inc(sem("keep_made"), 1)

                def select(n):
                    rule = ((1.0, ALU.is_ge), (0.0, ALU.is_ge), (1.0, ALU.is_ge), (0.0, ALU.is_le))
                    dve.wait_ge(sem("keep_made"), n + 1)
                    for j in range(4):
                        bound, op = rule[j]
                        dve.scalar_tensor_tensor(out=hid[:, j, :], in0=keep[:, j, :], scalar=bound, in1=hid[:, j, :],
                                                 op0=op, op1=ALU.mult).then_inc(sem("kept"), 1)

                def low_kept(n):
                    for j in range(4):
                        dve.wait_ge(sem("hs_high"), n * 4 + j + 1)
                        dve.tensor_tensor(hs_l[:, j, :], hid[:, j, :], hs_h[:, j, :], ALU.subtract)\
                           .then_inc(sem("hs_low"), 1)

                def add_down(n, g, tiles):
                    for t in tiles:
                        dve.wait_ge(sem("down_ready"), n * 4 + t + 1 + 4)
                        dve.tensor_tensor(acc[:, g * 4 + t, :], acc[:, g * 4 + t, :], down_bank[t % 2], ALU.add)\
                           .then_inc(sem("acc_done"), 2)

                def group(n, g, prev, extra=None):
                    hidden(n)
                    if extra:
                        extra()
                    compare(n)
                    if prev:
                        add_down(n - 1, 1 - g, (0, 1))
                    select(n)
                    if prev:
                        add_down(n - 1, 1 - g, (2, 3))
                    low_kept(n)

                dve.sem_inc(sem("hs_low"), 4)
                with dve.Fori(0, 2) as h:
                    dve.wait_ge(sem("acc_loaded"), h * 16 + 16)
                    for i in range(9):
                        if i % 4 == 0 and i < 8:
                            tile_statistics(dve, sem, "f", h * 2 + i // 4, acc[:, i:i + 4, :], stats, mv, idle)
                        if i < 8:
                            normalise_tile(dve, sem, "f", h * 8 + i, i % 4, h * 2 + i // 4, acc[:, i, :],
                                           xn[:, i % 2, :], mv, rstd)
                        if i >= 1:
                            k = i - 1
                            split_tile(dve, sem, "f", h * 8 + k, hT[:, k % 2, :], gT_h[:, :, k * P:(k + 1) * P],
                                       gT_l[:, :, k * P:(k + 1) * P])
                    for p in range(4):
                        low_gu(h * NIC, p)
                    n0 = h * (2 * NIC)
                    for p in (4, 5):
                        split_down(h * NIC, p)
                    group(n0, 0, False)
                    with dve.Fori(0, NIC - 1) as ic:
                        n = n0 + ic * 2
                        group(n + 1, 1, True, lambda: [low_gu(h * NIC + ic + 1, p) for p in range(4)])
                        hidden(n + 2)
                        compare(n + 2)
                        add_down(n + 1, 1, (0, 1))
                        select(n + 2)
                        add_down(n + 1, 1, (2, 3))
                        low_kept(n + 2)
                        for p in (4, 5):
                            split_down(h * NIC + ic + 1, p)
                    n = n0 + 2 * NIC - 1
                    group(n, 1, True)
                    add_down(n, 1, (0, 1, 2, 3))

            @block.tensor
            def _(pe):
                pe.sem_inc(sem("f_xn_turned"), 2)
                pe.sem_inc(sem("gu_free"), 4)
                pe.sem_inc(sem("down_ready"), 4)

                def gate_up(n, chunk, g, release):
                    cols = slice(g * TB, (g + 1) * TB)
                    for j in range(4):
                        if g == 0:
                            pe.wait_ge(sem("gu_high"), chunk * 4 + j + 1)
                            pe.wait_ge(sem("f_low"), chunk * 6 + j + 1 + 2)
                        pe.wait_ge(sem("hid_made"), n * 4 + j + 1)
                        for a, bank in ((0, gate_bank[j % 2]), (1, up_bank[j % 2])):
                            last = three_pass(pe, bank, [(gu_h[:, j, a, kt, :], gu_l[:, j, a, kt, :],
                                                          gT_h[:, kt, cols], gT_l[:, kt, cols]) for kt in range(KT)])
                            last.then_inc(sem(("gate_ready", "up_ready")[a]), 1)

                def down(n, chunk, g, prev):
                    pe.wait_ge(sem("hs_low"), n * 4 + 4 + 4)
                    if g == 0:
                        pe.wait_ge(sem("f_low"), chunk * 6 + 6 + 2)
                    for t in range(4):
                        if t >= 2:
                            pe.wait_ge(sem("acc_done"), n * 8 + 2 * (t - 1))
                        elif prev:
                            pe.wait_ge(sem("acc_done"), n * 8 - 2 * (1 - t))
                        three_pass(pe, down_bank[t % 2],
                                   [(hs_h[:, j, t * P:(t + 1) * P], hs_l[:, j, t * P:(t + 1) * P],
                                     dn_h[:, j, :], dn_l[:, j, :]) for j in range(4)])\
                            .then_inc(sem("down_ready"), 1)

                def release():
                    pe.sem_inc(sem("gu_free"), 4)

                with pe.Fori(0, 2) as h:
                    for i in range(8):
                        turn_tile(pe, sem, "f", h * 8 + i, xn[:, i % 2, :], turn_bank[i % 2], ident)
                    n0 = h * (2 * NIC)
                    pe.wait_ge(sem("f_h_split"), h * 8 + 8 + 2)
                    gate_up(n0, h * NIC, 0, False)
                    with pe.Fori(0, NIC - 1) as ic:
                        n = n0 + ic * 2
                        chunk = h * NIC + ic
                        gate_up(n + 1, chunk, 1, True)
                        pe.wait_ge(sem("hid_made"), (n + 1) * 4 + 4 + 2)
                        release()
                        down(n, chunk, 0, False)
                        gate_up(n + 2, chunk + 1, 0, False)
                        down(n + 1, chunk, 1, True)
                    n = n0 + 2 * NIC - 2
                    gate_up(n + 1, h * NIC + NIC - 1, 1, True)
                    pe.wait_ge(sem("hid_made"), (n + 1) * 4 + 4 + 2)
                    release()
                    down(n, h * NIC + NIC - 1, 0, False)
                    down(n + 1, h * NIC + NIC - 1, 1, True)


def kernel(L0_attn_u, L0_attn_in_proj_w, L0_attn_conv_w, L0_attn_conv_b, L0_attn_dt_bias, L0_attn_A_log,
           L0_attn_D_skip, L0_attn_norm_w, L0_attn_out_proj_w, L0_ffn_w_gate, L0_ffn_w_up, L0_ffn_w_down,
           L0_c, L0_wmod):
    import numpy as np
    import concourse.bacc as bacc
    from concourse.bass_utils import run_bass_kernel_spmd

    def own(a):
        return np.ascontiguousarray(a)

    def wide(a):
        return own(np.broadcast_to(np.asarray(a)[None, :], (P, np.asarray(a).shape[0])))

    u = np.asarray(L0_attn_u)
    gu = np.stack([np.asarray(w).reshape(KT, P, NIC, P, 4).transpose(2, 4, 1, 0, 3)
                   for w in (L0_ffn_w_gate, L0_ffn_w_up)], axis=3)
    down = np.asarray(L0_ffn_w_down).reshape(NIC, P, 2, 2, D).transpose(0, 2, 1, 3, 4)
    arrays = {
        "x": own(u.reshape(NCH, P, D)),
        "w_in": own(np.asarray(L0_attn_in_proj_w).T.reshape(KT, P, DIN).transpose(1, 0, 2)),
        "w_out": own(np.asarray(L0_attn_out_proj_w).T.reshape(CT, P, D)),
        "conv_w": own(np.asarray(L0_attn_conv_w).reshape(NXBC, P, TAPS).transpose(1, 0, 2)),
        "conv_b": own(np.asarray(L0_attn_conv_b).reshape(NXBC, P).T),
        "dt_bias": wide(L0_attn_dt_bias),
        "a_log": wide(L0_attn_A_log),
        "d_skip": own(np.broadcast_to(np.asarray(L0_attn_D_skip).reshape(CT, 2).T[:, None, :], (2, HD, CT))),
        "norm_w": own(np.asarray(L0_attn_norm_w).reshape(CT, P).T),
        "w_gu": own(gu.reshape(NIC, 4, P, 2 * KT * P)),
        "w_down": own(down.reshape(NIC, 2, P, 2 * D)),
        "c": own(np.asarray(L0_c).reshape(KT, P).T),
        "w_mod": own(np.asarray(L0_wmod).reshape(KT, P, 6 * D).transpose(1, 0, 2)),
    }
    nc = bacc.Bacc("TRN2", target_bir_lowering=False, num_devices=1)
    args = [nc.dram_tensor(n, a.shape, mybir.dt.from_np(a.dtype), kind="ExternalInput").ap()
            for n, a in arrays.items()]
    out = nc.dram_tensor("out", (NCH, P, D), F32, kind="ExternalOutput").ap()
    build(nc, *args, out)
    r = run_bass_kernel_spmd(nc, [arrays], core_ids=[0])
    return np.asarray(r.results[0]["out"]).reshape(1, L, D)
```

```python
from contextlib import ExitStack

import concourse.bass as bass
from concourse import mybir

F32 = mybir.dt.float32
F32R = mybir.dt.float32r
BF16 = mybir.dt.bfloat16
ALU = mybir.AluOpType
ACT = mybir.ActivationFunctionType
AX = mybir.AxisListType

P = 128
L = 2048
D = 512
DI = 1024
NS = 128
NH = 16
HD = DI // NH
KT = D // P
CT = DI // P
NXBC = CT + 2
DIN = 2 * DI + 2 * NS + NH
TB = 512
NB = L // TB
TT = TB // P
NCH = L // P
EPS = 1e-5
FI = 2048
NIC = FI // 512
TAPS = 4

WP = DIN // 8
NWP = DIN // WP
NJ = 1 + NXBC + CT
NST = NXBC + CT


def column_of(j):
    if j == 0:
        return DIN - P
    return DI + P * (j - 1) if j <= NXBC else P * (j - 1 - NXBC)


def broadcast(ap, shape):
    return ap.broadcast_to(shape)


def three_pass(pe, out, pairs):
    n = len(pairs)
    for i, (lh, ll, rh, rl) in enumerate(pairs):
        pe.matmul(out, lh, rh, start=(i == 0), stop=False)
        pe.matmul(out, lh, rl, start=False, stop=False)
        last = pe.matmul(out, ll, rh, start=False, stop=(i == n - 1))
    return last


def build(nc, x, w_in, w_out, conv_w, conv_b, dt_bias, a_log, d_skip, norm_w, w_gu, w_down, c, w_mod, out):
    with ExitStack() as ctx:
        sems = {}

        def sem(name):
            if name not in sems:
                sems[name] = ctx.enter_context(nc.semaphore(name))
            return sems[name]

        def sb(name, shape, dt=F32, stack=ctx):
            return stack.enter_context(nc.sbuf_tensor(name, shape, dt))

        xz_dram = nc.dram_tensor("xz_scratch", [NCH, P, NST, P], F32).ap()
        x1_dram = nc.dram_tensor("x1_scratch", [NCH, P, D], F32).ap()
        gT_dram = nc.dram_tensor("gT_scratch", [2, NCH, P, D], F32).ap()

        ident = sb("ident", [P, P])
        upto = sb("upto", [P, P])
        after = sb("after", [P, P])
        after_r = sb("after_r", [P, P], F32R)
        ones = sb("ones", [P, P])
        eps = sb("eps", [P, TT])
        neghalf = sb("neghalf", [P, TT])
        modrow = sb("modrow", [P, 6, D])
        modcol = sb("modcol", [P, 4, KT])
        dt_raw = sb("dt_raw", [P, NCH, NH])
        ps = ctx.enter_context(nc.psum_tensor("ps", [P, 8, 512], F32))

        project_stage(nc, sem, sb, ps, x, w_in, conv_w, conv_b, dt_bias, c, w_mod, xz_dram,
                      ident, upto, after, after_r, ones, neghalf, eps, modrow, modcol, dt_raw)
        scan_stage(nc, sem, sb, ps, x, w_out, a_log, d_skip, norm_w, xz_dram, x1_dram, gT_dram,
                   ident, upto, after, after_r, ones, neghalf, eps, modrow, modcol, dt_raw)
        ffn_stage(nc, sem, sb, ps, w_gu, w_down, x1_dram, gT_dram, out, modrow)


def tile_statistics(dve, sem, tag, blk, x_tiles, stats, mv, idle):
    step = sem(f"{tag}_ln_step")
    for i in range(TT):
        ins = dve.bn_stats(stats[:, i, :], x_tiles[:, i, :])
    ins.then_inc(step, 1)
    dve.wait_ge(step, blk * 2 + 1)
    dve.wait_ge(sem(f"{tag}_xn_ready"), blk * TT + 1)
    dve.memset(idle[:, :], 0.0)
    for i in range(TT):
        ins = dve.bn_aggr(mv[:, i, :], stats[:, i, :])
    ins.then_inc(step, 1)


def inverse_deviation(pool, sem, tag, blk, mv, rstd, neghalf, eps):
    pool.wait_ge(sem(f"{tag}_ln_step"), blk * 2 + 2)
    pool.wait_ge(sem(f"{tag}_xn_ready"), blk * TT + 1)
    pool.tensor_tensor(rstd[:, :], mv[:, :, 1], eps[:, :], ALU.add).then_inc(sem(f"{tag}_rstd"), 1)
    pool.wait_ge(sem(f"{tag}_rstd"), blk * 2 + 1)
    pool.tensor_tensor(rstd[:, :], rstd[:, :], neghalf[:, :], ALU.pow).then_inc(sem(f"{tag}_rstd"), 1)


def normalise_tile(dve, sem, tag, n, i, blk, x_tile, xn, mv, rstd):
    dve.wait_ge(sem(f"{tag}_rstd"), blk * 2 + 2)
    dve.wait_ge(sem(f"{tag}_xn_turned"), n + 1)
    dve.tensor_scalar(xn, x_tile, mv[:, i, 0:1], rstd[:, i:i + 1], ALU.subtract, ALU.mult)\
       .then_inc(sem(f"{tag}_xn_ready"), 1)


def turn_tile(pe, sem, tag, n, xn, bank, ident):
    pe.wait_ge(sem(f"{tag}_xn_ready"), n + 2)
    pe.wait_ge(sem(f"{tag}_modulated"), n + 1)
    for kt in range(KT):
        last = pe.transpose(bank[:, kt * P:(kt + 1) * P], xn[:, kt * P:(kt + 1) * P], ident[:, :])
    last.then_inc(sem(f"{tag}_xn_turned"), 1)


def modulate_tile(act, sem, tag, n, bank, full, scale, shift):
    act.wait_ge(sem(f"{tag}_xn_turned"), n + 3)
    act.wait_ge(sem(f"{tag}_h_split"), n + 1)
    for kt in range(KT):
        last = act.activation(full[:, kt * P:(kt + 1) * P], bank[:, kt * P:(kt + 1) * P], ACT.Identity,
                              bias=shift[:, kt:kt + 1], scale=scale[:, kt:kt + 1])
    last.then_inc(sem(f"{tag}_modulated"), 1)


def split_tile(dve, sem, tag, n, full, high, low):
    view = full.rearrange("p (k t) -> p k t", k=KT)
    dve.wait_ge(sem(f"{tag}_modulated"), n + 3)
    dve.tensor_copy(high, view).then_inc(sem(f"{tag}_h_high"), 1)
    dve.wait_ge(sem(f"{tag}_h_high"), n + 1)
    dve.tensor_tensor(low, view, high, ALU.subtract).then_inc(sem(f"{tag}_h_split"), 1)


def project_stage(nc, sem, sb0, ps, x, w_in, conv_w, conv_b, dt_bias, c, w_mod, xz_dram,
                  ident, upto, after, after_r, ones, neghalf, eps, modrow, modcol, dt_raw):
    with ExitStack() as st:
        def sb(name, shape, dt=F32):
            return sb0(name, shape, dt, st)

        win_h = sb("win_h", [P, KT, DIN], F32R)
        win_l = sb("win_l", [P, KT, DIN], F32R)
        raw = sb("win_raw", [P, 2, KT, WP])
        hT_h = sb("hT_h", [P, 2, KT, TB], F32R)
        hT_l = sb("hT_l", [P, 2, KT, TB], F32R)
        xblk = sb("xblk", [P, TT, D])
        xn = sb("xn", [P, 2, D])
        hT = sb("hT", [P, 2, D])
        xraw = sb("xraw", [P, NXBC, TAPS - 1 + TB])
        conv = sb("conv", [P, 2, TB])
        stage = sb("stage", [P, 6, TB])
        wm = sb("wm", [P, 2, KT, D])
        dtT = sb("dtT", [P, TB])
        cw = sb("cw", [P, NXBC, TAPS])
        cb = sb("cb", [P, NXBC])
        dtb = sb("dtb", [P, NH])
        ccol = sb("ccol", [P, KT])
        csilu = sb("csilu", [P, KT])
        cwide = sb("cwide", [P, KT, P])
        idle = sb("idle", [P, 1])
        stats = sb("stats", [P, TT, 6])
        mv = sb("mv", [P, TT, 2])
        rstd = sb("rstd", [P, TT])

        turn_bank = [ps[:, 0, :], ps[:, 1, :]]
        acc_bank = [ps[:, 2 + q, :] for q in range(4)]
        dt_bank = ps[:, 6, :]
        mod_bank = ps[:, 7, :]
        stored = [sem(f"stored{k}") for k in range(6)]

        made = []
        for j in range(NJ):
            if j > NXBC:
                made.append((True, j - 1 - NXBC))
            if 3 <= j < 3 + NXBC:
                made.append((False, j - 3))

        def slot_of(item):
            return made.index(item) % 6

        def turn_of(item):
            return made.index(item) // 6

        with nc.Block() as block:
            @block.sync
            def _(sp):
                for t in stored:
                    sp.sem_inc(t, 16)
                sp.dma_start(ccol[:, :], c).then_inc(sem("c_loaded"), 16)
                for r in range(2):
                    sp.dma_start(wm[:, r, :, :], w_mod[:, :, r * D:(r + 1) * D]).then_inc(sem(f"wm_loaded{r}"), 16)
                for dst, src in ((cw[:, :, :], conv_w), (cb[:, :], conv_b), (dtb[:, :], dt_bias)):
                    sp.dma_start(dst, src).then_inc(sem("params_loaded"), 16)
                for i in range(NWP):
                    if i >= 2:
                        sp.wait_ge(sem("win_low"), i - 1)
                    sp.dma_start(raw[:, i % 2, :, :], w_in[:, :, i * WP:(i + 1) * WP])\
                      .then_inc(sem(f"win_loaded{i % 2}"), 16)
                for r in range(2, 4):
                    sp.wait_ge(sem("mod_product"), r - 1)
                    sp.dma_start(wm[:, r % 2, :, :], w_mod[:, :, r * D:(r + 1) * D])\
                      .then_inc(sem(f"wm_loaded{r % 2}"), 16)
                with sp.Fori(0, NB) as b:
                    for item in made:
                        is_z, t = item
                        k = slot_of(item)
                        if is_z:
                            sp.wait_ge(sem("evacuated"), b * NJ + (1 + NXBC + t) + 1 + 3)
                        else:
                            sp.wait_ge(sem("conv_staged"), b * NXBC + t + 1 + 2)
                        tile_at = NXBC + t if is_z else t
                        sp.dma_start(
                            xz_dram[bass.ds(b * TT, TT), :, tile_at, :].rearrange("c p t -> p c t"),
                            stage[:, k, :].rearrange("p (c t) -> p c t", c=TT)).then_inc(stored[k], 16)
                for r in range(4, 6):
                    sp.wait_ge(sem("mod_product"), r - 1)
                    sp.dma_start(wm[:, r % 2, :, :], w_mod[:, :, r * D:(r + 1) * D])\
                      .then_inc(sem(f"wm_loaded{r % 2}"), 16)
                for t in stored:
                    sp.wait_ge(t, 16 + 16 * (NST // 6) * NB)

            @block.gpsimd
            def _(pool):
                pool.memset(ones[:, :], 1.0).then_inc(sem("const_made"), 1)
                pool.memset(neghalf[:, :], -0.5)
                pool.memset(eps[:, :], EPS)
                pool.memset(ident[:, :], 0.0).then_inc(sem("const_made"), 1)
                pool.wait_ge(sem("const_made"), 2)
                pool.affine_select(out=ident[:, :], in_=ident[:, :], compare_op=ALU.not_equal, fill=1.0, base=0,
                                   pattern=[[-1, P]], channel_multiplier=1).then_inc(sem("const_made"), 1)
                pool.affine_select(out=upto[:, :], in_=ones[:, :], compare_op=ALU.is_ge, fill=0.0, base=0,
                                   pattern=[[1, P]], channel_multiplier=-1).then_inc(sem("const_made"), 1)
                pool.affine_select(out=after[:, :], in_=ones[:, :], compare_op=ALU.is_gt, fill=0.0, base=0,
                                   pattern=[[-1, P]], channel_multiplier=1).then_inc(sem("const_made"), 1)
                with pool.Fori(0, NB) as b:
                    pool.wait_ge(sem("p_xn_ready"), b * TT + 1)
                    pool.dma_start(xblk[:, :, :],
                                   x[bass.ds(b * TT, TT), :, :].rearrange("t p d -> p t d"))\
                        .then_inc(sem("x_loaded"), 16)
                    inverse_deviation(pool, sem, "p", b, mv, rstd, neghalf, eps)

            @block.vector
            def _(dve):
                dve.sem_inc(sem("p_h_split"), 2)
                dve.sem_inc(sem("p_xn_ready"), 1)
                dve.memset(xraw[:, :, 0:TAPS - 1], 0.0).then_inc(sem("tail_kept"), 1)
                dve.wait_ge(sem("c_silu"), 1)
                dve.tensor_copy(cwide[:, :, :], csilu[:, :].unsqueeze(2).broadcast_to([P, KT, P]))\
                   .then_inc(sem("c_wide"), 1)
                dve.wait_ge(sem("const_made"), 5)
                dve.tensor_copy(after_r[:, :], after[:, :]).then_inc(sem("after_rounded"), 1)

                def keep_columns(n, row):
                    dve.wait_ge(sem("mod_turned"), n + 1)
                    src = dt_bank.rearrange("p (k t) -> p k t", k=KT)[:, :, 0]
                    dve.tensor_scalar(modcol[:, n, :], src, 1.0 if row in (1, 4) else 0.0, None, ALU.add)\
                       .then_inc(sem("mod_column"), 1)

                def normalise(b, i):
                    n = b * TT + i
                    normalise_tile(dve, sem, "p", n, i, b, xblk[:, i, :], xn[:, i % 2, :], mv, rstd)

                def statistics(b):
                    dve.wait_ge(sem("x_loaded"), b * 16 + 16)
                    tile_statistics(dve, sem, "p", b, xblk, stats, mv, idle)

                def split(b, i, slot):
                    split_tile(dve, sem, "p", b * TT + i, hT[:, i % 2, :],
                               hT_h[:, slot, :, i * P:(i + 1) * P] if isinstance(slot, int) else
                               hT_h[:, bass.ds(slot, 1), :, i * P:(i + 1) * P].rearrange("p o k t -> p (o k) t"),
                               hT_l[:, slot, :, i * P:(i + 1) * P] if isinstance(slot, int) else
                               hT_l[:, bass.ds(slot, 1), :, i * P:(i + 1) * P].rearrange("p o k t -> p (o k) t"))

                def convolve(b, t):
                    m = b * NXBC + t
                    u = conv[:, t % 2, :]
                    dve.wait_ge(sem("evacuated"), b * NJ + t + 2 + 3)
                    dve.wait_ge(sem("tail_kept"), b + 1)
                    dve.wait_ge(sem("conv_staged"), m + 1)
                    dve.tensor_scalar(u, xraw[:, t, TAPS - 1:TAPS - 1 + TB], cw[:, t, TAPS - 1:TAPS], cb[:, t:t + 1],
                                      ALU.mult, ALU.add).then_inc(sem("conv_step"), 1)
                    for k in range(TAPS - 1):
                        dve.wait_ge(sem("conv_step"), m * TAPS + k + 1)
                        dve.scalar_tensor_tensor(out=u, in0=xraw[:, t, k:k + TB], scalar=cw[:, t, k:k + 1], in1=u,
                                                 op0=ALU.mult, op1=ALU.add).then_inc(sem("conv_step"), 1)

                def keep_tail(b):
                    dve.wait_ge(sem("conv_step"), (b * NXBC + NXBC) * TAPS)
                    dve.tensor_copy(xraw[:, :, 0:TAPS - 1], xraw[:, :, TB:TB + TAPS - 1])\
                       .then_inc(sem("tail_kept"), 1)

                def add_dt_bias(b):
                    dve.wait_ge(sem("dt_turned"), b + 2)
                    dve.tensor_tensor(dt_raw[:, bass.ds(b * TT, TT), :] if not isinstance(b, int) else
                                      dt_raw[:, b * TT:(b + 1) * TT, :],
                                      dt_bank.rearrange("p (t c) -> p t c", t=TT)[:, :, P - NH:P],
                                      dtb[:, :].unsqueeze(1).broadcast_to([P, TT, NH]), ALU.add)\
                       .then_inc(sem("dt_kept"), 1)

                def split_weights(i):
                    dve.wait_ge(sem("win_high"), i + 1)
                    cols = slice(i * WP, (i + 1) * WP)
                    dve.tensor_tensor(win_l[:, :, cols], raw[:, i % 2, :, :], win_h[:, :, cols], ALU.subtract)\
                       .then_inc(sem("win_low"), 1)

                def block_body(b, has_next, slot):
                    for t in range(NXBC):
                        if has_next and t == 0:
                            statistics(b + 1)
                        if has_next and t in (1, 3, 6, 8):
                            normalise(b + 1, (1, 3, 6, 8).index(t))
                        convolve(b, t)
                        if t == 2:
                            add_dt_bias(b)
                        if has_next and t in (5, 8, 9):
                            split(b + 1, (5, 8, 9).index(t), slot)
                    keep_tail(b)
                    if has_next:
                        split(b + 1, 3, slot)

                statistics(0)
                normalise(0, 0)
                normalise(0, 1)
                keep_columns(0, 0)
                keep_columns(1, 1)
                for i in range(TT):
                    split(0, i, 0)
                    if i + 2 < TT:
                        normalise(0, i + 2)
                    split_weights(i)
                for i in range(TT, NWP):
                    split_weights(i)
                dve.wait_ge(sem("params_loaded"), 48)
                with dve.Fori(0, NB - 1) as b:
                    block_body(b, True, (b + 1) % 2)
                block_body(NB - 1, False, None)
                keep_columns(2, 3)
                keep_columns(3, 4)

            @block.scalar
            def _(act):
                act.sem_inc(sem("p_modulated"), 2)
                act.sem_inc(sem("evacuated"), 3)
                act.sem_inc(sem("conv_staged"), 2)
                act.wait_ge(sem("c_loaded"), 16)
                act.activation(csilu[:, :], ccol[:, :], ACT.Silu).then_inc(sem("c_silu"), 1)

                def keep_row(r):
                    act.wait_ge(sem("mod_product"), r + 1)
                    act.activation(modrow[:, r, :], mod_bank, ACT.Copy).then_inc(sem("mod_row"), 1)

                def round_weights(i):
                    act.wait_ge(sem(f"win_loaded{i % 2}"), 16 * (i // 2) + 16)
                    act.activation(win_h[:, :, i * WP:(i + 1) * WP], raw[:, i % 2, :, :], ACT.Copy)\
                       .then_inc(sem("win_high"), 1)

                def modulate(b, i):
                    modulate_tile(act, sem, "p", b * TT + i, turn_bank[i % 2], hT[:, i % 2, :],
                                  modcol[:, 1, :], modcol[:, 0, :])

                def evacuate(b, j):
                    act.wait_ge(sem("product_ready"), b * NJ + j + 1)
                    if j == 0:
                        act.wait_ge(sem("dt_turned"), b + 1)
                        act.activation(dtT[:, :], acc_bank[0], ACT.Copy).then_inc(sem("evacuated"), 1)
                    elif j <= NXBC:
                        act.wait_ge(sem("tail_kept"), b + 1)
                        act.activation(xraw[:, j - 1, TAPS - 1:TAPS - 1 + TB], acc_bank[j % 4], ACT.Copy)\
                           .then_inc(sem("evacuated"), 1)
                    else:
                        item = (True, j - 1 - NXBC)
                        act.wait_ge(stored[slot_of(item)], b * 48 + 16 * turn_of(item) + 16)
                        act.activation(stage[:, slot_of(item), :], acc_bank[j % 4], ACT.Silu)\
                           .then_inc(sem("evacuated"), 1)

                def activate(b, t):
                    item = (False, t)
                    act.wait_ge(sem("conv_step"), (b * NXBC + t + 1) * TAPS)
                    act.wait_ge(stored[slot_of(item)], b * 48 + 16 * turn_of(item) + 16)
                    act.activation(stage[:, slot_of(item), :], conv[:, t % 2, :], ACT.Silu)\
                       .then_inc(sem("conv_staged"), 1)

                def block_body(b, has_next):
                    for j in range(NJ):
                        evacuate(b, j)
                        if 3 <= j < 3 + NXBC:
                            activate(b, j - 3)
                        if has_next and j in (4, 7, 10, 13):
                            modulate(b + 1, (j - 4) // 3)

                keep_row(0)
                keep_row(1)
                act.wait_ge(sem("mod_column"), 2)
                for i in range(TT):
                    modulate(0, i)
                    round_weights(i)
                for i in range(TT, NWP):
                    round_weights(i)
                with act.Fori(0, NB - 1) as b:
                    block_body(b, True)
                block_body(NB - 1, False)
                for r in range(2, 6):
                    keep_row(r)

            @block.tensor
            def _(pe):
                pe.sem_inc(sem("p_xn_turned"), 2)
                pe.sem_inc(sem("dt_turned"), 1)

                def mod_row(r):
                    if r >= 1:
                        pe.wait_ge(sem("mod_row"), r)
                    pe.wait_ge(sem(f"wm_loaded{r % 2}"), 16 * (r // 2) + 16)
                    for kt in range(KT):
                        last = pe.matmul(mod_bank, cwide[:, kt, :], wm[:, r % 2, kt, :], start=(kt == 0),
                                         stop=(kt == KT - 1))
                    last.then_inc(sem("mod_product"), 1)

                def turn_row(n, row):
                    pe.wait_ge(sem("mod_row"), row + 1)
                    if n >= 1:
                        pe.wait_ge(sem("mod_column"), n)
                    for kt in range(KT):
                        last = pe.transpose(dt_bank[:, kt * P:(kt + 1) * P], modrow[:, row, kt * P:(kt + 1) * P],
                                            ident[:, :])
                    last.then_inc(sem("mod_turned"), 1)

                def turn(b, i):
                    turn_tile(pe, sem, "p", b * TT + i, xn[:, i % 2, :], turn_bank[i % 2], ident)

                def project(b, j, slot, first):
                    n = b * NJ + j
                    c0 = column_of(j)
                    pe.wait_ge(sem("evacuated"), n + 1)
                    if first:
                        pe.wait_ge(sem("win_low"), (c0 + P - 1) // WP + 1)
                    if j == 0:
                        pe.wait_ge(sem("p_h_split"), b * TT + TT + 2)
                    rhs = []
                    for kt in range(KT):
                        if isinstance(slot, int):
                            rhs.append((hT_h[:, slot, kt, :], hT_l[:, slot, kt, :]))
                        else:
                            rhs.append(tuple(h[:, bass.ds(slot, 1), kt, :].rearrange("p o t -> p (o t)")
                                             for h in (hT_h, hT_l)))
                    three_pass(pe, acc_bank[j % 4],
                               [(win_h[:, kt, c0:c0 + P], win_l[:, kt, c0:c0 + P], *rhs[kt]) for kt in range(KT)])\
                        .then_inc(sem("product_ready"), 1)

                def turn_dt(b):
                    pe.wait_ge(sem("evacuated"), b * NJ + 1 + 3)
                    if isinstance(b, int) and b == 0:
                        pe.wait_ge(sem("mod_column"), 2)
                    else:
                        pe.wait_ge(sem("dt_kept"), b)
                    for i in range(TT):
                        last = pe.transpose(dt_bank[:, i * P:(i + 1) * P], dtT[:, i * P:(i + 1) * P], ident[:, :])
                    last.then_inc(sem("dt_turned"), 1)

                def block_body(b, has_next, slot, first=False):
                    for j in range(NJ):
                        project(b, j, slot, first)
                        if j == 2:
                            turn_dt(b)
                        if has_next and j in (3, 6, 9, 12):
                            turn(b + 1, (j - 3) // 3)

                pe.wait_ge(sem("c_wide"), 1)
                mod_row(0)
                pe.wait_ge(sem("const_made"), 5)
                turn_row(0, 0)
                mod_row(1)
                turn_row(1, 1)
                for i in range(TT):
                    turn(0, i)
                block_body(0, True, 0, first=True)
                with pe.Fori(1, NB - 1) as b:
                    block_body(b, True, b % 2)
                block_body(NB - 1, False, (NB - 1) % 2)
                for r in range(2, 6):
                    mod_row(r)
                    if r in (3, 4):
                        if r == 3:
                            pe.wait_ge(sem("dt_kept"), NB)
                        turn_row(r - 1, r)


def scan_stage(nc, sem, sb0, ps, x, w_out, a_log, d_skip, norm_w, xz_dram, x1_dram, gT_dram,
               ident, upto, after, after_r, ones, neghalf, eps, modrow, modcol, dt_raw):
    with ExitStack() as st:
        def sb(name, shape, dt=F32):
            return sb0(name, shape, dt, st)

        NC = NCH * NH
        wo_h = sb("wo_h", [P, CT, D], F32R)
        wo_l = sb("wo_l", [P, CT, D], F32R)
        wo_raw = sb("wo_raw", [P, 2, D])
        nw = sb("nw", [P, CT])
        dskip = sb("dskip", [P, CT])
        alog = sb("alog", [P, NH])
        arow = sb("arow", [P, NH])
        small = sb("small", [P, 8, NC])
        dt = sb("dt", [P, NCH, NH])
        dA = sb("dA", [P, NCH, NH])
        dA_h = sb("dA_h", [P, NCH, NH], F32R)
        dA_l = sb("dA_l", [P, NCH, NH], F32R)
        grown = sb("grown", [P, NCH, NH])
        left = sb("left", [P, NCH, NH])
        whole = sb("whole", [P, NCH, NH])
        dt_left = sb("dt_left", [P, NCH, NH])
        ga = sb("ga", [P, D])
        ga_t = sb("ga_t", [P, D])
        ga_s = sb("ga_s", [P, 2, D])
        xz = sb("xz", [P, 2, NST, P])
        xres = sb("xres", [P, 2, D])
        step_h = sb("step_h", [P, NH, P], F32R)
        step_l = sb("step_l", [P, NH, P], F32R)
        M = sb("M", [P, 2, NH, P])
        cbm = sb("cbm", [P, P])
        btok = sb("btok", [P, P])
        xdt = sb("xdt", [P, 2, DI])
        xdl = sb("xdl", [P, DI])
        state = sb("state", [P, DI])
        faded = sb("faded", [P, DI])
        yoff = sb("yoff", [P, DI])
        dx = sb("dx", [P, CT, P])
        y1 = sb("y1", [P, CT, P])
        y = sb("y", [P, CT, P])
        y_h = sb("y_h", [P, CT, P], F32R)
        y_l = sb("y_l", [P, CT, P], F32R)
        ysq = sb("ysq", [P, CT, P])
        ysum = sb("ysum", [P, P])
        rms = sb("rms", [P, 1])
        x1 = sb("x1", [P, 2, D])
        idle = sb("idle_s", [P, 1])
        stats = sb("stats_s", [P, 6])
        mv = sb("mv_s", [P, 2, 2])
        rstd = sb("rstd_s", [P, 2])
        xn = sb("xn_s", [P, 2, D])
        g = sb("g", [P, 2, D])
        g_h = sb("g_h", [P, 2, D], F32R)
        g_l = sb("g_l", [P, 2, D], F32R)

        seg_bank = [ps[:, 0, :], ps[:, 1, :]]
        pair = ps[:, 2:4, :]
        pair_flat = pair.rearrange("p a b -> p (a b)")
        y_pair = ps[:, 4:6, :]
        y_flat = y_pair.rearrange("p a b -> p (a b)")
        out_bank = ps[:, 6, :]
        cb_ps = ps[:, 7, 0:P]
        bt_ps = ps[:, 7, P:2 * P]
        ss_ps = ps[:, 7, 2 * P:2 * P + 1]
        x_view = x.rearrange("t p d -> t p d")

        with nc.Block() as block:
            def load_xbc(eng, c, r):
                eng.dma_start(xz[:, r, 0:NXBC, :], one(xz_dram, c, 0, NXBC)).then_inc(sem(f"xbc_loaded{r}"), 16)

            def load_z(eng, c, r):
                eng.dma_start(xz[:, r, NXBC:NST, :], one(xz_dram, c, NXBC, NST)).then_inc(sem(f"z_loaded{r}"), 16)

            def load_x(eng, c, r):
                eng.dma_start(xres[:, r, :], one(x_view, c)).then_inc(sem(f"xres_loaded{r}"), 16)

            def turn(c, r):
                return c // 2 if isinstance(c, int) else (c - r) // 2

            def one(ap, c, lo=0, hi=None):
                if isinstance(c, int):
                    return ap[c] if hi is None else ap[c, :, lo:hi, :]
                if hi is not None:
                    return ap[bass.ds(c, 1), :, lo:hi, :].rearrange("o p a b -> p (o a) b")
                return ap[bass.ds(c, 1), :, :].rearrange("o p a -> p (o a)")

            def chunk_cols(ap, c):
                if isinstance(c, int):
                    return ap[:, c, :]
                return ap[:, bass.ds(c, 1), :].rearrange("p o h -> p (o h)")

            def by_head(ap, width):
                return ap.unsqueeze(2).broadcast_to([P, NH, width])

            def over_chunks(eng, body):
                body(0, 0, False, False, True)
                body(1, 1, True, False, True)
                with eng.Fori(0, NCH // 2 - 2) as i:
                    body(i * 2 + 2, 0, True, True, True)
                    body(i * 2 + 3, 1, True, True, True)
                body(NCH - 2, 0, True, True, True)
                body(NCH - 1, 1, True, True, False)

            @block.sync
            def _(sp):
                sp.sem_inc(sem("x1_stored0"), 16)
                sp.sem_inc(sem("x1_stored1"), 16)
                sp.sem_inc(sem("g_stored0"), 32)
                sp.sem_inc(sem("g_stored1"), 32)
                sp.dma_start(alog[:, :], a_log).then_inc(sem("scan_params"), 16)
                sp.dma_start(nw[:, :], norm_w).then_inc(sem("scan_params"), 16)
                for half in range(2):
                    sp.dma_start(dskip[half * HD:(half + 1) * HD, :], d_skip[half]).then_inc(sem("scan_params"), 16)
                for c_ in range(2):
                    load_xbc(sp, c_, c_)
                    load_z(sp, c_, c_)
                    load_x(sp, c_, c_)
                for t in range(CT):
                    if t >= 2:
                        sp.wait_ge(sem("wo_scaled"), t - 1)
                    sp.dma_start(wo_raw[:, t % 2, :], w_out[t]).then_inc(sem(f"wo_loaded{t % 2}"), 16)

                def store_g(c, r):
                    sp.wait_ge(sem("g_low"), c + 1)
                    sp.dma_start(one(gT_dram[0], c), g_h[:, r, :].bitcast(F32)).then_inc(sem(f"g_stored{r}"), 16)
                    sp.dma_start(one(gT_dram[1], c), g_l[:, r, :].bitcast(F32)).then_inc(sem(f"g_stored{r}"), 16)

                def store_x1(c, r):
                    sp.wait_ge(sem("x1_made"), c + 1)
                    sp.dma_start(one(x1_dram, c), x1[:, r, :]).then_inc(sem(f"x1_stored{r}"), 16)

                def body(c, r, prev, prev2, nxt, second=True):
                    if second:
                        sp.wait_ge(sem("off_ready"), c + 1)
                        sp.wait_ge(sem("dx_made"), c + 1)
                        load_xbc(sp, c + 2, r)
                    if prev:
                        store_x1(c - 1, 1 - r)
                        if nxt:
                            load_x(sp, c + 1, 1 - r)
                    if prev2:
                        store_g(c - 2, r)
                    if second:
                        sp.wait_ge(sem("gated"), c + 1)
                        load_z(sp, c + 2, r)

                body(0, 0, False, False, True)
                body(1, 1, True, False, True)
                with sp.Fori(0, NCH // 2 - 2) as i:
                    body(i * 2 + 2, 0, True, True, True)
                    body(i * 2 + 3, 1, True, True, True)
                body(NCH - 2, 0, True, True, True, False)
                body(NCH - 1, 1, True, True, False, False)
                store_x1(NCH - 1, 1)
                store_g(NCH - 2, 0)
                store_g(NCH - 1, 1)
                for r in range(2):
                    sp.wait_ge(sem(f"x1_stored{r}"), 16 + 16 * NCH // 2)
                    sp.wait_ge(sem(f"g_stored{r}"), 32 + 32 * NCH // 2)

            @block.gpsimd
            def _(pool):
                pool.memset(state[:, :], 0.0).then_inc(sem("state_made"), 1)

                def skip_part(c, r):
                    pool.wait_ge(sem(f"xbc_loaded{r}"), turn(c, r) * 16 + 16)
                    pool.tensor_tensor(dx[:, :, :], xz[:, r, 0:CT, :], dskip[:, :].unsqueeze(2).broadcast_to([P, CT, P]),
                                       ALU.mult).then_inc(sem("dx_made"), 1)

                def high_steps(c):
                    pool.tensor_tensor(step_h[:, :, :], upto[:, :].unsqueeze(1).broadcast_to([P, NH, P]),
                                       by_head(chunk_cols(dA_h, c), P), ALU.mult).then_inc(sem("step_high"), 1)

                def low_steps(c):
                    pool.tensor_tensor(step_l[:, :, :], upto[:, :].unsqueeze(1).broadcast_to([P, NH, P]),
                                       by_head(chunk_cols(dA_l, c), P), ALU.mult).then_inc(sem("step_low"), 1)

                def invert(c, r):
                    pool.wait_ge(sem("x1_step"), c * 2 + 2)
                    pool.tensor_tensor(rstd[:, r:r + 1], mv[:, r, 1:2], eps[:, 0:1], ALU.add)\
                        .then_inc(sem("x1_rstd"), 1)
                    pool.wait_ge(sem("x1_rstd"), c * 2 + 1)
                    pool.tensor_tensor(rstd[:, r:r + 1], rstd[:, r:r + 1], neghalf[:, 0:1], ALU.pow)\
                        .then_inc(sem("x1_rstd"), 1)

                def invert_rms(c):
                    pool.wait_ge(sem("rms_step"), c + 1)
                    pool.tensor_tensor(rms[:, :], rms[:, :], neghalf[:, 0:1], ALU.pow)\
                        .then_inc(sem("rms_inverted"), 1)

                def fade(c):
                    pool.wait_ge(sem("state_made"), c + 1)
                    pool.tensor_tensor(faded[:, :].rearrange("p (h d) -> p h d", h=NH),
                                       state[:, :].rearrange("p (h d) -> p h d", h=NH),
                                       by_head(chunk_cols(whole, c), HD), ALU.mult).then_inc(sem("state_faded"), 1)

                def body(c, r, prev, prev2, nxt):
                    further = nxt and not (isinstance(c, int) and c == NCH - 2)
                    if further:
                        pool.wait_ge(sem("seg_read"), (c + 2) * 4)
                        high_steps(c + 2)
                    if prev:
                        invert_rms(c - 1)
                    if further:
                        low_steps(c + 2)
                    if nxt:
                        fade(c + 1)
                    if prev:
                        invert(c - 1, 1 - r)
                    if nxt:
                        pool.wait_ge(sem("skip_added"), c + 1)
                        skip_part(c + 1, 1 - r)

                pool.wait_ge(sem("scan_params"), 64)
                skip_part(0, 0)
                pool.wait_ge(sem("dA_split"), 2)
                low_steps(0)
                pool.wait_ge(sem("whole_made"), 1)
                fade(0)
                pool.wait_ge(sem("seg_read"), 4)
                high_steps(1)
                low_steps(1)
                over_chunks(pool, body)
                invert_rms(NCH - 1)
                invert(NCH - 1, 1)

            @block.vector
            def _(dve):
                link = [0]

                def linked(ins):
                    link[0] += 1
                    ins.then_inc(sem("scan_link"), 1)
                    dve.wait_ge(sem("scan_link"), link[0])

                raw = dt_raw[:, :, :].rearrange("p c h -> p (c h)")
                neg, na, e, t, d, z, q, sp_ = (small[:, k, :] for k in range(8))
                linked(dve.tensor_scalar(neg, raw, -1.0, None, ALU.mult))
                dve.tensor_tensor(na, raw, neg, ALU.min).then_inc(sem("dt_neg"), 1)
                dve.wait_ge(sem("dt_exp"), 1)
                dve.tensor_scalar(t, e, 1.0, None, ALU.add).then_inc(sem("dt_one"), 1)
                dve.wait_ge(sem("dt_one"), 1)
                linked(dve.tensor_scalar(d, t, 1.0, None, ALU.subtract))
                linked(dve.tensor_scalar(z, d, 0.0, None, ALU.is_equal))
                linked(dve.tensor_tensor(d, d, z, ALU.add))
                linked(dve.reciprocal(q, d))
                linked(dve.tensor_tensor(q, q, e, ALU.mult))
                dve.wait_ge(sem("dt_ln"), 1)
                linked(dve.tensor_tensor(q, q, sp_, ALU.mult))
                linked(dve.tensor_tensor(z, z, e, ALU.mult))
                linked(dve.tensor_tensor(q, q, z, ALU.add))
                linked(dve.scalar_tensor_tensor(out=dt[:, :, :].rearrange("p c h -> p (c h)"), in0=raw, scalar=0.0,
                                                in1=q, op0=ALU.max, op1=ALU.add))
                dve.wait_ge(sem("a_exp"), 1)
                dve.scalar_tensor_tensor(out=dA[:, :, :], in0=dt[:, :, :], scalar=-1.0,
                                         in1=arow[:, :].unsqueeze(1).broadcast_to([P, NCH, NH]),
                                         op0=ALU.mult, op1=ALU.mult).then_inc(sem("dA_made"), 1)
                dve.wait_ge(sem("dA_made"), 1)
                dve.tensor_copy(dA_h[:, :, :], dA[:, :, :]).then_inc(sem("dA_split"), 1)
                dve.wait_ge(sem("dA_split"), 1)
                dve.tensor_tensor(dA_l[:, :, :], dA[:, :, :], dA_h[:, :, :], ALU.subtract).then_inc(sem("dA_split"), 1)

                def set_gate(dst, tmp, row):
                    linked(dve.scalar_tensor_tensor(out=dst, in0=row, scalar=-1.0, in1=row, op0=ALU.mult, op1=ALU.max))
                    linked(dve.tensor_scalar(tmp, row, 0.0, 2.0, ALU.is_ge, ALU.mult))
                    linked(dve.tensor_scalar(tmp, tmp, -1.0, None, ALU.add))
                    linked(dve.scalar_tensor_tensor(out=dst, in0=dst, scalar=0.25, in1=tmp, op0=ALU.max, op1=ALU.mult))

                def weights_out():
                    set_gate(ga[:, :], ga_t[:, :], modrow[:, 2, :])
                    linked(dve.tensor_copy(ga_s[:, 0, :], modrow[:, 5, :]))
                    set_gate(modrow[:, 5, :], ga_t[:, :], ga_s[:, 0, :])
                    dve.wait_ge(sem("scan_params"), 64)
                    for t_ in range(CT):
                        dve.wait_ge(sem(f"wo_loaded{t_ % 2}"), 16 * (t_ // 2) + 16)
                        dve.scalar_tensor_tensor(out=ga_s[:, t_ % 2, :], in0=wo_raw[:, t_ % 2, :],
                                                 scalar=nw[:, t_:t_ + 1], in1=ga[:, :], op0=ALU.mult, op1=ALU.mult)\
                           .then_inc(sem("wo_scaled"), 1)
                        dve.wait_ge(sem("wo_scaled"), t_ + 1)
                        scaled = ga_s[:, t_ % 2, :]
                        linked(dve.tensor_copy(wo_h[:, t_, :], scaled))
                        linked(dve.tensor_tensor(wo_l[:, t_, :], scaled, wo_h[:, t_, :], ALU.subtract))

                def first_steps():
                    dve.tensor_tensor(step_h[:, :, :], upto[:, :].unsqueeze(1).broadcast_to([P, NH, P]),
                                      by_head(dA_h[:, 0, :], P), ALU.mult).then_inc(sem("step_high"), 1)

                def mask_cb(c):
                    dve.wait_ge(sem("cb_ready"), c + 1)
                    if not (isinstance(c, int) and c == 0):
                        dve.wait_ge(sem("M_ready"), c * 4)
                    dve.tensor_tensor(cbm[:, :], cb_ps, upto[:, :], ALU.mult).then_inc(sem("cb_masked"), 1)

                def mask_decay(c, r):
                    dve.wait_ge(sem("cb_masked"), c + 1)
                    for g in range(4):
                        dve.wait_ge(sem("seg_exp"), c * 4 + g + 1)
                        m = M[:, r, 4 * g:4 * g + 4, :]
                        dve.tensor_tensor(m, m, cbm[:, :].unsqueeze(1).broadcast_to([P, 4, P]), ALU.mult)\
                           .then_inc(sem("M_ready"), 1)

                def weigh_x(c, r):
                    dve.wait_ge(sem("x_turned"), c + 1)
                    src = pair_flat.rearrange("p (h d) -> p h d", h=NH)
                    dve.tensor_tensor(xdt[:, r, :].rearrange("p (h d) -> p h d", h=NH), src,
                                      by_head(chunk_cols(dt, c), HD), ALU.mult)
                    dve.tensor_tensor(xdl[:, :].rearrange("p (h d) -> p h d", h=NH), src,
                                      by_head(chunk_cols(dt_left, c), HD), ALU.mult).then_inc(sem("x_weighed"), 1)

                def body(c, r, prev, prev2, nxt):
                    dve.wait_ge(sem("off_ready"), c + 1)
                    dve.tensor_tensor(yoff[:, :].rearrange("p (h d) -> p h d", h=NH),
                                      pair_flat.rearrange("p (h d) -> p h d", h=NH),
                                      by_head(chunk_cols(grown, c), HD), ALU.mult).then_inc(sem("off_scaled"), 1)
                    if prev:
                        low_y(c - 1)
                    if nxt:
                        mask_cb(c + 1)
                    if prev:
                        sum_squares(c - 1)
                    if nxt:
                        mask_decay(c + 1, 1 - r)
                    if prev:
                        mean_square(c - 1)
                    dve.wait_ge(sem("states_ready"), c + 1)
                    dve.wait_ge(sem("state_faded"), c + 1)
                    dve.tensor_tensor(state[:, :], faded[:, :], pair_flat, ALU.add).then_inc(sem("state_made"), 1)
                    if prev2:
                        split_g(c - 2, r)
                    if prev:
                        finish(c - 1, 1 - r)
                        deviation(c - 1, 1 - r)
                    if nxt:
                        weigh_x(c + 1, 1 - r)
                    if prev:
                        centre(c - 1, 1 - r)
                    dve.wait_ge(sem("y_summed"), c + 1)
                    dve.wait_ge(sem("dx_made"), c + 1)
                    dve.tensor_tensor(y1[:, :, :].rearrange("p t l -> p (t l)"), y_flat,
                                      dx[:, :, :].rearrange("p t l -> p (t l)"), ALU.add)\
                       .then_inc(sem("skip_added"), 1)
                    dve.wait_ge(sem("skip_added"), c + 1)
                    if prev:
                        dve.wait_ge(sem("y_squared"), c)
                        dve.wait_ge(sem("y_low"), c)
                    dve.wait_ge(sem(f"z_loaded{r}"), turn(c, r) * 16 + 16)
                    dve.tensor_tensor(y[:, :, :], y1[:, :, :], xz[:, r, NXBC:NST, :], ALU.mult)\
                       .then_inc(sem("gated"), 1)

                def low_y(c):
                    dve.wait_ge(sem("y_high"), c + 1)
                    dve.tensor_tensor(y_l[:, :, :], y[:, :, :], y_h[:, :, :], ALU.subtract).then_inc(sem("y_low"), 1)

                def sum_squares(c):
                    dve.wait_ge(sem("y_squared"), c + 1)
                    dve.tensor_reduce(ysum[:, :], ysq[:, :, :].rearrange("p t l -> p l t"), AX.X, ALU.add)\
                       .then_inc(sem("squares_summed"), 1)

                def mean_square(c):
                    dve.wait_ge(sem("rms_ready"), c + 1)
                    if not (isinstance(c, int) and c == 0):
                        dve.wait_ge(sem("x1_made"), c)
                    dve.tensor_scalar(rms[:, :], ss_ps, 1.0 / DI, EPS, ALU.mult, ALU.add)\
                       .then_inc(sem("rms_step"), 1)

                def deviation(c, r):
                    dve.wait_ge(sem("x1_made"), c + 1)
                    dve.bn_stats(stats[:, :], x1[:, r, :]).then_inc(sem("x1_step"), 1)
                    dve.wait_ge(sem("x1_step"), c * 2 + 1)
                    dve.memset(idle[:, :], 0.0)
                    dve.bn_aggr(mv[:, r, :], stats[:, :]).then_inc(sem("x1_step"), 1)

                def centre(c, r):
                    dve.wait_ge(sem("x1_rstd"), c * 2 + 2)
                    dve.tensor_scalar(xn[:, r, :], x1[:, r, :], mv[:, r, 0:1], rstd[:, r:r + 1],
                                      ALU.subtract, ALU.mult).then_inc(sem("x1_centred"), 1)

                def split_g(c, r):
                    dve.wait_ge(sem("g_made"), c + 1)
                    dve.wait_ge(sem(f"g_stored{r}"), turn(c, r) * 32 + 32)
                    dve.tensor_copy(g_h[:, r, :], g[:, r, :]).then_inc(sem("g_high"), 1)
                    dve.wait_ge(sem("g_high"), c + 1)
                    dve.tensor_tensor(g_l[:, r, :], g[:, r, :], g_h[:, r, :], ALU.subtract).then_inc(sem("g_low"), 1)

                def finish(c, r):
                    dve.wait_ge(sem("out_ready"), c + 1)
                    dve.wait_ge(sem("rms_inverted"), c + 1)
                    k = turn(c, r)
                    dve.wait_ge(sem(f"xres_loaded{r}"), k * 16 + 16)
                    dve.wait_ge(sem(f"x1_stored{r}"), k * 16 + 16)
                    dve.scalar_tensor_tensor(out=x1[:, r, :], in0=out_bank, scalar=rms[:, 0:1], in1=xres[:, r, :],
                                             op0=ALU.mult, op1=ALU.add).then_inc(sem("x1_made"), 1)

                first_steps()
                dve.wait_ge(sem("decays_exp"), 1)
                linked(dve.tensor_tensor(dt_left[:, :, :], dt[:, :, :], left[:, :, :], ALU.mult))
                weigh_x(0, 0)
                mask_cb(0)
                mask_decay(0, 0)
                weights_out()
                over_chunks(dve, body)
                low_y(NCH - 1)
                sum_squares(NCH - 1)
                mean_square(NCH - 1)
                split_g(NCH - 2, 0)
                finish(NCH - 1, 1)
                deviation(NCH - 1, 1)
                centre(NCH - 1, 1)
                split_g(NCH - 1, 1)

            @block.scalar
            def _(act):
                na, e, t, sp_ = (small[:, k, :] for k in (1, 2, 3, 7))
                act.wait_ge(sem("scan_params"), 64)
                act.activation(arow[:, :], alog[:, :], ACT.Exp).then_inc(sem("a_exp"), 1)
                act.wait_ge(sem("dt_neg"), 1)
                act.activation(e, na, ACT.Exp).then_inc(sem("dt_exp"), 1)
                act.wait_ge(sem("dt_one"), 1)
                act.activation(sp_, t, ACT.Ln).then_inc(sem("dt_ln"), 1)
                act.wait_ge(sem("decay_sums"), 1)
                flat = lambda a: a[:, :, :].rearrange("p c h -> p (c h)")
                act.activation(flat(grown), seg_bank[0][:, 0:NC], ACT.Exp)
                act.activation(flat(left), seg_bank[0][:, NC:2 * NC], ACT.Exp).then_inc(sem("decays_exp"), 1)
                act.activation(flat(whole), seg_bank[1][:, 0:NC], ACT.Exp).then_inc(sem("whole_made"), 1)

                def decay(c, r, groups):
                    for g in groups:
                        act.wait_ge(sem("seg_read"), c * 4 + g + 1)
                        act.activation(M[:, r, 4 * g:4 * g + 4, :].rearrange("p h l -> p (h l)"), seg_bank[g % 2],
                                       ACT.Exp).then_inc(sem("seg_exp"), 1)

                def keep_b(c):
                    act.wait_ge(sem("b_turned"), c + 1)
                    act.activation(btok[:, :], bt_ps, ACT.Copy).then_inc(sem("b_kept"), 1)

                def modulate_g(c, r):
                    act.wait_ge(sem("x1_turned"), c + 1)
                    for kt in range(KT):
                        last = act.activation(g[:, r, kt * P:(kt + 1) * P], out_bank[:, kt * P:(kt + 1) * P],
                                              ACT.Identity, bias=modcol[:, 2, kt:kt + 1], scale=modcol[:, 3, kt:kt + 1])
                    last.then_inc(sem("g_made"), 1)

                def high_y(c):
                    act.wait_ge(sem("gated"), c + 1)
                    if not (isinstance(c, int) and c == 0):
                        act.wait_ge(sem("out_ready"), c)
                    act.activation(y_h[:, :, :], y[:, :, :], ACT.Copy).then_inc(sem("y_high"), 1)

                def square_y(c):
                    if not (isinstance(c, int) and c == 0):
                        act.wait_ge(sem("squares_summed"), c)
                    act.activation(ysq[:, :, :], y[:, :, :], ACT.Square).then_inc(sem("y_squared"), 1)

                def body(c, r, prev, prev2, nxt):
                    if prev:
                        high_y(c - 1)
                    if nxt:
                        decay(c + 1, 1 - r, (0, 1))
                    if prev:
                        square_y(c - 1)
                    if prev2:
                        modulate_g(c - 2, r)
                    if nxt:
                        decay(c + 1, 1 - r, (2, 3))
                        keep_b(c + 1)

                decay(0, 0, range(4))
                keep_b(0)
                over_chunks(act, body)
                high_y(NCH - 1)
                square_y(NCH - 1)
                modulate_g(NCH - 2, 0)
                modulate_g(NCH - 1, 1)

            @block.tensor
            def _(pe):
                pe.wait_ge(sem("dA_made"), 1)
                flat = dA[:, :, :].rearrange("p c h -> p (c h)")
                pe.matmul(seg_bank[0][:, 0:NC], upto[:, :], flat, start=True, stop=True)
                pe.matmul(seg_bank[0][:, NC:2 * NC], after[:, :], flat, start=True, stop=True)
                pe.matmul(seg_bank[1][:, 0:NC], ones[:, :], flat, start=True, stop=True)\
                  .then_inc(sem("decay_sums"), 1)

                def cb(c, r):
                    pe.wait_ge(sem(f"xbc_loaded{r}"), turn(c, r) * 16 + 16)
                    pe.matmul(cb_ps, xz[:, r, CT, :], xz[:, r, CT + 1, :], start=True, stop=True)\
                      .then_inc(sem("cb_ready"), 1)

                def segments(c, groups, first=False):
                    pe.wait_ge(sem("step_high"), c + 1)
                    pe.wait_ge(sem("step_low"), c + 1)
                    for g in groups:
                        if first:
                            pe.wait_ge(sem("whole_made"), 1)
                            if g >= 2:
                                pe.wait_ge(sem("seg_exp"), g - 1)
                        else:
                            pe.wait_ge(sem("seg_exp"), c * 4 + g - 1)
                        pe.matmul(seg_bank[g % 2], after_r[:, :],
                                  step_h[:, 4 * g:4 * g + 4, :].rearrange("p h l -> p (h l)"), start=True, stop=False)
                        pe.matmul(seg_bank[g % 2], after_r[:, :],
                                  step_l[:, 4 * g:4 * g + 4, :].rearrange("p h l -> p (h l)"), start=False, stop=True)\
                          .then_inc(sem("seg_read"), 1)

                def turn_x(c, r, first=False):
                    if not first:
                        pe.wait_ge(sem("state_made"), c + 1)
                    for t in range(CT):
                        last = pe.transpose(pair_flat[:, t * P:(t + 1) * P], xz[:, r, t, :], ident[:, :])
                    last.then_inc(sem("x_turned"), 1)
                    pe.wait_ge(sem("cb_masked"), c + 1)
                    if not (isinstance(c, int) and c <= 1):
                        pe.wait_ge(sem("rms_step"), c - 1)
                    pe.transpose(bt_ps, xz[:, r, CT, :], ident[:, :]).then_inc(sem("b_turned"), 1)

                def project_out(c):
                    pe.wait_ge(sem("y_low"), c + 1)
                    three_pass(pe, out_bank, [(y_h[:, t, :], y_l[:, t, :], wo_h[:, t, :], wo_l[:, t, :])
                                              for t in range(CT)]).then_inc(sem("out_ready"), 1)

                def turn_x1(c, r):
                    pe.wait_ge(sem("x1_centred"), c + 1)
                    for kt in range(KT):
                        last = pe.transpose(out_bank[:, kt * P:(kt + 1) * P], xn[:, r, kt * P:(kt + 1) * P], ident[:, :])
                    last.then_inc(sem("x1_turned"), 1)

                def square_sum(c):
                    pe.wait_ge(sem("squares_summed"), c + 1)
                    pe.matmul(ss_ps, ysum[:, :], ones[:, 0:1], start=True, stop=True).then_inc(sem("rms_ready"), 1)

                def body(c, r, prev, prev2, nxt):
                    pe.wait_ge(sem("x_weighed"), c + 1)
                    pe.wait_ge(sem("state_made"), c + 1)
                    for n in range(2):
                        last = pe.matmul(pair[:, n, :], xz[:, r, CT + 1, :], state[:, n * 512:(n + 1) * 512],
                                         start=True, stop=True)
                    last.then_inc(sem("off_ready"), 1)
                    if prev2:
                        turn_x1(c - 2, r)
                    if nxt:
                        segments(c + 1, (0, 1))
                    pe.wait_ge(sem("b_kept"), c + 1)
                    if nxt:
                        cb(c + 1, 1 - r)
                    pe.wait_ge(sem("off_scaled"), c + 1)
                    for n in range(2):
                        last = pe.matmul(pair[:, n, :], btok[:, :], xdl[:, n * 512:(n + 1) * 512], start=True, stop=True)
                    last.then_inc(sem("states_ready"), 1)
                    if nxt:
                        segments(c + 1, (2, 3))
                    if prev:
                        if nxt:
                            pe.wait_ge(sem("cb_masked"), c + 2)
                        square_sum(c - 1)
                    if prev2:
                        pe.wait_ge(sem("g_made"), c - 1)
                    if prev:
                        project_out(c - 1)
                    if nxt:
                        turn_x(c + 1, 1 - r)
                    pe.wait_ge(sem("M_ready"), c * 4 + 4)
                    if prev:
                        pe.wait_ge(sem("skip_added"), c)
                    for t in range(CT):
                        y_t = y_flat[:, t * P:(t + 1) * P]
                        pe.matmul(y_t, yoff[:, t * P:(t + 1) * P], ident[:, :], start=True, stop=False,
                                  skip_group_check=True)
                        for half in range(2):
                            h = 2 * t + half
                            last = pe.matmul(y_t[half * HD:(half + 1) * HD, :], xdt[:, r, h * HD:(h + 1) * HD],
                                             M[:, r, h, :], start=False, stop=True, skip_group_check=True)
                    last.then_inc(sem("y_summed"), 1)

                cb(0, 0)
                turn_x(0, 0, True)
                segments(0, range(4), first=True)
                over_chunks(pe, body)
                square_sum(NCH - 1)
                turn_x1(NCH - 2, 0)
                pe.wait_ge(sem("g_made"), NCH - 1)
                project_out(NCH - 1)
                turn_x1(NCH - 1, 1)


def ffn_stage(nc, sem, sb0, ps, w_gu, w_down, x1_dram, gT_dram, out, modrow):
    with ExitStack() as st:
        def sb(name, shape, dt=F32):
            return sb0(name, shape, dt, st)

        HT = 8
        NN = 2 * NIC
        LAST = 2 * NN - 1
        RING = 3
        gu_h = sb("gu_h", [P, 4, 2, KT, P], F32R)
        gu_l = sb("gu_l", [P, 4, 2, KT, P], F32R)
        dn_h = sb("dn_h", [P, 4, D], F32R)
        dn_l = sb("dn_l", [P, 4, D], F32R)
        raw = sb("ffn_raw", [P, RING, 1024])
        dn_s = sb("dn_s", [P, 2, D])
        acc = sb("acc", [P, HT, D])
        gT_h = sb("gT_h", [P, HT, KT, P], F32R)
        gT_l = sb("gT_l", [P, HT, KT, P], F32R)
        sg = sb("sg", [P, 2, TB])
        hid = sb("hid", [P, 4, TB])
        mag = sb("mag", [P, 4, TB])
        top = sb("top", [P, 2, TB])
        low = sb("low", [P, 2, TB])
        first = sb("first", [P, 2, TB], BF16)
        both = sb("both", [P, 2, TB], BF16)
        lead = sb("lead", [P, TB], BF16)
        keep = sb("keep", [P, 4, TB], BF16)
        hs_h = sb("hs_h", [P, 4, TB], F32R)
        hs_l = sb("hs_l", [P, 4, TB], F32R)

        gate_bank = [ps[:, 0, :], ps[:, 1, :]]
        up_bank = [ps[:, 2, :], ps[:, 3, :]]
        down_bank = [ps[:, 4 + t, :] for t in range(4)]
        HID0, DOWN0, ACC0, LOW0, HS0 = 2, 4, 4, RING, 4

        with nc.Block() as block:
            @block.sync
            def _(sp):
                with sp.Fori(0, NN) as N:
                    for p in range(6):
                        sp.wait_ge(sem("piece_split"), N * 6 + p + 1)
                        if p < 4:
                            src = w_gu[bass.ds(N % NIC, 1), p, :, :].rearrange("o p n -> p (o n)")
                        else:
                            src = w_down[bass.ds(N % NIC, 1), p - 4, :, :].rearrange("o p n -> p (o n)")
                        sp.dma_start(raw[:, p % RING, :], src).then_inc(sem(f"piece_loaded{p % RING}"), 16)

            @block.gpsimd
            def _(pool):
                def load_g(h, g):
                    tiles = slice(g * TT, (g + 1) * TT)
                    rows = slice(h * HT + g * TT, h * HT + (g + 1) * TT)
                    for part, dst in ((0, gT_h), (1, gT_l)):
                        pool.dma_start(dst[:, tiles, :, :].rearrange("p t k q -> p t (k q)"),
                                       gT_dram[part, rows, :, :].rearrange("t p n -> p t n"))\
                            .then_inc(sem(f"g_loaded{g}"), 16)

                def load_acc(h, g):
                    rows = slice(h * HT + g * TT, h * HT + (g + 1) * TT)
                    pool.dma_start(acc[:, g * TT:(g + 1) * TT, :], x1_dram[rows, :, :].rearrange("t p n -> p t n"))\
                        .then_inc(sem(f"acc_loaded{g}"), 16)

                def store(h, g):
                    rows = slice(h * HT + g * TT, h * HT + (g + 1) * TT)
                    pool.wait_ge(sem("acc_added"), ACC0 + 4 * ((h * NIC + NIC - 1) * 2 + g + 1))
                    pool.dma_start(out[rows, :, :].rearrange("t p n -> p t n"), acc[:, g * TT:(g + 1) * TT, :])\
                        .then_inc(sem(f"out_stored{g}"), 16)

                for g in range(2):
                    load_g(0, g)
                for g in range(2):
                    load_acc(0, g)
                for g in range(2):
                    pool.wait_ge(sem("up_ready"), 4 * ((NIC - 1) * 2 + g + 1))
                    load_g(1, g)
                for g in range(2):
                    store(0, g)
                    pool.wait_ge(sem(f"out_stored{g}"), 16)
                    load_acc(1, g)
                for g in range(2):
                    store(1, g)
                for g in range(2):
                    pool.wait_ge(sem(f"out_stored{g}"), 32)

            def piece_ready(eng, N, p):
                eng.wait_ge(sem(f"piece_loaded{p % RING}"), N * 32 + 16 * (p // RING) + 16)

            def flat(ap):
                return ap.rearrange("p a k q -> p (a k q)")

            @block.scalar
            def _(act):
                def round_gu(N, p, free=True):
                    piece_ready(act, N, p)
                    if free:
                        act.wait_ge(sem("up_ready"), N * 8 - 3 + p)
                    act.activation(flat(gu_h[:, p, :, :, :]), raw[:, p % RING, :], ACT.Copy)\
                       .then_inc(sem("gu_high"), 1)

                def magnitude(n, j):
                    act.wait_ge(sem("hid_made"), n * 4 + j + 1 + HID0)
                    act.activation(mag[:, j, :], hid[:, j, :], ACT.Abs).then_inc(sem("mag_made"), 1)

                def group(n, following=None):
                    for j in range(4):
                        act.wait_ge(sem("gate_ready"), n * 4 + j + 1)
                        act.wait_ge(sem("hid_made"), n * 4 + j - 2 + 1 + HID0)
                        act.activation(sg[:, j % 2, :], gate_bank[j % 2], ACT.Silu).then_inc(sem("gate_silu"), 1)
                        if j >= 1:
                            magnitude(n, j - 1)
                            if following is not None:
                                round_gu(following, j - 1)
                    magnitude(n, 3)
                    if following is not None:
                        round_gu(following, 3)
                    for j in range(4):
                        act.wait_ge(sem("kept"), n * 4 + j + 1)
                        act.wait_ge(sem("down_ready"), n * 4 + DOWN0)
                        act.activation(hs_h[:, j, :], hid[:, j, :], ACT.Copy).then_inc(sem("hs_high"), 1)

                for p in range(4):
                    round_gu(0, p, free=False)
                with act.Fori(0, NN - 1) as N:
                    group(N * 2)
                    group(N * 2 + 1, N + 1)
                group(LAST - 1)
                group(LAST)

            @block.vector
            def _(dve):
                def low_gu(N, p):
                    dve.wait_ge(sem("gu_high"), N * 4 + p + 1)
                    dve.tensor_tensor(flat(gu_l[:, p, :, :, :]), raw[:, p % RING, :], flat(gu_h[:, p, :, :, :]),
                                      ALU.subtract).then_inc(sem("piece_split"), 1)

                def split_down(N):
                    for p in (4, 5):
                        k = N * 2 + (p - 4)
                        piece_ready(dve, N, p)
                        dve.wait_ge(sem("piece_split"), N * 6 + p + LOW0)
                        dst = slice((p - 4) * 2, (p - 4) * 2 + 2)
                        dve.tensor_tensor(dn_s[:, :, :], raw[:, p % RING, :].rearrange("p (a d) -> p a d", a=2),
                                          modrow[:, 5, :].unsqueeze(1).broadcast_to([P, 2, D]), ALU.mult)\
                           .then_inc(sem("dn_step"), 1)
                        dve.wait_ge(sem("dn_step"), k * 2 + 1)
                        dve.wait_ge(sem("down_ready"), N * 8 + DOWN0)
                        dve.tensor_copy(dn_h[:, dst, :], dn_s[:, :, :]).then_inc(sem("dn_step"), 1)
                        dve.wait_ge(sem("dn_step"), k * 2 + 2)
                        dve.tensor_tensor(dn_l[:, dst, :], dn_s[:, :, :], dn_h[:, dst, :], ALU.subtract)\
                           .then_inc(sem("piece_split"), 1)

                def compare(n):
                    m4 = mag[:, :, :].rearrange("p (a e) t -> p a e t", e=2)
                    dve.wait_ge(sem("mag_made"), n * 4 + 4)
                    dve.tensor_tensor(top[:, :, :], m4[:, :, 0, :], m4[:, :, 1, :], ALU.max)
                    dve.tensor_tensor(low[:, :, :], m4[:, :, 0, :], m4[:, :, 1, :], ALU.min)
                    dve.tensor_tensor(first[:, :, :], m4[:, :, 0, :], m4[:, :, 1, :], ALU.is_ge)\
                       .then_inc(sem("compared"), 1)
                    dve.wait_ge(sem("compared"), n * 3 + 1)
                    dve.tensor_tensor(both[:, 0, :], low[:, 0, :], top[:, 1, :], ALU.is_ge)
                    dve.tensor_tensor(both[:, 1, :], low[:, 1, :], top[:, 0, :], ALU.is_gt)\
                       .then_inc(sem("compared"), 1)
                    dve.wait_ge(sem("compared"), n * 3 + 2)
                    dve.tensor_tensor(lead[:, :], both[:, 0, :], both[:, 1, :], ALU.subtract)\
                       .then_inc(sem("compared"), 1)
                    dve.wait_ge(sem("compared"), n * 3 + 3)
                    dve.tensor_tensor(keep[:, 0, :], first[:, 0, :], lead[:, :], ALU.add)
                    dve.tensor_tensor(keep[:, 1, :], lead[:, :], first[:, 0, :], ALU.subtract)
                    dve.tensor_tensor(keep[:, 2, :], first[:, 1, :], lead[:, :], ALU.subtract)
                    dve.tensor_tensor(keep[:, 3, :], first[:, 1, :], lead[:, :], ALU.add)\
                       .then_inc(sem("keep_made"), 1)

                def select(n):
                    rule = ((1.0, ALU.is_ge), (0.0, ALU.is_ge), (1.0, ALU.is_ge), (0.0, ALU.is_le))
                    dve.wait_ge(sem("keep_made"), n + 1)
                    for j in range(4):
                        bound, op = rule[j]
                        dve.scalar_tensor_tensor(out=hid[:, j, :], in0=keep[:, j, :], scalar=bound, in1=hid[:, j, :],
                                                 op0=op, op1=ALU.mult).then_inc(sem("kept"), 1)

                def low_kept(n):
                    for j in range(4):
                        dve.wait_ge(sem("hs_high"), n * 4 + j + 1)
                        dve.tensor_tensor(hs_l[:, j, :], hid[:, j, :], hs_h[:, j, :], ALU.subtract)\
                           .then_inc(sem("hs_low"), 1)

                def add_down(n, g, N):
                    dve.wait_ge(sem(f"acc_loaded{g}"), N // NIC * 16 + 16)
                    for t in range(TT):
                        dve.wait_ge(sem("down_ready"), n * 4 + t + 1 + DOWN0)
                        dve.tensor_tensor(acc[:, g * TT + t, :], acc[:, g * TT + t, :], down_bank[t], ALU.add)\
                           .then_inc(sem("acc_added"), 1)

                def group(n, following=None, before=None, down_of=None):
                    for j in range(4):
                        dve.wait_ge(sem("gate_silu"), n * 4 + j + 1)
                        dve.wait_ge(sem("up_ready"), n * 4 + j + 1)
                        dve.wait_ge(sem("hs_low"), n * 4 + HS0)
                        dve.tensor_tensor(hid[:, j, :], sg[:, j % 2, :], up_bank[j % 2], ALU.mult)\
                           .then_inc(sem("hid_made"), 1)
                        if following is not None and j >= 1:
                            low_gu(following, j - 1)
                    if following is not None:
                        low_gu(following, 3)
                    compare(n)
                    select(n)
                    if before is not None:
                        add_down(*before)
                    low_kept(n)
                    if down_of is not None:
                        split_down(down_of)

                dve.sem_inc(sem("hid_made"), HID0)
                dve.sem_inc(sem("acc_added"), ACC0)
                dve.sem_inc(sem("piece_split"), LOW0)
                dve.sem_inc(sem("hs_low"), HS0)
                for p in range(4):
                    low_gu(0, p)
                group(0, down_of=0)
                with dve.Fori(0, NN - 1) as N:
                    group(N * 2 + 1, following=N + 1, before=(N * 2, 0, N))
                    group(N * 2 + 2, before=(N * 2 + 1, 1, N), down_of=N + 1)
                group(LAST, before=(LAST - 1, 0, NN - 1))
                add_down(LAST, 1, NN - 1)

            @block.tensor
            def _(pe):
                def gate_up(n, N, g):
                    tiles = slice(g * TT, (g + 1) * TT)
                    pe.wait_ge(sem(f"g_loaded{g}"), N // NIC * 32 + 32)
                    for j in range(4):
                        if g == 0:
                            pe.wait_ge(sem("gu_high"), N * 4 + j + 1)
                            pe.wait_ge(sem("piece_split"), N * 6 + j + 1 + LOW0)
                        pe.wait_ge(sem("hid_made"), n * 4 + j - 2 + 1 + HID0)
                        for a, bank, ready in ((0, gate_bank[j % 2], "gate_ready"), (1, up_bank[j % 2], "up_ready")):
                            three_pass(pe, bank, [(gu_h[:, j, a, kt, :], gu_l[:, j, a, kt, :],
                                                   gT_h[:, tiles, kt, :], gT_l[:, tiles, kt, :])
                                                  for kt in range(KT)]).then_inc(sem(ready), 1)

                def down(n, N, g):
                    pe.wait_ge(sem("hs_low"), n * 4 + 4 + HS0)
                    if g == 0:
                        pe.wait_ge(sem("piece_split"), N * 6 + 6 + LOW0)
                    for t in range(TT):
                        pe.wait_ge(sem("acc_added"), n * 4 + t - 4 + 1 + ACC0)
                        three_pass(pe, down_bank[t],
                                   [(hs_h[:, j, t * P:(t + 1) * P], hs_l[:, j, t * P:(t + 1) * P],
                                     dn_h[:, j, :], dn_l[:, j, :]) for j in range(4)])\
                            .then_inc(sem("down_ready"), 1)

                pe.sem_inc(sem("down_ready"), DOWN0)
                gate_up(0, 0, 0)
                with pe.Fori(0, NN - 1) as N:
                    gate_up(N * 2 + 1, N, 1)
                    down(N * 2, N, 0)
                    gate_up(N * 2 + 2, N + 1, 0)
                    down(N * 2 + 1, N, 1)
                gate_up(LAST, NN - 1, 1)
                down(LAST - 1, NN - 1, 0)
                down(LAST, NN - 1, 1)


def kernel(L0_attn_u, L0_attn_in_proj_w, L0_attn_conv_w, L0_attn_conv_b, L0_attn_dt_bias, L0_attn_A_log,
           L0_attn_D_skip, L0_attn_norm_w, L0_attn_out_proj_w, L0_ffn_w_gate, L0_ffn_w_up, L0_ffn_w_down,
           L0_c, L0_wmod):
    import numpy as np
    import concourse.bacc as bacc
    from concourse.bass_utils import run_bass_kernel_spmd

    def own(a):
        return np.ascontiguousarray(a)

    def wide(a):
        return own(np.broadcast_to(np.asarray(a)[None, :], (P, np.asarray(a).shape[0])))

    u = np.asarray(L0_attn_u)
    gu = np.stack([np.asarray(w).reshape(KT, P, NIC, P, 4).transpose(2, 4, 1, 0, 3)
                   for w in (L0_ffn_w_gate, L0_ffn_w_up)], axis=3)
    down = np.asarray(L0_ffn_w_down).reshape(NIC, P, 2, 2, D).transpose(0, 2, 1, 3, 4)
    arrays = {
        "x": own(u.reshape(NCH, P, D)),
        "w_in": own(np.asarray(L0_attn_in_proj_w).T.reshape(KT, P, DIN).transpose(1, 0, 2)),
        "w_out": own(np.asarray(L0_attn_out_proj_w).T.reshape(CT, P, D)),
        "conv_w": own(np.asarray(L0_attn_conv_w).reshape(NXBC, P, TAPS).transpose(1, 0, 2)),
        "conv_b": own(np.asarray(L0_attn_conv_b).reshape(NXBC, P).T),
        "dt_bias": wide(L0_attn_dt_bias),
        "a_log": wide(L0_attn_A_log),
        "d_skip": own(np.broadcast_to(np.asarray(L0_attn_D_skip).reshape(CT, 2).T[:, None, :], (2, HD, CT))),
        "norm_w": own(np.asarray(L0_attn_norm_w).reshape(CT, P).T),
        "w_gu": own(gu.reshape(NIC, 4, P, 2 * KT * P)),
        "w_down": own(down.reshape(NIC, 2, P, 2 * D)),
        "c": own(np.asarray(L0_c).reshape(KT, P).T),
        "w_mod": own(np.asarray(L0_wmod).reshape(KT, P, 6 * D).transpose(1, 0, 2)),
    }
    nc = bacc.Bacc("TRN2", target_bir_lowering=False, num_devices=1)
    args = [nc.dram_tensor(n, a.shape, mybir.dt.from_np(a.dtype), kind="ExternalInput").ap()
            for n, a in arrays.items()]
    out = nc.dram_tensor("out", (NCH, P, D), F32, kind="ExternalOutput").ap()
    build(nc, *args, out)
    r = run_bass_kernel_spmd(nc, [arrays], core_ids=[0])
    return np.asarray(r.results[0]["out"]).reshape(1, L, D)
```

```python
from contextlib import ExitStack

import concourse.bass as bass
from concourse import mybir

F32 = mybir.dt.float32
F32R = mybir.dt.float32r
BF16 = mybir.dt.bfloat16
ALU = mybir.AluOpType
ACT = mybir.ActivationFunctionType
AX = mybir.AxisListType

P = 128
L = 2048
D = 512
DI = 1024
NS = 128
NH = 16
HD = DI // NH
KT = D // P
CT = DI // P
NXBC = CT + 2
DIN = 2 * DI + 2 * NS + NH
TB = 512
NB = L // TB
TT = TB // P
NCH = L // P
EPS = 1e-5
FI = 2048
NIC = FI // 512
HT = NCH // 2
RING = 3
PIECE = 1024
TAPS = 4

WP = DIN // 8
NWP = DIN // WP
WORDER = tuple(range(NWP - 1, NWP)) + tuple(range(DI // WP, NWP - 1)) + tuple(range(DI // WP))
NJ = 1 + NXBC + CT
NST = NXBC + CT


def column_of(j):
    if j == 0:
        return DIN - P
    return DI + P * (j - 1) if j <= NXBC else P * (j - 1 - NXBC)


def piece(i):
    return slice(WORDER[i] * WP, (WORDER[i] + 1) * WP)


def pieces_until(c0):
    return max(WORDER.index(c0 // WP), WORDER.index((c0 + P - 1) // WP)) + 1


def three_pass(pe, out, pairs, start=True, stop=True):
    n = len(pairs)
    for i, (lh, ll, rh, rl) in enumerate(pairs):
        pe.matmul(out, lh, rh, start=(start and i == 0), stop=False)
        pe.matmul(out, lh, rl, start=False, stop=False)
        last = pe.matmul(out, ll, rh, start=False, stop=(stop and i == n - 1))
    return last


class Mixer:
    def __init__(self, nc, sb):
        self.wo_h = sb("wo_h", [P, CT, D], F32R)
        self.wo_h_at = nc.sbuf_top
        self.wo_l = sb("wo_l", [P, CT, D], F32R)
        self.wo_l_at = nc.sbuf_top
        self.dA_h = sb("dA_h", [P, NCH, NH], F32R)
        self.dA_l = sb("dA_l", [P, NCH, NH], F32R)
        decays = sb("decays", [P, 2, NCH, NH])
        self.decays_at = nc.sbuf_top
        self.grown = decays[:, 0, :, :]
        self.whole = decays[:, 1, :, :]
        self.left = sb("left", [P, NCH, NH])
        self.dskip = sb("dskip", [P, CT])


def build(nc, x, w_in, w_out, conv_w, conv_b, dt_bias, a_log, d_skip, norm_w, w_gu, w_down, c, w_mod, out):
    with ExitStack() as ctx:
        sems = {}

        def sem(name):
            if name not in sems:
                sems[name] = ctx.enter_context(nc.semaphore(name))
            return sems[name]

        def sb(name, shape, dt=F32, stack=ctx):
            return stack.enter_context(nc.sbuf_tensor(name, shape, dt))

        xz_dram = nc.dram_tensor("xz_scratch", [NCH, P, NST, P], F32).ap()
        x1_dram = nc.dram_tensor("x1_scratch", [NCH, P, D], F32).ap()
        gT_dram = nc.dram_tensor("gT_scratch", [2, NCH, P, D], F32).ap()

        ident = sb("ident", [P, P])
        upto = sb("upto", [P, P])
        after = sb("after", [P, P])
        after_r = sb("after_r", [P, P], F32R)
        ones = sb("ones", [P, P])
        eps = sb("eps", [P, TT])
        neghalf = sb("neghalf", [P, TT])
        modrow = sb("modrow", [P, 6, D])
        modcol = sb("modcol", [P, 4, KT])
        dt = sb("dt", [P, NCH, NH])
        ps = ctx.enter_context(nc.psum_tensor("ps", [P, 8, 512], F32))

        def over(name, shape, place, dt=F32):
            return nc.alloc_sbuf_tensor_at(name, shape, dt, offset=place)

        gT_h = sb("gT_h", [P, HT, KT, P], F32R)
        gT_l = sb("gT_l", [P, HT, KT, P], F32R)
        g_at = nc.sbuf_base - 2 * HT * D * 4

        raw_at = nc.sbuf_base
        raw = over("ffn_raw", [P, RING, PIECE], raw_at)

        with ExitStack() as mixer:
            mx = Mixer(nc, lambda name, shape, dt=F32: mixer.enter_context(nc.sbuf_tensor(name, shape, dt,
                                                                                          side="right")))
            project_stage(nc, sem, sb, ps, x, w_in, w_out, conv_w, conv_b, dt_bias, a_log, d_skip, norm_w, c, w_mod,
                          xz_dram, ident, upto, after, after_r, ones, neghalf, eps, modrow, modcol, dt, mx,
                          over, g_at)
            scan_stage(nc, sem, sb, ps, x, xz_dram, x1_dram, gT_dram, ident, upto, after_r, ones, neghalf, eps,
                       modcol, dt, mx, gT_h, gT_l, raw, w_gu)
        ffn_stage(nc, sem, sb, ps, w_gu, w_down, x1_dram, gT_dram, out, modrow, gT_h, gT_l, raw)


def tile_statistics(dve, sem, tag, blk, x_tiles, stats, mv, idle):
    step = sem(f"{tag}_ln_step")
    for i in range(TT):
        ins = dve.bn_stats(stats[:, i, :], x_tiles[:, i, :])
    ins.then_inc(step, 1)
    dve.wait_ge(step, blk * 2 + 1)
    dve.wait_ge(sem(f"{tag}_xn_ready"), blk * TT + 1)
    dve.memset(idle[:, :], 0.0)
    for i in range(TT):
        ins = dve.bn_aggr(mv[:, i, :], stats[:, i, :])
    ins.then_inc(step, 1)


def inverse_deviation(pool, sem, tag, blk, mv, rstd, neghalf, eps):
    pool.wait_ge(sem(f"{tag}_ln_step"), blk * 2 + 2)
    pool.wait_ge(sem(f"{tag}_xn_ready"), blk * TT + 1)
    pool.tensor_tensor(rstd[:, :], mv[:, :, 1], eps[:, :], ALU.add).then_inc(sem(f"{tag}_rstd"), 1)
    pool.wait_ge(sem(f"{tag}_rstd"), blk * 2 + 1)
    pool.tensor_tensor(rstd[:, :], rstd[:, :], neghalf[:, :], ALU.pow).then_inc(sem(f"{tag}_rstd"), 1)


def normalise_tile(dve, sem, tag, n, i, blk, x_tile, xn, mv, rstd):
    dve.wait_ge(sem(f"{tag}_rstd"), blk * 2 + 2)
    dve.wait_ge(sem(f"{tag}_xn_turned"), n + 1)
    dve.tensor_scalar(xn, x_tile, mv[:, i, 0:1], rstd[:, i:i + 1], ALU.subtract, ALU.mult)\
       .then_inc(sem(f"{tag}_xn_ready"), 1)


def turn_tile(pe, sem, tag, n, xn, bank, ident):
    pe.wait_ge(sem(f"{tag}_xn_ready"), n + 2)
    pe.wait_ge(sem(f"{tag}_modulated"), n + 1)
    for kt in range(KT):
        last = pe.transpose(bank[:, kt * P:(kt + 1) * P], xn[:, kt * P:(kt + 1) * P], ident[:, :])
    last.then_inc(sem(f"{tag}_xn_turned"), 1)


def modulate_tile(act, sem, tag, n, bank, full, scale, shift):
    act.wait_ge(sem(f"{tag}_xn_turned"), n + 3)
    act.wait_ge(sem(f"{tag}_h_split"), n + 1)
    for kt in range(KT):
        last = act.activation(full[:, kt * P:(kt + 1) * P], bank[:, kt * P:(kt + 1) * P], ACT.Identity,
                              bias=shift[:, kt:kt + 1], scale=scale[:, kt:kt + 1])
    last.then_inc(sem(f"{tag}_modulated"), 1)


def split_tile(dve, sem, tag, n, full, high, low):
    view = full.rearrange("p (k t) -> p k t", k=KT)
    dve.wait_ge(sem(f"{tag}_modulated"), n + 3)
    dve.tensor_copy(high, view).then_inc(sem(f"{tag}_h_high"), 1)
    dve.wait_ge(sem(f"{tag}_h_high"), n + 1)
    dve.tensor_tensor(low, view, high, ALU.subtract).then_inc(sem(f"{tag}_h_split"), 1)


def project_stage(nc, sem, sb0, ps, x, w_in, w_out, conv_w, conv_b, dt_bias, a_log, d_skip, norm_w, c, w_mod,
                  xz_dram, ident, upto, after, after_r, ones, neghalf, eps, modrow, modcol, dt, mx, over, steps_at):
    with ExitStack() as st:
        def sb(name, shape, dt=F32):
            return sb0(name, shape, dt, st)

        win_h = sb("win_h", [P, KT, DIN], F32R)
        win_l = sb("win_l", [P, KT, DIN], F32R)
        raw = sb("win_raw", [P, 2, KT, WP])
        hT_h = over("hT_h", [P, 2, KT, TB], steps_at, F32R)
        hT_l = over("hT_l", [P, 2, KT, TB], steps_at + 2 * KT * TB * 4, F32R)
        wm = over("wm", [P, 2, KT, D], mx.wo_h_at)
        xblk = over("xblk", [P, TT, D], mx.wo_l_at)
        xn = over("xn", [P, 2, D], mx.wo_l_at + TT * D * 4)
        hT = over("hT", [P, 2, D], mx.wo_l_at + (TT + 2) * D * 4)
        xraw = sb("xraw", [P, NXBC, TAPS - 1 + TB])
        conv = sb("conv", [P, 2, TB])
        stage = sb("stage", [P, 6, TB])
        dtT = sb("dtT", [P, TB])
        cw = sb("cw", [P, NXBC, TAPS])
        cb = sb("cb", [P, NXBC])
        dtb = sb("dtb", [P, NH])
        ccol = sb("ccol", [P, KT])
        csilu = sb("csilu", [P, KT])
        cwide = over("cwide", [P, KT, P], mx.decays_at)
        nw = sb("nw", [P, CT])
        alog = sb("alog", [P, NH])
        arow = sb("arow", [P, NH])
        NC = NCH * NH
        steps = over("steps", [P, 8, NC], steps_at)
        neg, na, e, t1, d, z, q, ln = (steps[:, k, :] for k in range(8))
        dA = over("dA", [P, NC], steps_at + 2 * KT * TB * 4)[:, :]
        wo_raw = over("wo_raw", [P, 3, D], steps_at + 2 * KT * TB * 4 + NC * 4)
        wo_s = raw[:, :, :, :].rearrange("p s k w -> p s (k w)")[:, :, 0:D]
        idle = sb("idle", [P, 1])
        stats = sb("stats", [P, TT, 6])
        mv = sb("mv", [P, TT, 2])
        rstd = sb("rstd", [P, TT])

        turn_bank = [ps[:, 0, :], ps[:, 1, :]]
        acc_bank = [ps[:, 2 + q, :] for q in range(4)]
        dt_bank = ps[:, 6, :]
        mod_bank = ps[:, 7, :]
        stored = [sem(f"stored{k}") for k in range(6)]

        made = []
        for j in range(NJ):
            if j > NXBC:
                made.append((True, j - 1 - NXBC))
            if 3 <= j < 3 + NXBC:
                made.append((False, j - 3))

        def slot_of(item):
            return made.index(item) % 6

        def turn_of(item):
            return made.index(item) // 6

        with nc.Block() as block:
            @block.sync
            def _(sp):
                for t in stored:
                    sp.sem_inc(t, 16)
                sp.dma_start(ccol[:, :], c).then_inc(sem("c_loaded"), 16)
                for r in range(2):
                    sp.dma_start(wm[:, r, :, :], w_mod[:, :, r * D:(r + 1) * D]).then_inc(sem(f"wm_loaded{r}"), 16)
                for dst, src in ((cw[:, :, :], conv_w), (cb[:, :], conv_b), (dtb[:, :], dt_bias), (alog[:, :], a_log),
                                 (nw[:, :], norm_w), (mx.dskip[0:HD, :], d_skip[0]), (mx.dskip[HD:P, :], d_skip[1])):
                    sp.dma_start(dst, src).then_inc(sem("params_loaded"), 16)
                for i in range(NWP):
                    if i >= 2:
                        sp.wait_ge(sem("win_low"), i - 1)
                    sp.dma_start(raw[:, i % 2, :, :], w_in[:, :, piece(i)])\
                      .then_inc(sem(f"win_loaded{i % 2}"), 16)
                with sp.Fori(0, NB) as b:
                    for item in made:
                        is_z, t = item
                        k = slot_of(item)
                        if is_z:
                            sp.wait_ge(sem("evacuated"), b * NJ + (1 + NXBC + t) + 1 + 3)
                        else:
                            sp.wait_ge(sem("conv_staged"), b * NXBC + t + 1 + 2)
                        tile_at = NXBC + t if is_z else t
                        sp.dma_start(
                            xz_dram[bass.ds(b * TT, TT), :, tile_at, :].rearrange("c p t -> p c t"),
                            stage[:, k, :].rearrange("p (c t) -> p c t", c=TT)).then_inc(stored[k], 16)
                for t in stored:
                    sp.wait_ge(t, 16 + 16 * (NST // 6) * NB)

            @block.gpsimd
            def _(pool):
                pool.memset(ones[:, :], 1.0).then_inc(sem("const_made"), 1)
                pool.memset(neghalf[:, :], -0.5)
                pool.memset(eps[:, :], EPS)
                pool.memset(ident[:, :], 0.0).then_inc(sem("const_made"), 1)
                pool.wait_ge(sem("const_made"), 2)
                pool.affine_select(out=ident[:, :], in_=ident[:, :], compare_op=ALU.not_equal, fill=1.0, base=0,
                                   pattern=[[-1, P]], channel_multiplier=1).then_inc(sem("const_made"), 1)
                pool.affine_select(out=upto[:, :], in_=ones[:, :], compare_op=ALU.is_ge, fill=0.0, base=0,
                                   pattern=[[1, P]], channel_multiplier=-1).then_inc(sem("const_made"), 1)
                pool.affine_select(out=after[:, :], in_=ones[:, :], compare_op=ALU.is_gt, fill=0.0, base=0,
                                   pattern=[[-1, P]], channel_multiplier=1).then_inc(sem("const_made"), 1)

                def load_x(b):
                    pool.wait_ge(sem("p_xn_ready"), b * TT + 1)
                    pool.dma_start(xblk[:, :, :], x[bass.ds(b * TT, TT), :, :].rearrange("t p d -> p t d"))\
                        .then_inc(sem("x_loaded"), 16)

                def load_wm(r):
                    pool.wait_ge(sem("mod_product"), r - 1)
                    pool.dma_start(wm[:, r % 2, :, :], w_mod[:, :, r * D:(r + 1) * D])\
                        .then_inc(sem(f"wm_later{r % 2}"), 16)

                load_x(0)
                inverse_deviation(pool, sem, "p", 0, mv, rstd, neghalf, eps)
                load_x(1)
                inverse_deviation(pool, sem, "p", 1, mv, rstd, neghalf, eps)
                pool.wait_ge(sem("win_low"), NWP - 2)
                load_wm(2)
                load_wm(3)
                load_wm(4)
                load_wm(5)
                with pool.Fori(2, NB) as b:
                    load_x(b)
                    inverse_deviation(pool, sem, "p", b, mv, rstd, neghalf, eps)
                pool.wait_ge(sem("product_ready"), (NB - 1) * NJ + 1)
                for t in range(3):
                    pool.dma_start(wo_raw[:, t, :], w_out[t]).then_inc(sem("wo_first"), 16)
                for t in range(0, CT, 2):
                    pool.wait_ge(sem("wo_high"), t + 1)
                    pool.tensor_tensor(mx.wo_l[:, t, :], wo_s[:, 0, :], mx.wo_h[:, t, :], ALU.subtract)\
                        .then_inc(sem("wo_split_even"), 1)

            @block.vector
            def _(dve):
                dve.sem_inc(sem("p_h_split"), 2)
                dve.sem_inc(sem("p_xn_ready"), 1)
                dve.memset(xraw[:, :, 0:TAPS - 1], 0.0).then_inc(sem("tail_kept"), 1)
                dve.wait_ge(sem("c_silu"), 1)
                dve.tensor_copy(cwide[:, :, :], csilu[:, :].unsqueeze(2).broadcast_to([P, KT, P]))\
                   .then_inc(sem("c_wide"), 1)
                dve.wait_ge(sem("const_made"), 5)
                dve.tensor_copy(after_r[:, :], after[:, :])

                def keep_columns(n, row):
                    dve.wait_ge(sem("mod_turned"), n + 1)
                    src = dt_bank.rearrange("p (k t) -> p k t", k=KT)[:, :, 0]
                    dve.tensor_scalar(modcol[:, n, :], src, 1.0 if row in (1, 4) else 0.0, None, ALU.add)\
                       .then_inc(sem("mod_column"), 1)

                def normalise(b, i):
                    n = b * TT + i
                    normalise_tile(dve, sem, "p", n, i, b, xblk[:, i, :], xn[:, i % 2, :], mv, rstd)

                def statistics(b):
                    dve.wait_ge(sem("x_loaded"), b * 16 + 16)
                    tile_statistics(dve, sem, "p", b, xblk, stats, mv, idle)

                def split(b, i, slot):
                    split_tile(dve, sem, "p", b * TT + i, hT[:, i % 2, :],
                               hT_h[:, slot, :, i * P:(i + 1) * P] if isinstance(slot, int) else
                               hT_h[:, bass.ds(slot, 1), :, i * P:(i + 1) * P].rearrange("p o k t -> p (o k) t"),
                               hT_l[:, slot, :, i * P:(i + 1) * P] if isinstance(slot, int) else
                               hT_l[:, bass.ds(slot, 1), :, i * P:(i + 1) * P].rearrange("p o k t -> p (o k) t"))

                def convolve(b, t):
                    m = b * NXBC + t
                    u = conv[:, t % 2, :]
                    dve.wait_ge(sem("evacuated"), b * NJ + t + 2 + 3)
                    dve.wait_ge(sem("tail_kept"), b + 1)
                    dve.wait_ge(sem("conv_staged"), m + 1)
                    dve.tensor_scalar(u, xraw[:, t, TAPS - 1:TAPS - 1 + TB], cw[:, t, TAPS - 1:TAPS], cb[:, t:t + 1],
                                      ALU.mult, ALU.add).then_inc(sem("conv_step"), 1)
                    for k in range(TAPS - 1):
                        dve.wait_ge(sem("conv_step"), m * TAPS + k + 1)
                        dve.scalar_tensor_tensor(out=u, in0=xraw[:, t, k:k + TB], scalar=cw[:, t, k:k + 1], in1=u,
                                                 op0=ALU.mult, op1=ALU.add).then_inc(sem("conv_step"), 1)

                def keep_tail(b):
                    dve.wait_ge(sem("conv_step"), (b * NXBC + NXBC) * TAPS)
                    dve.tensor_copy(xraw[:, :, 0:TAPS - 1], xraw[:, :, TB:TB + TAPS - 1])\
                       .then_inc(sem("tail_kept"), 1)

                def add_dt_bias(b):
                    dve.wait_ge(sem("dt_turned"), b + 2)
                    dve.tensor_tensor(dt[:, bass.ds(b * TT, TT), :] if not isinstance(b, int) else
                                      dt[:, b * TT:(b + 1) * TT, :],
                                      dt_bank.rearrange("p (t c) -> p t c", t=TT)[:, :, P - NH:P],
                                      dtb[:, :].unsqueeze(1).broadcast_to([P, TT, NH]), ALU.add)\
                       .then_inc(sem("dt_kept"), 1)

                def split_weights(i):
                    dve.wait_ge(sem("win_high"), i + 1)
                    cols = piece(i)
                    dve.tensor_tensor(win_l[:, :, cols], raw[:, i % 2, :, :], win_h[:, :, cols], ALU.subtract)\
                       .then_inc(sem("win_low"), 1)

                link = [0]

                def linked(ins):
                    link[0] += 1
                    ins.then_inc(sem("dve_link"), 1)
                    dve.wait_ge(sem("dve_link"), link[0])

                def set_gate(row):
                    size, sign = modrow[:, 0, :], modrow[:, 3, :]
                    linked(dve.scalar_tensor_tensor(out=size, in0=row, scalar=-1.0, in1=row, op0=ALU.mult, op1=ALU.max))
                    linked(dve.tensor_scalar(sign, row, 0.0, 2.0, ALU.is_ge, ALU.mult))
                    linked(dve.tensor_scalar(sign, sign, -1.0, None, ALU.add))
                    linked(dve.scalar_tensor_tensor(out=row, in0=size, scalar=0.25, in1=sign, op0=ALU.max,
                                                    op1=ALU.mult))

                flat_dt = dt[:, :, :].rearrange("p c h -> p (c h)")

                def softplus_exponent():
                    dve.wait_ge(sem("dt_kept"), NB)
                    linked(dve.tensor_scalar(neg, flat_dt, -1.0, None, ALU.mult))
                    dve.tensor_tensor(na, flat_dt, neg, ALU.min).then_inc(sem("dt_neg"), 1)

                def softplus_ratio():
                    dve.wait_ge(sem("dt_exp"), 1)
                    dve.tensor_scalar(t1, e, 1.0, None, ALU.add).then_inc(sem("dt_one"), 1)
                    dve.wait_ge(sem("dt_one"), 1)
                    linked(dve.tensor_scalar(d, t1, 1.0, None, ALU.subtract))
                    linked(dve.tensor_scalar(z, d, 0.0, None, ALU.is_equal))
                    linked(dve.tensor_tensor(d, d, z, ALU.add))
                    linked(dve.reciprocal(q, d))
                    linked(dve.tensor_tensor(q, q, e, ALU.mult))

                def softplus_end():
                    dve.wait_ge(sem("dt_ln"), 1)
                    linked(dve.tensor_tensor(q, q, ln, ALU.mult))
                    linked(dve.tensor_tensor(z, z, e, ALU.mult))
                    linked(dve.tensor_tensor(q, q, z, ALU.add))
                    linked(dve.scalar_tensor_tensor(out=flat_dt, in0=flat_dt, scalar=0.0, in1=q, op0=ALU.max,
                                                    op1=ALU.add))
                    by_chunk = dA.rearrange("p (c h) -> p c h", h=NH)
                    dve.scalar_tensor_tensor(out=by_chunk, in0=dt[:, :, :], scalar=-1.0,
                                             in1=arow[:, :].unsqueeze(1).broadcast_to([P, NCH, NH]),
                                             op0=ALU.mult, op1=ALU.mult).then_inc(sem("dA_made"), 1)
                    dve.wait_ge(sem("dA_made"), 1)
                    linked(dve.tensor_copy(mx.dA_h[:, :, :], by_chunk))
                    dve.tensor_tensor(mx.dA_l[:, :, :], by_chunk, mx.dA_h[:, :, :], ALU.subtract)

                def weights_out():
                    dve.wait_ge(sem("mod_product"), 6)
                    dve.wait_ge(sem("p_xn_turned"), NB * TT + 2)
                    dve.wait_ge(sem("p_h_split"), NB * TT + 2)
                    for t in range(CT):
                        if t < 3:
                            dve.wait_ge(sem("wo_first"), 48)
                        else:
                            dve.wait_ge(sem(f"wo_loaded{t % 3}"), 16 * (t // 3))
                        if t >= 2:
                            dve.wait_ge(sem(("wo_split_even", "wo_split_odd")[t % 2]), t // 2)
                        dve.scalar_tensor_tensor(out=wo_s[:, t % 2, :], in0=wo_raw[:, t % 3, :],
                                                 scalar=nw[:, t:t + 1], in1=modrow[:, 2, :],
                                                 op0=ALU.mult, op1=ALU.mult).then_inc(sem("wo_scaled"), 1)
                        if t % 2 == 0 and t >= 2:
                            low_odd(t - 1)
                    low_odd(CT - 1)

                def low_odd(t):
                    dve.wait_ge(sem("wo_high"), t + 1)
                    dve.tensor_tensor(mx.wo_l[:, t, :], wo_s[:, 1, :], mx.wo_h[:, t, :], ALU.subtract)\
                       .then_inc(sem("wo_split_odd"), 1)

                def block_body(b, has_next, slot):
                    for t in range(NXBC):
                        if has_next and t == 0:
                            statistics(b + 1)
                        if has_next and t in (1, 3, 6, 8):
                            normalise(b + 1, (1, 3, 6, 8).index(t))
                        if isinstance(b, int) and b == 0 and t < NWP - TT:
                            split_weights(TT + t)
                        convolve(b, t)
                        if t == 2:
                            add_dt_bias(b)
                        if has_next and t in (5, 8, 9):
                            split(b + 1, (5, 8, 9).index(t), slot)
                        if not has_next and t in (3, 5, 7):
                            (softplus_exponent, softplus_ratio, softplus_end)[(3, 5, 7).index(t)]()
                    keep_tail(b)
                    if has_next:
                        split(b + 1, 3, slot)

                statistics(0)
                keep_columns(0, 0)
                normalise(0, 0)
                keep_columns(1, 1)
                normalise(0, 1)
                for i in range(TT):
                    split(0, i, 0)
                    if i + 2 < TT:
                        normalise(0, i + 2)
                    if i == 1:
                        split_weights(0)
                for i in range(1, TT):
                    split_weights(i)
                dve.wait_ge(sem("params_loaded"), 7 * 16)
                block_body(0, True, 1)
                keep_columns(2, 3)
                dve.wait_ge(sem("mod_row"), 6)
                set_gate(modrow[:, 2, :])
                keep_columns(3, 4)
                set_gate(modrow[:, 5, :])
                with dve.Fori(1, NB - 1) as b:
                    block_body(b, True, (b + 1) % 2)
                block_body(NB - 1, False, None)
                weights_out()

            @block.scalar
            def _(act):
                act.sem_inc(sem("p_modulated"), 2)
                act.sem_inc(sem("evacuated"), 3)
                act.sem_inc(sem("conv_staged"), 2)
                act.wait_ge(sem("c_loaded"), 16)
                act.activation(csilu[:, :], ccol[:, :], ACT.Silu).then_inc(sem("c_silu"), 1)

                def keep_row(r):
                    act.wait_ge(sem("mod_product"), r + 1)
                    act.activation(modrow[:, r, :], acc_bank[0] if r == 1 else mod_bank, ACT.Copy).then_inc(sem("mod_row"), 1)

                def round_weights(i):
                    act.wait_ge(sem(f"win_loaded{i % 2}"), 16 * (i // 2) + 16)
                    act.activation(win_h[:, :, piece(i)], raw[:, i % 2, :, :], ACT.Copy)\
                       .then_inc(sem("win_high"), 1)

                def modulate(b, i):
                    modulate_tile(act, sem, "p", b * TT + i, turn_bank[i % 2], hT[:, i % 2, :],
                                  modcol[:, 1, :], modcol[:, 0, :])

                def evacuate(b, j):
                    act.wait_ge(sem("product_ready"), b * NJ + j + 1)
                    if j == 0:
                        act.wait_ge(sem("dt_turned"), b + 1)
                        act.activation(dtT[:, :], acc_bank[0], ACT.Copy).then_inc(sem("evacuated"), 1)
                    elif j <= NXBC:
                        act.wait_ge(sem("tail_kept"), b + 1)
                        act.activation(xraw[:, j - 1, TAPS - 1:TAPS - 1 + TB], acc_bank[j % 4], ACT.Copy)\
                           .then_inc(sem("evacuated"), 1)
                    else:
                        item = (True, j - 1 - NXBC)
                        act.wait_ge(stored[slot_of(item)], b * 48 + 16 * turn_of(item) + 16)
                        act.activation(stage[:, slot_of(item), :], acc_bank[j % 4], ACT.Silu)\
                           .then_inc(sem("evacuated"), 1)

                def activate(b, t):
                    item = (False, t)
                    act.wait_ge(sem("conv_step"), (b * NXBC + t + 1) * TAPS)
                    act.wait_ge(stored[slot_of(item)], b * 48 + 16 * turn_of(item) + 16)
                    act.activation(stage[:, slot_of(item), :], conv[:, t % 2, :], ACT.Silu)\
                       .then_inc(sem("conv_staged"), 1)

                def block_body(b, has_next):
                    turns = [j + 2 for j in (4, 7, 10, 13)] if isinstance(b, int) else (4, 7, 10, 13)
                    for j in range(NJ):
                        evacuate(b, j)
                        if 3 <= j < 3 + NXBC:
                            activate(b, j - 3)
                        if has_next and j in turns:
                            modulate(b + 1, turns.index(j))
                        if isinstance(b, int) and b == 0:
                            if j < NWP - TT:
                                round_weights(TT + j)
                            if j in (10, 12, 16, 18):
                                keep_row(2 + (10, 12, 16, 18).index(j))
                        if not has_next and j == 7:
                            act.activation(arow[:, :], alog[:, :], ACT.Exp)
                            act.wait_ge(sem("dt_neg"), 1)
                            act.activation(e, na, ACT.Exp).then_inc(sem("dt_exp"), 1)
                        if not has_next and j >= 15:
                            for t in ((j - 15) * 2, (j - 15) * 2 + 1):
                                act.wait_ge(sem("wo_scaled"), t + 1)
                                act.activation(mx.wo_h[:, t, :], wo_s[:, t % 2, :], ACT.Copy)\
                                   .then_inc(sem("wo_high"), 1)
                                if t + 3 < CT:
                                    act.dma_start(wo_raw[:, t % 3, :], w_out[t + 3])\
                                       .then_inc(sem(f"wo_loaded{t % 3}"), 16)
                        if not has_next and j == 9:
                            act.wait_ge(sem("dt_one"), 1)
                            act.activation(ln, t1, ACT.Ln).then_inc(sem("dt_ln"), 1)
                    if not has_next:
                        act.wait_ge(sem("decay_sums"), 1)
                        for dst, src in ((mx.grown.rearrange("p c h -> p (c h)"), turn_bank[0][:, 0:NC]),
                                         (mx.left[:, :, :].rearrange("p c h -> p (c h)"), turn_bank[0][:, NC:2 * NC]),
                                         (mx.whole.rearrange("p c h -> p (c h)"), turn_bank[1][:, 0:NC])):
                            act.activation(dst, src, ACT.Exp)

                keep_row(0)
                keep_row(1)
                act.wait_ge(sem("mod_column"), 2)
                for i in range(TT):
                    modulate(0, i)
                    if i == 1:
                        round_weights(0)
                for i in range(1, TT):
                    round_weights(i)
                block_body(0, True)
                with act.Fori(1, NB - 1) as b:
                    block_body(b, True)
                block_body(NB - 1, False)

            @block.tensor
            def _(pe):
                pe.sem_inc(sem("p_xn_turned"), 2)
                pe.sem_inc(sem("dt_turned"), 1)

                def mod_row(r):
                    bank = acc_bank[0] if r == 1 else mod_bank
                    if r >= 2:
                        pe.wait_ge(sem("mod_row"), r)
                    if r < 2:
                        pe.wait_ge(sem(f"wm_loaded{r}"), 16)
                    else:
                        pe.wait_ge(sem(f"wm_later{r % 2}"), 16 * (r // 2))
                    for kt in range(KT):
                        last = pe.matmul(bank, cwide[:, kt, :], wm[:, r % 2, kt, :], start=(kt == 0),
                                         stop=(kt == KT - 1))
                    last.then_inc(sem("mod_product"), 1)

                def turn_row(n, row):
                    pe.wait_ge(sem("mod_row"), row + 1)
                    if n >= 1:
                        pe.wait_ge(sem("mod_column"), n)
                    for kt in range(KT):
                        last = pe.transpose(dt_bank[:, kt * P:(kt + 1) * P], modrow[:, row, kt * P:(kt + 1) * P],
                                            ident[:, :])
                    last.then_inc(sem("mod_turned"), 1)

                def turn(b, i):
                    turn_tile(pe, sem, "p", b * TT + i, xn[:, i % 2, :], turn_bank[i % 2], ident)

                def project(b, j, slot, first):
                    n = b * NJ + j
                    c0 = column_of(j)
                    pe.wait_ge(sem("evacuated"), n + 1)
                    if first:
                        pe.wait_ge(sem("win_low"), pieces_until(c0))
                    if j == 0:
                        pe.wait_ge(sem("p_h_split"), b * TT + TT + 2)
                    rhs = []
                    for kt in range(KT):
                        if isinstance(slot, int):
                            rhs.append((hT_h[:, slot, kt, :], hT_l[:, slot, kt, :]))
                        else:
                            rhs.append(tuple(h[:, bass.ds(slot, 1), kt, :].rearrange("p o t -> p (o t)")
                                             for h in (hT_h, hT_l)))
                    three_pass(pe, acc_bank[j % 4],
                               [(win_h[:, kt, c0:c0 + P], win_l[:, kt, c0:c0 + P], *rhs[kt]) for kt in range(KT)])\
                        .then_inc(sem("product_ready"), 1)

                def turn_dt(b):
                    pe.wait_ge(sem("evacuated"), b * NJ + 1 + 3)
                    if isinstance(b, int) and b == 0:
                        pe.wait_ge(sem("mod_column"), 2)
                    else:
                        pe.wait_ge(sem("dt_kept"), b)
                        pe.wait_ge(sem("mod_column"), 4)
                    for i in range(TT):
                        last = pe.transpose(dt_bank[:, i * P:(i + 1) * P], dtT[:, i * P:(i + 1) * P], ident[:, :])
                    last.then_inc(sem("dt_turned"), 1)

                def block_body(b, has_next, slot, first=False):
                    turns = [j + 2 for j in (3, 6, 9, 12)] if first else (3, 6, 9, 12)
                    for j in range(NJ):
                        project(b, j, slot, first)
                        if j == 2:
                            turn_dt(b)
                        if has_next and j in turns:
                            turn(b + 1, turns.index(j))
                        if first:
                            if j in (9, 11, 15, 17):
                                mod_row(2 + (9, 11, 15, 17).index(j))
                            if j == 13:
                                pe.wait_ge(sem("dt_kept"), 1)
                                turn_row(2, 3)
                        if not has_next and j == 14:
                            pe.wait_ge(sem("dA_made"), 1)
                            pe.matmul(turn_bank[0][:, 0:NC], upto[:, :], dA, start=True, stop=True)
                            pe.matmul(turn_bank[0][:, NC:2 * NC], after[:, :], dA, start=True, stop=True)
                            pe.matmul(turn_bank[1][:, 0:NC], ones[:, :], dA, start=True, stop=True)\
                              .then_inc(sem("decay_sums"), 1)
                    if first:
                        turn_row(3, 4)

                pe.wait_ge(sem("c_wide"), 1)
                mod_row(0)
                mod_row(1)
                pe.wait_ge(sem("const_made"), 5)
                turn_row(0, 0)
                turn_row(1, 1)
                for i in range(TT):
                    turn(0, i)
                block_body(0, True, 0, first=True)
                with pe.Fori(1, NB - 1) as b:
                    block_body(b, True, b % 2)
                block_body(NB - 1, False, (NB - 1) % 2)


def load_g(pool, sem, h, g, gT_dram, gT_h, gT_l):
    tiles = slice(g * TT, (g + 1) * TT)
    rows = slice(h * HT + g * TT, h * HT + (g + 1) * TT)
    for part, dst in ((0, gT_h), (1, gT_l)):
        pool.dma_start(dst[:, tiles, :, :].rearrange("p t k q -> p t (k q)"),
                       gT_dram[part, rows, :, :].rearrange("t p n -> p t n")).then_inc(sem(f"g_loaded{g}"), 16)


def scan_stage(nc, sem, sb0, ps, x, xz_dram, x1_dram, gT_dram, ident, upto, after_r, ones, neghalf, eps,
               modcol, dt, mx, gT_h, gT_l, raw, w_gu):
    with ExitStack() as st:
        def sb(name, shape, dt=F32):
            return sb0(name, shape, dt, st)

        step_h = sb("step_h", [P, NH, P], F32R)
        step_l = sb("step_l", [P, NH, P], F32R)
        xz = sb("xz", [P, 2, NST, P])
        xres = sb("xres", [P, 2, D])
        M = sb("M", [P, 2, NH, P])
        cbm = sb("cbm", [P, P])
        btok = sb("btok", [P, P])
        xdt = sb("xdt", [P, 2, DI])
        xdl = sb("xdl", [P, DI])
        state = sb("state", [P, DI])
        faded = sb("faded", [P, DI])
        yoff = sb("yoff", [P, DI])
        dx = sb("dx", [P, CT, P])
        y = sb("y", [P, CT, P])
        y_h = sb("y_h", [P, CT, P], F32R)
        y_l = sb("y_l", [P, CT, P], F32R)
        ysq = sb("ysq", [P, CT, P])
        ysum = sb("ysum", [P, P])
        rms = sb("rms", [P, 1])
        x1 = sb("x1", [P, 2, D])
        idle = sb("idle_s", [P, 1])
        stats = sb("stats_s", [P, 6])
        mv = sb("mv_s", [P, 2, 2])
        rstd = sb("rstd_s", [P, 2])
        xn = sb("xn_s", [P, D])
        g = sb("g", [P, D])
        g_h = sb("g_h", [P, 2, D], F32R)
        g_l = sb("g_l", [P, 2, D], F32R)

        seg_bank = [ps[:, 0, :], ps[:, 1, :]]
        pair = ps[:, 2:4, :]
        pair_flat = pair.rearrange("p a b -> p (a b)")
        y_pair = ps[:, 4:6, :]
        y_flat = y_pair.rearrange("p a b -> p (a b)")
        out_bank = ps[:, 6, :]
        cb_ps = ps[:, 7, 0:P]
        bt_ps = ps[:, 7, P:2 * P]
        ss_ps = ps[:, 7, 2 * P:2 * P + 1]
        x_view = x.rearrange("t p d -> t p d")

        with nc.Block() as block:
            def load_xbc(eng, c, r):
                eng.dma_start(xz[:, r, 0:NXBC, :], one(xz_dram, c, 0, NXBC)).then_inc(sem(f"xbc_loaded{r}"), 16)

            def load_z(eng, c, r):
                eng.dma_start(xz[:, r, NXBC:NST, :], one(xz_dram, c, NXBC, NST)).then_inc(sem(f"z_loaded{r}"), 16)

            def load_x(eng, c, r):
                eng.dma_start(xres[:, r, :], one(x_view, c)).then_inc(sem(f"xres_loaded{r}"), 16)

            def turn(c, r):
                return c // 2 if isinstance(c, int) else (c - r) // 2

            def one(ap, c, lo=0, hi=None):
                if isinstance(c, int):
                    return ap[c] if hi is None else ap[c, :, lo:hi, :]
                if hi is not None:
                    return ap[bass.ds(c, 1), :, lo:hi, :].rearrange("o p a b -> p (o a) b")
                return ap[bass.ds(c, 1), :, :].rearrange("o p a -> p (o a)")

            def chunk_cols(ap, c):
                if isinstance(c, int):
                    return ap[:, c, :]
                return ap[:, bass.ds(c, 1), :].rearrange("p o h -> p (o h)")

            def by_head(ap, width):
                return ap.unsqueeze(2).broadcast_to([P, NH, width])

            def over_chunks(eng, body):
                body(0, 0, False, False, True)
                body(1, 1, True, False, True)
                with eng.Fori(0, NCH // 2 - 2) as i:
                    body(i * 2 + 2, 0, True, True, True)
                    body(i * 2 + 3, 1, True, True, True)
                body(NCH - 2, 0, True, True, True)
                body(NCH - 1, 1, True, True, False)

            @block.sync
            def _(sp):
                sp.sem_inc(sem("x1_stored0"), 16)
                sp.sem_inc(sem("x1_stored1"), 16)
                sp.sem_inc(sem("g_stored0"), 32)
                sp.sem_inc(sem("g_stored1"), 32)
                for c_ in range(2):
                    load_xbc(sp, c_, c_)
                    load_z(sp, c_, c_)
                    load_x(sp, c_, c_)

                def store_g(c, r):
                    sp.wait_ge(sem("g_low"), c + 1)
                    sp.dma_start(one(gT_dram[0], c), g_h[:, r, :].bitcast(F32)).then_inc(sem(f"g_stored{r}"), 16)
                    sp.dma_start(one(gT_dram[1], c), g_l[:, r, :].bitcast(F32)).then_inc(sem(f"g_stored{r}"), 16)

                def store_x1(c, r):
                    sp.wait_ge(sem("x1_made"), c + 1)
                    sp.dma_start(one(x1_dram, c), x1[:, r, :]).then_inc(sem(f"x1_stored{r}"), 16)

                def body(c, r, prev, prev2, nxt, second=True):
                    if second:
                        sp.wait_ge(sem("off_ready"), c + 1)
                        sp.wait_ge(sem("dx_made"), c + 1)
                        load_xbc(sp, c + 2, r)
                    if prev:
                        store_x1(c - 1, 1 - r)
                        if nxt:
                            load_x(sp, c + 1, 1 - r)
                    if prev2:
                        store_g(c - 2, r)
                    if second:
                        sp.wait_ge(sem("gated"), c + 1)
                        load_z(sp, c + 2, r)

                body(0, 0, False, False, True)
                body(1, 1, True, False, True)
                with sp.Fori(0, NCH // 2 - 2) as i:
                    body(i * 2 + 2, 0, True, True, True)
                    body(i * 2 + 3, 1, True, True, True)
                body(NCH - 2, 0, True, True, True, False)
                body(NCH - 1, 1, True, True, False, False)
                sp.wait_ge(sem("seg_read"), NCH * 4)
                for p in range(RING):
                    sp.dma_start(raw[:, p, :], w_gu[0, p]).then_inc(sem(f"piece_loaded{p}"), 16)
                store_x1(NCH - 1, 1)
                store_g(NCH - 2, 0)
                store_g(NCH - 1, 1)

            @block.gpsimd
            def _(pool):

                def skip_part(c, r):
                    pool.wait_ge(sem(f"xbc_loaded{r}"), turn(c, r) * 16 + 16)
                    pool.tensor_tensor(dx[:, :, :], xz[:, r, 0:CT, :], mx.dskip[:, :].unsqueeze(2).broadcast_to([P, CT, P]),
                                       ALU.mult).then_inc(sem("dx_made"), 1)

                def high_steps(c):
                    pool.tensor_tensor(step_h[:, :, :], upto[:, :].unsqueeze(1).broadcast_to([P, NH, P]),
                                       by_head(chunk_cols(mx.dA_h, c), P), ALU.mult).then_inc(sem("step_high"), 1)

                def low_steps(c):
                    pool.tensor_tensor(step_l[:, :, :], upto[:, :].unsqueeze(1).broadcast_to([P, NH, P]),
                                       by_head(chunk_cols(mx.dA_l, c), P), ALU.mult).then_inc(sem("step_low"), 1)

                def invert(c, r):
                    pool.wait_ge(sem("x1_step"), c * 2 + 2)
                    pool.tensor_tensor(rstd[:, r:r + 1], mv[:, r, 1:2], eps[:, 0:1], ALU.add)\
                        .then_inc(sem("x1_rstd"), 1)
                    pool.wait_ge(sem("x1_rstd"), c * 2 + 1)
                    pool.tensor_tensor(rstd[:, r:r + 1], rstd[:, r:r + 1], neghalf[:, 0:1], ALU.pow)\
                        .then_inc(sem("x1_rstd"), 1)

                def invert_rms(c):
                    pool.wait_ge(sem("rms_step"), c + 1)
                    pool.tensor_tensor(rms[:, :], rms[:, :], neghalf[:, 0:1], ALU.pow)\
                        .then_inc(sem("rms_inverted"), 1)

                def weigh_left(c, r):
                    pool.wait_ge(sem("x_weighed"), c + 1)
                    if not (isinstance(c, int) and c == 0):
                        pool.wait_ge(sem("states_ready"), c)
                    pool.tensor_tensor(xdl[:, :].rearrange("p (h d) -> p h d", h=NH),
                                       xdt[:, r, :].rearrange("p (h d) -> p h d", h=NH),
                                       by_head(chunk_cols(mx.left, c), HD), ALU.mult).then_inc(sem("left_weighed"), 1)

                def fade(c):
                    pool.wait_ge(sem("state_made"), c + 1)
                    pool.tensor_tensor(faded[:, :].rearrange("p (h d) -> p h d", h=NH),
                                       state[:, :].rearrange("p (h d) -> p h d", h=NH),
                                       by_head(chunk_cols(mx.whole, c), HD), ALU.mult).then_inc(sem("state_faded"), 1)

                def body(c, r, prev, prev2, nxt):
                    further = nxt and not (isinstance(c, int) and c == NCH - 2)
                    if further:
                        pool.wait_ge(sem("seg_read"), (c + 2) * 4)
                        high_steps(c + 2)
                    if prev:
                        invert_rms(c - 1)
                    if further:
                        low_steps(c + 2)
                    if prev:
                        invert(c - 1, 1 - r)
                    if nxt:
                        fade(c + 1)
                        weigh_left(c + 1, 1 - r)
                    if isinstance(c, int) and c == NCH - 2:
                        for k in range(2):
                            pool.wait_ge(sem(f"g_stored{k}"), 32 + 32 * (NCH // 4))
                        for k in range(2):
                            load_g(pool, sem, 0, k, gT_dram, gT_h, gT_l)
                    if nxt:
                        pool.wait_ge(sem("gated"), c + 1)
                        skip_part(c + 1, 1 - r)

                for half in range(2):
                    heads = slice(half * NH // 2, (half + 1) * NH // 2)
                    pool.tensor_tensor(step_l[:, heads, :], upto[:, :].unsqueeze(1).broadcast_to([P, NH // 2, P]),
                                       mx.dA_l[:, 0, heads].unsqueeze(2).broadcast_to([P, NH // 2, P]), ALU.mult)\
                        .then_inc(sem(("first_low", "step_low")[half]), 1)
                pool.wait_ge(sem("seg_read"), 4)
                low_steps(1)
                weigh_left(0, 0)
                skip_part(0, 0)
                fade(0)
                over_chunks(pool, body)
                invert_rms(NCH - 1)
                invert(NCH - 1, 1)

            @block.vector
            def _(dve):
                def first_steps(c):
                    dve.tensor_tensor(step_h[:, :, :], upto[:, :].unsqueeze(1).broadcast_to([P, NH, P]),
                                      by_head(mx.dA_h[:, c, :], P), ALU.mult).then_inc(sem("step_high"), 1)

                def mask_cb(c):
                    dve.wait_ge(sem("cb_ready"), c + 1)
                    if not (isinstance(c, int) and c == 0):
                        dve.wait_ge(sem("M_ready"), c * 4)
                    dve.tensor_tensor(cbm[:, :], cb_ps, upto[:, :], ALU.mult).then_inc(sem("cb_masked"), 1)

                def mask_decay(c, r, groups):
                    dve.wait_ge(sem("cb_masked"), c + 1)
                    for g in groups:
                        dve.wait_ge(sem("seg_exp"), c * 4 + g + 1)
                        m = M[:, r, 4 * g:4 * g + 4, :]
                        dve.tensor_tensor(m, m, cbm[:, :].unsqueeze(1).broadcast_to([P, 4, P]), ALU.mult)\
                           .then_inc(sem("M_ready"), 1)

                def weigh_x(c, r):
                    dve.wait_ge(sem("x_turned"), c + 1)
                    dve.tensor_tensor(xdt[:, r, :].rearrange("p (h d) -> p h d", h=NH),
                                      pair_flat.rearrange("p (h d) -> p h d", h=NH),
                                      by_head(chunk_cols(dt, c), HD), ALU.mult).then_inc(sem("x_weighed"), 1)

                def body(c, r, prev, prev2, nxt):
                    dve.wait_ge(sem("off_ready"), c + 1)
                    dve.tensor_tensor(yoff[:, :].rearrange("p (h d) -> p h d", h=NH),
                                      pair_flat.rearrange("p (h d) -> p h d", h=NH),
                                      by_head(chunk_cols(mx.grown, c), HD), ALU.mult).then_inc(sem("off_scaled"), 1)
                    if prev:
                        low_y(c - 1)
                    if nxt:
                        mask_cb(c + 1)
                        mask_decay(c + 1, 1 - r, (0, 1))
                    if prev:
                        sum_squares(c - 1)
                    if nxt:
                        mask_decay(c + 1, 1 - r, (2, 3))
                    dve.wait_ge(sem("states_ready"), c + 1)
                    dve.wait_ge(sem("state_faded"), c + 1)
                    dve.tensor_tensor(state[:, :], faded[:, :], pair_flat, ALU.add).then_inc(sem("state_made"), 1)
                    if prev:
                        mean_square(c - 1)
                    if prev2:
                        split_g(c - 2, r)
                    if nxt:
                        weigh_x(c + 1, 1 - r)
                    if prev:
                        finish(c - 1, 1 - r)
                        deviation(c - 1, 1 - r)
                    gate_y(c, r, prev)

                def gate_y(c, r, prev):
                    for half in range(2):
                        tiles = slice(half * CT // 2, (half + 1) * CT // 2)
                        part = dx[:, tiles, :]
                        dve.wait_ge(sem("y_summed"), c * 2 + half + 1)
                        dve.wait_ge(sem("dx_made"), c + 1)
                        dve.tensor_tensor(part.rearrange("p t l -> p (t l)"), y_pair[:, half, :],
                                          part.rearrange("p t l -> p (t l)"), ALU.add).then_inc(sem("skip_added"), 1)
                        dve.wait_ge(sem("skip_added"), c * 2 + half + 1)
                        if half == 0:
                            if prev:
                                dve.wait_ge(sem("y_squared"), c)
                                dve.wait_ge(sem("y_low"), c)
                            dve.wait_ge(sem(f"z_loaded{r}"), turn(c, r) * 16 + 16)
                        ins = dve.tensor_tensor(y[:, tiles, :], part, xz[:, r, NXBC + tiles.start:NXBC + tiles.stop, :],
                                                ALU.mult)
                        if half == 0 and prev:
                            centre(c - 1, 1 - r)
                    ins.then_inc(sem("gated"), 1)

                def low_y(c):
                    dve.wait_ge(sem("y_high"), c + 1)
                    dve.tensor_tensor(y_l[:, :, :], y[:, :, :], y_h[:, :, :], ALU.subtract).then_inc(sem("y_low"), 1)

                def sum_squares(c):
                    dve.wait_ge(sem("y_squared"), c + 1)
                    dve.tensor_reduce(ysum[:, :], ysq[:, :, :].rearrange("p t l -> p l t"), AX.X, ALU.add)\
                       .then_inc(sem("squares_summed"), 1)

                def mean_square(c):
                    dve.wait_ge(sem("rms_ready"), c + 1)
                    if not (isinstance(c, int) and c == 0):
                        dve.wait_ge(sem("x1_made"), c)
                    dve.tensor_scalar(rms[:, :], ss_ps, 1.0 / DI, EPS, ALU.mult, ALU.add)\
                       .then_inc(sem("rms_step"), 1)

                def deviation(c, r):
                    dve.wait_ge(sem("x1_made"), c + 1)
                    dve.bn_stats(stats[:, :], x1[:, r, :]).then_inc(sem("x1_step"), 1)
                    dve.wait_ge(sem("x1_step"), c * 2 + 1)
                    dve.memset(idle[:, :], 0.0)
                    dve.bn_aggr(mv[:, r, :], stats[:, :]).then_inc(sem("x1_step"), 1)

                def centre(c, r):
                    dve.wait_ge(sem("x1_rstd"), c * 2 + 2)
                    dve.tensor_scalar(xn[:, :], x1[:, r, :], mv[:, r, 0:1], rstd[:, r:r + 1],
                                      ALU.subtract, ALU.mult).then_inc(sem("x1_centred"), 1)

                def split_g(c, r):
                    dve.wait_ge(sem("g_high"), c + 1)
                    dve.tensor_tensor(g_l[:, r, :], g[:, :], g_h[:, r, :], ALU.subtract).then_inc(sem("g_low"), 1)

                def finish(c, r):
                    dve.wait_ge(sem("out_ready"), c + 1)
                    dve.wait_ge(sem("rms_inverted"), c + 1)
                    k = turn(c, r)
                    dve.wait_ge(sem(f"xres_loaded{r}"), k * 16 + 16)
                    dve.wait_ge(sem(f"x1_stored{r}"), k * 16 + 16)
                    dve.scalar_tensor_tensor(out=x1[:, r, :], in0=out_bank, scalar=rms[:, 0:1], in1=xres[:, r, :],
                                             op0=ALU.mult, op1=ALU.add).then_inc(sem("x1_made"), 1)

                first_steps(0)
                dve.memset(state[:, :], 0.0).then_inc(sem("state_made"), 1)
                mask_cb(0)
                weigh_x(0, 0)
                dve.wait_ge(sem("seg_read"), 4)
                first_steps(1)
                mask_decay(0, 0, range(4))
                over_chunks(dve, body)
                low_y(NCH - 1)
                sum_squares(NCH - 1)
                mean_square(NCH - 1)
                split_g(NCH - 2, 0)
                finish(NCH - 1, 1)
                deviation(NCH - 1, 1)
                centre(NCH - 1, 1)
                split_g(NCH - 1, 1)

            @block.scalar
            def _(act):
                def decay(c, r, groups):
                    for g in groups:
                        act.wait_ge(sem("seg_read"), c * 4 + g + 1)
                        act.activation(M[:, r, 4 * g:4 * g + 4, :].rearrange("p h l -> p (h l)"), seg_bank[g % 2],
                                       ACT.Exp).then_inc(sem("seg_exp"), 1)

                def keep_b(c):
                    act.wait_ge(sem("b_turned"), c + 1)
                    act.activation(btok[:, :], bt_ps, ACT.Copy).then_inc(sem("b_kept"), 1)

                def modulate_g(c, r):
                    act.wait_ge(sem("x1_turned"), c + 1)
                    if not (isinstance(c, int) and c == 0):
                        act.wait_ge(sem("g_low"), c)
                    for kt in range(KT):
                        last = act.activation(g[:, kt * P:(kt + 1) * P], out_bank[:, kt * P:(kt + 1) * P],
                                              ACT.Identity, bias=modcol[:, 2, kt:kt + 1], scale=modcol[:, 3, kt:kt + 1])
                    last.then_inc(sem("g_made"), 1)

                def high_g(c, r):
                    act.wait_ge(sem("g_made"), c + 1)
                    act.wait_ge(sem(f"g_stored{r}"), turn(c, r) * 32 + 32)
                    act.activation(g_h[:, r, :], g[:, :], ACT.Copy).then_inc(sem("g_high"), 1)

                def high_y(c):
                    act.wait_ge(sem("gated"), c + 1)
                    if not (isinstance(c, int) and c == 0):
                        act.wait_ge(sem("out_ready"), c)
                    act.activation(y_h[:, :, :], y[:, :, :], ACT.Copy).then_inc(sem("y_high"), 1)

                def square_y(c):
                    if not (isinstance(c, int) and c == 0):
                        act.wait_ge(sem("squares_summed"), c)
                    act.activation(ysq[:, :, :], y[:, :, :], ACT.Square).then_inc(sem("y_squared"), 1)

                def body(c, r, prev, prev2, nxt):
                    if prev:
                        high_y(c - 1)
                    if nxt:
                        decay(c + 1, 1 - r, (0, 1))
                    if prev2:
                        modulate_g(c - 2, r)
                    if prev:
                        square_y(c - 1)
                    if nxt:
                        decay(c + 1, 1 - r, (2, 3))
                    if prev2:
                        high_g(c - 2, r)
                    if nxt:
                        keep_b(c + 1)

                decay(0, 0, range(4))
                keep_b(0)
                over_chunks(act, body)
                high_y(NCH - 1)
                square_y(NCH - 1)
                modulate_g(NCH - 2, 0)
                high_g(NCH - 2, 0)
                modulate_g(NCH - 1, 1)
                high_g(NCH - 1, 1)

            @block.tensor
            def _(pe):
                def cb(c, r):
                    pe.wait_ge(sem(f"xbc_loaded{r}"), turn(c, r) * 16 + 16)
                    pe.matmul(cb_ps, xz[:, r, CT, :], xz[:, r, CT + 1, :], start=True, stop=True)\
                      .then_inc(sem("cb_ready"), 1)

                def segments(c, groups, first=False):
                    pe.wait_ge(sem("step_high"), c + 1)
                    pe.wait_ge(sem("first_low" if first else "step_low"), c + 1)
                    for g in groups:
                        if first:
                            if g == 2:
                                pe.wait_ge(sem("step_low"), c + 1)
                            if g >= 2:
                                pe.wait_ge(sem("seg_exp"), g - 1)
                        else:
                            pe.wait_ge(sem("seg_exp"), c * 4 + g - 1)
                        pe.matmul(seg_bank[g % 2], after_r[:, :],
                                  step_h[:, 4 * g:4 * g + 4, :].rearrange("p h l -> p (h l)"), start=True, stop=False)
                        pe.matmul(seg_bank[g % 2], after_r[:, :],
                                  step_l[:, 4 * g:4 * g + 4, :].rearrange("p h l -> p (h l)"), start=False, stop=True)\
                          .then_inc(sem("seg_read"), 1)

                def turn_x(c, r, first=False):
                    if not first:
                        pe.wait_ge(sem("state_made"), c + 1)
                    for t in range(CT):
                        last = pe.transpose(pair_flat[:, t * P:(t + 1) * P], xz[:, r, t, :], ident[:, :])
                    last.then_inc(sem("x_turned"), 1)

                def turn_b(c, r):
                    pe.wait_ge(sem("cb_masked"), c + 1)
                    if not (isinstance(c, int) and c <= 1):
                        pe.wait_ge(sem("rms_step"), c - 1)
                    pe.transpose(bt_ps, xz[:, r, CT, :], ident[:, :]).then_inc(sem("b_turned"), 1)

                def project_out(c, r, nxt):
                    pe.wait_ge(sem("y_low"), c + 1)
                    parts = [(y_h[:, t, :], y_l[:, t, :], mx.wo_h[:, t, :], mx.wo_l[:, t, :]) for t in range(CT)]
                    three_pass(pe, out_bank, parts[:6], stop=False)
                    pe.wait_ge(sem("squares_summed"), c + 1)
                    pe.matmul(ss_ps, ysum[:, :], ones[:, 0:1], start=True, stop=True).then_inc(sem("rms_ready"), 1)
                    if nxt:
                        turn_x(c + 2, r)
                    three_pass(pe, out_bank, parts[6:], start=False).then_inc(sem("out_ready"), 1)

                def turn_x1(c, r):
                    pe.wait_ge(sem("x1_centred"), c + 1)
                    for kt in range(KT):
                        last = pe.transpose(out_bank[:, kt * P:(kt + 1) * P], xn[:, kt * P:(kt + 1) * P], ident[:, :])
                    last.then_inc(sem("x1_turned"), 1)

                def body(c, r, prev, prev2, nxt):
                    pe.wait_ge(sem("x_weighed"), c + 1)
                    pe.wait_ge(sem("state_made"), c + 1)
                    for n in range(2):
                        last = pe.matmul(pair[:, n, :], xz[:, r, CT + 1, :], state[:, n * 512:(n + 1) * 512],
                                         start=True, stop=True)
                    last.then_inc(sem("off_ready"), 1)
                    if prev2:
                        turn_x1(c - 2, r)
                    if nxt:
                        segments(c + 1, (0, 1))
                    pe.wait_ge(sem("b_kept"), c + 1)
                    if nxt:
                        cb(c + 1, 1 - r)
                    pe.wait_ge(sem("off_scaled"), c + 1)
                    pe.wait_ge(sem("left_weighed"), c + 1)
                    for n in range(2):
                        last = pe.matmul(pair[:, n, :], btok[:, :], xdl[:, n * 512:(n + 1) * 512], start=True, stop=True)
                    last.then_inc(sem("states_ready"), 1)
                    if nxt:
                        segments(c + 1, (2, 3))
                    if prev2:
                        pe.wait_ge(sem("g_made"), c - 1)
                    if prev:
                        if nxt:
                            pe.wait_ge(sem("cb_masked"), c + 2)
                        project_out(c - 1, 1 - r, nxt)
                    elif nxt:
                        turn_x(c + 1, 1 - r)
                    if nxt:
                        turn_b(c + 1, 1 - r)
                    pe.wait_ge(sem("M_ready"), c * 4 + 4)
                    if prev:
                        pe.wait_ge(sem("skip_added"), c * 2)
                    for t in range(CT):
                        y_t = y_flat[:, t * P:(t + 1) * P]
                        pe.transpose(y_t, yoff[:, t * P:(t + 1) * P], ident[:, :])
                        for half in range(2):
                            h = 2 * t + half
                            ins = pe.matmul(y_t[half * HD:(half + 1) * HD, :], xdt[:, r, h * HD:(h + 1) * HD],
                                             M[:, r, h, :], start=False, stop=True, skip_group_check=True)
                        if t in (CT // 2 - 1, CT - 1):
                            ins.then_inc(sem("y_summed"), 1)

                segments(0, range(4), first=True)
                cb(0, 0)
                turn_x(0, 0, True)
                turn_b(0, 0)
                over_chunks(pe, body)
                turn_x1(NCH - 2, 0)
                pe.wait_ge(sem("g_made"), NCH - 1)
                project_out(NCH - 1, 1, False)
                turn_x1(NCH - 1, 1)


def ffn_stage(nc, sem, sb0, ps, w_gu, w_down, x1_dram, gT_dram, out, modrow, gT_h, gT_l, raw):
    with ExitStack() as st:
        def sb(name, shape, dt=F32):
            return sb0(name, shape, dt, st)

        NN = 2 * NIC
        LAST = 2 * NN - 1
        sb("raw_place", [P, RING, PIECE])
        gu_h = sb("gu_h", [P, 4, 2, KT, P], F32R)
        gu_l = sb("gu_l", [P, 4, 2, KT, P], F32R)
        dn_h = sb("dn_h", [P, 4, D], F32R)
        dn_l = sb("dn_l", [P, 4, D], F32R)
        dn_s = sb("dn_s", [P, 2, D])
        acc = sb("acc", [P, HT, D])
        sg = sb("sg", [P, 2, TB])
        hid = sb("hid", [P, 4, TB])
        mag = sb("mag", [P, 4, TB])
        top = sb("top", [P, 2, TB])
        low = sb("low", [P, 2, TB])
        first = sb("first", [P, 2, TB], BF16)
        both = sb("both", [P, 2, TB], BF16)
        lead = sb("lead", [P, TB], BF16)
        keep = sb("keep", [P, 4, TB], BF16)
        hs_h = sb("hs_h", [P, 4, TB], F32R)
        hs_l = sb("hs_l", [P, 4, TB], F32R)

        gate_bank = [ps[:, 0, :], ps[:, 1, :]]
        up_bank = [ps[:, 2, :], ps[:, 3, :]]
        down_bank = [ps[:, 4 + t, :] for t in range(4)]
        HID0, DOWN0, ACC0, LOW0, HS0 = 2, 4, 4, RING, 4

        with nc.Block() as block:
            @block.sync
            def _(sp):
                def load_pieces(N, pieces):
                    for p in pieces:
                        sp.wait_ge(sem("piece_split"), N * 6 + p + 1)
                        ap, at = (w_gu, p) if p < 4 else (w_down, p - 4)
                        src = ap[N, at] if isinstance(N, int) else \
                            ap[bass.ds(N % NIC, 1), at, :, :].rearrange("o p n -> p (o n)")
                        sp.dma_start(raw[:, p % RING, :], src).then_inc(sem(f"piece_loaded{p % RING}"), 16)

                load_pieces(0, range(RING, 6))
                with sp.Fori(1, NN) as N:
                    load_pieces(N, range(6))
                for t in range(TT):
                    sp.wait_ge(sem("acc_added"), ACC0 + 4 * LAST + t + 1)
                    sp.dma_start(out[NCH - TT + t], acc[:, TT + t, :]).then_inc(sem("end_stored"), 16)
                sp.wait_ge(sem("end_stored"), 16 * TT)

            @block.gpsimd
            def _(pool):
                def load_acc(h, g):
                    rows = slice(h * HT + g * TT, h * HT + (g + 1) * TT)
                    pool.dma_start(acc[:, g * TT:(g + 1) * TT, :], x1_dram[rows, :, :].rearrange("t p n -> p t n"))\
                        .then_inc(sem(f"acc_loaded{g}"), 16)

                def store(h, g):
                    rows = slice(h * HT + g * TT, h * HT + (g + 1) * TT)
                    pool.wait_ge(sem("acc_added"), ACC0 + 4 * ((h * NIC + NIC - 1) * 2 + g + 1))
                    pool.dma_start(out[rows, :, :].rearrange("t p n -> p t n"), acc[:, g * TT:(g + 1) * TT, :])\
                        .then_inc(sem(f"out_stored{g}"), 16)

                for r in range(2):
                    pool.wait_ge(sem(f"x1_stored{r}"), 16 + 16 * NCH // 2)
                    pool.wait_ge(sem(f"g_stored{r}"), 32 + 32 * NCH // 2)
                for g in range(2):
                    load_acc(0, g)
                for g in range(2):
                    pool.wait_ge(sem("up_ready"), 4 * ((NIC - 1) * 2 + g + 1))
                    load_g(pool, sem, 1, g, gT_dram, gT_h, gT_l)
                for g in range(2):
                    store(0, g)
                    pool.wait_ge(sem(f"out_stored{g}"), 16)
                    load_acc(1, g)
                store(1, 0)
                pool.wait_ge(sem("out_stored0"), 32)
                pool.wait_ge(sem("out_stored1"), 16)

            def piece_ready(eng, N, p):
                eng.wait_ge(sem(f"piece_loaded{p % RING}"), N * 32 + 16 * (p // RING) + 16)

            def flat(ap):
                return ap.rearrange("p a k q -> p (a k q)")

            @block.scalar
            def _(act):
                def round_gu(N, p, free=True):
                    piece_ready(act, N, p)
                    if free:
                        act.wait_ge(sem("up_ready"), N * 8 - 3 + p)
                    act.activation(flat(gu_h[:, p, :, :, :]), raw[:, p % RING, :], ACT.Copy)\
                       .then_inc(sem("gu_high"), 1)

                def magnitude(n, j):
                    act.wait_ge(sem("hid_made"), n * 4 + j + 1 + HID0)
                    act.activation(mag[:, j, :], hid[:, j, :], ACT.Abs).then_inc(sem("mag_made"), 1)

                def group(n, following=None):
                    for j in range(4):
                        act.wait_ge(sem("gate_ready"), n * 4 + j + 1)
                        act.wait_ge(sem("hid_made"), n * 4 + j - 2 + 1 + HID0)
                        act.activation(sg[:, j % 2, :], gate_bank[j % 2], ACT.Silu).then_inc(sem("gate_silu"), 1)
                        if j >= 1:
                            magnitude(n, j - 1)
                            if following is not None:
                                round_gu(following, j - 1)
                    magnitude(n, 3)
                    if following is not None:
                        round_gu(following, 3)
                    for j in range(4):
                        act.wait_ge(sem("kept"), n * 4 + j + 1)
                        act.wait_ge(sem("down_ready"), n * 4 + DOWN0)
                        act.activation(hs_h[:, j, :], hid[:, j, :], ACT.Copy).then_inc(sem("hs_high"), 1)

                for p in range(4):
                    round_gu(0, p, free=False)
                with act.Fori(0, NN - 1) as N:
                    group(N * 2)
                    group(N * 2 + 1, N + 1)
                group(LAST - 1)
                group(LAST)

            @block.vector
            def _(dve):
                def low_gu(N, p):
                    dve.wait_ge(sem("gu_high"), N * 4 + p + 1)
                    dve.tensor_tensor(flat(gu_l[:, p, :, :, :]), raw[:, p % RING, :], flat(gu_h[:, p, :, :, :]),
                                      ALU.subtract).then_inc(sem("piece_split"), 1)

                def split_down(N, p):
                    k = N * 2 + (p - 4)
                    piece_ready(dve, N, p)
                    dve.wait_ge(sem("piece_split"), N * 6 + p + LOW0)
                    dst = slice((p - 4) * 2, (p - 4) * 2 + 2)
                    dve.tensor_tensor(dn_s[:, :, :], raw[:, p % RING, :].rearrange("p (a d) -> p a d", a=2),
                                      modrow[:, 5, :].unsqueeze(1).broadcast_to([P, 2, D]), ALU.mult)\
                       .then_inc(sem("dn_step"), 1)
                    dve.wait_ge(sem("dn_step"), k * 2 + 1)
                    dve.wait_ge(sem("down_ready"), N * 8 + DOWN0)
                    dve.tensor_copy(dn_h[:, dst, :], dn_s[:, :, :]).then_inc(sem("dn_step"), 1)
                    dve.wait_ge(sem("dn_step"), k * 2 + 2)
                    dve.tensor_tensor(dn_l[:, dst, :], dn_s[:, :, :], dn_h[:, dst, :], ALU.subtract)\
                       .then_inc(sem("piece_split"), 1)

                def compare(n):
                    m4 = mag[:, :, :].rearrange("p (a e) t -> p a e t", e=2)
                    dve.wait_ge(sem("mag_made"), n * 4 + 4)
                    dve.tensor_tensor(top[:, :, :], m4[:, :, 0, :], m4[:, :, 1, :], ALU.max)
                    dve.tensor_tensor(low[:, :, :], m4[:, :, 0, :], m4[:, :, 1, :], ALU.min)
                    dve.tensor_tensor(first[:, :, :], m4[:, :, 0, :], m4[:, :, 1, :], ALU.is_ge)\
                       .then_inc(sem("compared"), 1)
                    dve.wait_ge(sem("compared"), n * 3 + 1)
                    dve.tensor_tensor(both[:, 0, :], low[:, 0, :], top[:, 1, :], ALU.is_ge)
                    dve.tensor_tensor(both[:, 1, :], low[:, 1, :], top[:, 0, :], ALU.is_gt)\
                       .then_inc(sem("compared"), 1)
                    dve.wait_ge(sem("compared"), n * 3 + 2)
                    dve.tensor_tensor(lead[:, :], both[:, 0, :], both[:, 1, :], ALU.subtract)\
                       .then_inc(sem("compared"), 1)
                    dve.wait_ge(sem("compared"), n * 3 + 3)
                    dve.tensor_tensor(keep[:, 0, :], first[:, 0, :], lead[:, :], ALU.add)
                    dve.tensor_tensor(keep[:, 1, :], lead[:, :], first[:, 0, :], ALU.subtract)
                    dve.tensor_tensor(keep[:, 2, :], first[:, 1, :], lead[:, :], ALU.subtract)
                    dve.tensor_tensor(keep[:, 3, :], first[:, 1, :], lead[:, :], ALU.add)\
                       .then_inc(sem("keep_made"), 1)

                def select(n, j):
                    bound, op = ((1.0, ALU.is_ge), (0.0, ALU.is_ge), (1.0, ALU.is_ge), (0.0, ALU.is_le))[j]
                    dve.wait_ge(sem("keep_made"), n + 1)
                    dve.scalar_tensor_tensor(out=hid[:, j, :], in0=keep[:, j, :], scalar=bound, in1=hid[:, j, :],
                                             op0=op, op1=ALU.mult).then_inc(sem("kept"), 1)

                def low_kept(n, j):
                    dve.wait_ge(sem("hs_high"), n * 4 + j + 1)
                    dve.tensor_tensor(hs_l[:, j, :], hid[:, j, :], hs_h[:, j, :], ALU.subtract)\
                       .then_inc(sem("hs_low"), 1)

                def add_down(n, g, N, tiles):
                    dve.wait_ge(sem(f"acc_loaded{g}"), N // NIC * 16 + 16)
                    for t in tiles:
                        dve.wait_ge(sem("down_ready"), n * 4 + t + 1 + DOWN0)
                        dve.tensor_tensor(acc[:, g * TT + t, :], acc[:, g * TT + t, :], down_bank[t], ALU.add)\
                           .then_inc(sem("acc_added"), 1)

                def group(n, following=None, before=None, down_of=None):
                    for j in range(4):
                        dve.wait_ge(sem("gate_silu"), n * 4 + j + 1)
                        dve.wait_ge(sem("up_ready"), n * 4 + j + 1)
                        dve.wait_ge(sem("hs_low"), n * 4 + HS0)
                        dve.tensor_tensor(hid[:, j, :], sg[:, j % 2, :], up_bank[j % 2], ALU.mult)\
                           .then_inc(sem("hid_made"), 1)
                        if down_of is not None and j < 2:
                            split_down(down_of, 4 + j)
                        if following is not None and j >= 2:
                            for p in (2 * j - 4, 2 * j - 3):
                                low_gu(following, p)
                    compare(n)
                    select(n, 0)
                    if before is not None:
                        add_down(*before, (0,))
                    for j in range(1, 4):
                        select(n, j)
                        low_kept(n, j - 1)
                    low_kept(n, 3)
                    if before is not None:
                        add_down(*before, (1, 2, 3))

                dve.sem_inc(sem("hid_made"), HID0)
                dve.sem_inc(sem("acc_added"), ACC0)
                dve.sem_inc(sem("piece_split"), LOW0)
                dve.sem_inc(sem("hs_low"), HS0)
                for p in range(4):
                    low_gu(0, p)
                group(0, down_of=0)
                group(1, following=1, before=(0, 0, 0))
                with dve.Fori(0, NN - 2) as N:
                    group(N * 2 + 2, before=(N * 2 + 1, 1, N))
                    group(N * 2 + 3, down_of=N + 1, following=N + 2, before=(N * 2 + 2, 0, N + 1))
                group(LAST - 1, before=(LAST - 2, 1, NN - 2))
                group(LAST, down_of=NN - 1, before=(LAST - 1, 0, NN - 1))
                add_down(LAST, 1, NN - 1, range(TT))

            @block.tensor
            def _(pe):
                def gate_up(n, N, g):
                    tiles = slice(g * TT, (g + 1) * TT)
                    pe.wait_ge(sem(f"g_loaded{g}"), N // NIC * 32 + 32)
                    for j in range(4):
                        if g == 0:
                            pe.wait_ge(sem("gu_high"), N * 4 + j + 1)
                            pe.wait_ge(sem("piece_split"), N * 6 + j + 1 + LOW0)
                        pe.wait_ge(sem("hid_made"), n * 4 + j - 2 + 1 + HID0)
                        for a, bank, ready in ((0, gate_bank[j % 2], "gate_ready"), (1, up_bank[j % 2], "up_ready")):
                            three_pass(pe, bank, [(gu_h[:, j, a, kt, :], gu_l[:, j, a, kt, :],
                                                   gT_h[:, tiles, kt, :], gT_l[:, tiles, kt, :])
                                                  for kt in range(KT)]).then_inc(sem(ready), 1)

                def down(n, N, g):
                    if g == 0:
                        pe.wait_ge(sem("piece_split"), N * 6 + 6 + LOW0)
                    for t in range(TT):
                        pe.wait_ge(sem("acc_added"), n * 4 + t - 4 + 1 + ACC0)
                        for j in range(4):
                            if t == 0:
                                pe.wait_ge(sem("hs_low"), n * 4 + j + 1 + HS0)
                            last = three_pass(pe, down_bank[t],
                                              [(hs_h[:, j, t * P:(t + 1) * P], hs_l[:, j, t * P:(t + 1) * P],
                                                dn_h[:, j, :], dn_l[:, j, :])], start=(j == 0), stop=(j == 3))
                        last.then_inc(sem("down_ready"), 1)

                pe.sem_inc(sem("down_ready"), DOWN0)
                gate_up(0, 0, 0)
                with pe.Fori(0, NN - 1) as N:
                    gate_up(N * 2 + 1, N, 1)
                    down(N * 2, N, 0)
                    gate_up(N * 2 + 2, N + 1, 0)
                    down(N * 2 + 1, N, 1)
                gate_up(LAST, NN - 1, 1)
                down(LAST - 1, NN - 1, 0)
                down(LAST, NN - 1, 1)


def kernel(L0_attn_u, L0_attn_in_proj_w, L0_attn_conv_w, L0_attn_conv_b, L0_attn_dt_bias, L0_attn_A_log,
           L0_attn_D_skip, L0_attn_norm_w, L0_attn_out_proj_w, L0_ffn_w_gate, L0_ffn_w_up, L0_ffn_w_down,
           L0_c, L0_wmod):
    import numpy as np
    import concourse.bacc as bacc
    from concourse.bass_utils import run_bass_kernel_spmd

    def own(a):
        return np.ascontiguousarray(a)

    def wide(a):
        return own(np.broadcast_to(np.asarray(a)[None, :], (P, np.asarray(a).shape[0])))

    u = np.asarray(L0_attn_u)
    gu = np.stack([np.asarray(w).reshape(KT, P, NIC, P, 4).transpose(2, 4, 1, 0, 3)
                   for w in (L0_ffn_w_gate, L0_ffn_w_up)], axis=3)
    down = np.asarray(L0_ffn_w_down).reshape(NIC, P, 2, 2, D).transpose(0, 2, 1, 3, 4)
    arrays = {
        "x": own(u.reshape(NCH, P, D)),
        "w_in": own(np.asarray(L0_attn_in_proj_w).T.reshape(KT, P, DIN).transpose(1, 0, 2)),
        "w_out": own(np.asarray(L0_attn_out_proj_w).T.reshape(CT, P, D)),
        "conv_w": own(np.asarray(L0_attn_conv_w).reshape(NXBC, P, TAPS).transpose(1, 0, 2)),
        "conv_b": own(np.asarray(L0_attn_conv_b).reshape(NXBC, P).T),
        "dt_bias": wide(L0_attn_dt_bias),
        "a_log": wide(L0_attn_A_log),
        "d_skip": own(np.broadcast_to(np.asarray(L0_attn_D_skip).reshape(CT, 2).T[:, None, :], (2, HD, CT))),
        "norm_w": own(np.asarray(L0_attn_norm_w).reshape(CT, P).T),
        "w_gu": own(gu.reshape(NIC, 4, P, 2 * KT * P)),
        "w_down": own(down.reshape(NIC, 2, P, 2 * D)),
        "c": own(np.asarray(L0_c).reshape(KT, P).T),
        "w_mod": own(np.asarray(L0_wmod).reshape(KT, P, 6 * D).transpose(1, 0, 2)),
    }
    nc = bacc.Bacc("TRN2", target_bir_lowering=False, num_devices=1)
    args = [nc.dram_tensor(n, a.shape, mybir.dt.from_np(a.dtype), kind="ExternalInput").ap()
            for n, a in arrays.items()]
    out = nc.dram_tensor("out", (NCH, P, D), F32, kind="ExternalOutput").ap()
    build(nc, *args, out)
    r = run_bass_kernel_spmd(nc, [arrays], core_ids=[0])
    return np.asarray(r.results[0]["out"]).reshape(1, L, D)
```
